# Optimizing a Trainium2 kernel written in Bass

```python
import numpy as np
import jax
import jax.numpy as jnp

def _softmax(x, axis=-1):
    return jax.nn.softmax(x, axis=axis)

def _gelu(x):
    return jax.nn.gelu(x, approximate=True)

def _silu(x):
    return jax.nn.silu(x)

def _sigmoid(x):
    return jax.nn.sigmoid(x)

def _layernorm(x, axis=-1, eps=1e-05):
    m = jnp.mean(x, axis=axis, keepdims=True)
    v = jnp.var(x, axis=axis, keepdims=True)
    return (x - m) / jnp.sqrt(v + eps)

def _scatter_add(tgt, idx, src, axis=0):
    return tgt.at[idx].add(src)

def _segment_sum(src, seg, n):
    return jax.ops.segment_sum(src, seg, n)
kernel_name = 'mk_gnn_resnorm_d4_gnn_r8_fdc012'

def setup_inputs(seed: int=0):
    np.random.seed(seed)
    _w = jnp.asarray

    def _rec_inputs():
        import jax
        import jax.numpy as jnp
        _gk = jax.random.key(seed)
        x = -8.776e-05 + 1 * jax.random.normal(jax.random.fold_in(_gk, 1), (6250, 256), jnp.float32)
        _s = jax.random.randint(jax.random.fold_in(_gk, 2), (50000,), 0, 6250, jnp.int32)
        _d = jax.random.randint(jax.random.fold_in(_gk, 3), (50000,), 0, 6250, jnp.int32)
        _loop = jnp.arange(6250, dtype=jnp.int32)
        src = jnp.concatenate([_s, _d, _loop])
        dst = jnp.concatenate([_d, _s, _loop])
        _o = jnp.argsort(dst, stable=True)
        src = src[_o]
        dst = dst[_o]
        edge_attr_20 = jax.random.uniform(jax.random.fold_in(_gk, 11), (106250, 20), jnp.float32, 0.0, 1)
        edge_attr_64 = 0.000151818 + 1.00006 * jax.random.normal(jax.random.fold_in(_gk, 12), (106250, 64), jnp.float32)
        edge_weight = jax.random.uniform(jax.random.fold_in(_gk, 14), (106250,), jnp.float32, 0.0, 4.99999)
        return (x, src, dst, edge_attr_20, edge_attr_64, edge_weight)
    x, src, dst, edge_attr_20, edge_attr_64, edge_weight = _rec_inputs()

    def _L0_gnn_setup():
        import jax, jax.numpy as jnp
        import numpy as np
        H = 256
        R = 64
        N = 2500
        E = 40000
        CUTOFF_LO = 0.0
        CUTOFF_UP = 5.0
        LN_EPS = 1e-05

        def _layernorm(x, g, b):
            mu = jnp.mean(x, axis=-1, keepdims=True)
            var = jnp.var(x, axis=-1, keepdims=True)
            return (x - mu) * jax.lax.rsqrt(var + LN_EPS) * g + b

        def _cosine_cutoff(r):
            c = 0.5 * (jnp.cos(r * (jnp.pi / CUTOFF_UP)) + 1.0)
            return c * (r < CUTOFF_UP).astype(r.dtype)
        key = jax.random.key(seed)
        ks = jax.random.split(key, 16)

        def xavier(k, shape):
            fan_in, fan_out = (shape[1], shape[0])
            lim = np.sqrt(6.0 / (fan_in + fan_out))
            return jax.random.uniform(k, shape, jnp.float32, -lim, lim)
        x = jax.random.normal(ks[0], (N, H), jnp.float32)
        edge_index = jax.random.randint(ks[1], (2, E), 0, N, jnp.int64)
        edge_weight = jax.random.uniform(ks[2], (E,), jnp.float32, 0.0, CUTOFF_UP)
        edge_attr = jax.random.normal(ks[3], (E, R), jnp.float32)
        return {'x': x, 'edge_index': edge_index, 'edge_weight': edge_weight, 'edge_attr': edge_attr, 'ln_g': jnp.ones((H,), jnp.float32), 'ln_b': jnp.zeros((H,), jnp.float32), 'Wq': xavier(ks[4], (H, H)), 'bq': jnp.zeros((H,), jnp.float32), 'Wk': xavier(ks[5], (H, H)), 'bk': jnp.zeros((H,), jnp.float32), 'Wv': xavier(ks[6], (H, H)), 'bv': jnp.zeros((H,), jnp.float32), 'Wo': xavier(ks[7], (H, H)), 'bo': jnp.zeros((H,), jnp.float32), 'Wdk': xavier(ks[8], (H, R)), 'bdk': jnp.zeros((H,), jnp.float32), 'Wdv': xavier(ks[9], (H, R)), 'bdv': jnp.zeros((H,), jnp.float32)}
    _L0_gnn_all = _L0_gnn_setup()
    _L0_gnn_in = {k: v for k, v in _L0_gnn_all.items() if k in ('ln_g', 'ln_b', 'Wq', 'bq', 'Wk', 'bk', 'Wv', 'bv', 'Wo', 'bo', 'Wdk', 'bdk', 'Wdv', 'bdv')}
    del _L0_gnn_all

    def _L1_gnn_setup():
        import jax, jax.numpy as jnp
        import numpy as np
        N, E, HDIM, NG = (1250, 40000, 256, 20)
        BN_EPS = 1e-05
        key = jax.random.key(seed)
        ks = jax.random.split(key, 12)
        inp = {'x': jax.random.normal(ks[0], (N, HDIM), dtype=jnp.float32), 'rbf': jax.random.uniform(ks[1], (E, NG), dtype=jnp.float32), 'ei': jax.random.randint(ks[2], (2, E), 0, N, dtype=jnp.int64), 'Wf1': jax.random.normal(ks[3], (NG, HDIM), dtype=jnp.float32) / np.sqrt(NG), 'bf1': jnp.zeros((HDIM,), dtype=jnp.float32), 'Wf2': jax.random.normal(ks[4], (HDIM, HDIM), dtype=jnp.float32) / np.sqrt(HDIM), 'bf2': jnp.zeros((HDIM,), dtype=jnp.float32), 'Wu1': jax.random.normal(ks[5], (HDIM, HDIM), dtype=jnp.float32) / np.sqrt(HDIM), 'bu1': jnp.zeros((HDIM,), dtype=jnp.float32), 'Wu2': jax.random.normal(ks[6], (HDIM, HDIM), dtype=jnp.float32) / np.sqrt(HDIM), 'bu2': jnp.zeros((HDIM,), dtype=jnp.float32), 'gamma': jnp.ones((HDIM,), dtype=jnp.float32), 'beta': jnp.zeros((HDIM,), dtype=jnp.float32)}
        return inp
    _L1_gnn_all = _L1_gnn_setup()
    _L1_gnn_in = {k: v for k, v in _L1_gnn_all.items() if k in ('Wf1', 'bf1', 'Wf2', 'bf2', 'Wu1', 'bu1', 'Wu2', 'bu2', 'gamma', 'beta')}
    del _L1_gnn_all

    def _L2_gnn_setup():
        import jax, jax.numpy as jnp
        import numpy as np
        N_NODES = 12500
        N_EDGES = 400000
        D_IN = 256
        D_OUT = 256
        key = jax.random.key(seed)
        k1, k2, k3, k4 = jax.random.split(key, 4)
        x = jax.random.normal(k1, (N_NODES, D_IN), dtype=jnp.float32)
        edge_index = jax.random.randint(k2, (2, N_EDGES), 0, N_NODES, dtype=jnp.int64)
        limit = np.sqrt(6.0 / (D_IN + D_OUT)).astype(np.float32)
        W = jax.random.uniform(k3, (D_IN, D_OUT), dtype=jnp.float32, minval=-limit, maxval=limit)
        b = jnp.zeros((D_OUT,), dtype=jnp.float32)
        return {'x': x, 'edge_index': edge_index, 'W': W, 'b': b}
    _L2_gnn_all = _L2_gnn_setup()
    _L2_gnn_in = {k: v for k, v in _L2_gnn_all.items() if k in ('W', 'b')}
    del _L2_gnn_all

    def _L3_gnn_setup():
        import jax, jax.numpy as jnp
        import numpy as np
        N_NODES = 6250
        N_EDGES = 200000
        IN_DIM, OUT_DIM, N_HEADS = (256, 64, 4)
        EPS = 1e-12
        key = jax.random.key(seed)
        k1, k2, k3, k4, k5 = jax.random.split(key, 5)
        h = jax.random.normal(k1, (N_NODES, IN_DIM), dtype=jnp.float32)
        edge_index = jax.random.randint(k2, (2, N_EDGES), 0, N_NODES, dtype=jnp.int32)
        W = jax.random.normal(k3, (IN_DIM, OUT_DIM), dtype=jnp.float32) * 0.05
        Wl = jax.random.normal(k4, (N_HEADS, OUT_DIM), dtype=jnp.float32) * 0.05
        Wr = jax.random.normal(k5, (N_HEADS, OUT_DIM), dtype=jnp.float32) * 0.05
        b = jnp.zeros((OUT_DIM,), dtype=jnp.float32)
        return {'h': h, 'W': W, 'Wl': Wl, 'Wr': Wr, 'b': b, 'edge_index': edge_index}
    _L3_gnn_all = _L3_gnn_setup()
    _L3_gnn_in = {k: v for k, v in _L3_gnn_all.items() if k in ('W', 'Wl', 'Wr', 'b')}
    del _L3_gnn_all
    return {'x': x, 'src': src, 'dst': dst, 'edge_attr_20': edge_attr_20, 'edge_attr_64': edge_attr_64, 'edge_weight': edge_weight, 'L0_gnn_ln_g': _L0_gnn_in['ln_g'], 'L0_gnn_ln_b': _L0_gnn_in['ln_b'], 'L0_gnn_Wq': _L0_gnn_in['Wq'], 'L0_gnn_bq': _L0_gnn_in['bq'], 'L0_gnn_Wk': _L0_gnn_in['Wk'], 'L0_gnn_bk': _L0_gnn_in['bk'], 'L0_gnn_Wv': _L0_gnn_in['Wv'], 'L0_gnn_bv': _L0_gnn_in['bv'], 'L0_gnn_Wo': _L0_gnn_in['Wo'], 'L0_gnn_bo': _L0_gnn_in['bo'], 'L0_gnn_Wdk': _L0_gnn_in['Wdk'], 'L0_gnn_bdk': _L0_gnn_in['bdk'], 'L0_gnn_Wdv': _L0_gnn_in['Wdv'], 'L0_gnn_bdv': _L0_gnn_in['bdv'], 'L1_gnn_Wf1': _L1_gnn_in['Wf1'], 'L1_gnn_bf1': _L1_gnn_in['bf1'], 'L1_gnn_Wf2': _L1_gnn_in['Wf2'], 'L1_gnn_bf2': _L1_gnn_in['bf2'], 'L1_gnn_Wu1': _L1_gnn_in['Wu1'], 'L1_gnn_bu1': _L1_gnn_in['bu1'], 'L1_gnn_Wu2': _L1_gnn_in['Wu2'], 'L1_gnn_bu2': _L1_gnn_in['bu2'], 'L1_gnn_gamma': _L1_gnn_in['gamma'], 'L1_gnn_beta': _L1_gnn_in['beta'], 'L2_gnn_W': _L2_gnn_in['W'], 'L2_gnn_b': _L2_gnn_in['b'], 'L3_gnn_W': _L3_gnn_in['W'], 'L3_gnn_Wl': _L3_gnn_in['Wl'], 'L3_gnn_Wr': _L3_gnn_in['Wr'], 'L3_gnn_b': _L3_gnn_in['b']}

def reference(x, src, dst, edge_attr_20, edge_attr_64, edge_weight, L0_gnn_ln_g, L0_gnn_ln_b, L0_gnn_Wq, L0_gnn_bq, L0_gnn_Wk, L0_gnn_bk, L0_gnn_Wv, L0_gnn_bv, L0_gnn_Wo, L0_gnn_bo, L0_gnn_Wdk, L0_gnn_bdk, L0_gnn_Wdv, L0_gnn_bdv, L1_gnn_Wf1, L1_gnn_bf1, L1_gnn_Wf2, L1_gnn_bf2, L1_gnn_Wu1, L1_gnn_bu1, L1_gnn_Wu2, L1_gnn_bu2, L1_gnn_gamma, L1_gnn_beta, L2_gnn_W, L2_gnn_b, L3_gnn_W, L3_gnn_Wl, L3_gnn_Wr, L3_gnn_b):
    import jax
    import jax.numpy as jnp

    def _L0_gnn_ref(x, edge_index, edge_weight, edge_attr, ln_g, ln_b, Wq, bq, Wk, bk, Wv, bv, Wo, bo, Wdk, bdk, Wdv, bdv):
        import jax, jax.numpy as jnp
        import numpy as np
        H = 256
        R = 64
        N = 2500
        E = 40000
        CUTOFF_LO = 0.0
        CUTOFF_UP = 5.0
        LN_EPS = 1e-05

        def _layernorm(x, g, b):
            mu = jnp.mean(x, axis=-1, keepdims=True)
            var = jnp.var(x, axis=-1, keepdims=True)
            return (x - mu) * jax.lax.rsqrt(var + LN_EPS) * g + b

        def _cosine_cutoff(r):
            c = 0.5 * (jnp.cos(r * (jnp.pi / CUTOFF_UP)) + 1.0)
            return c * (r < CUTOFF_UP).astype(r.dtype)
        src = edge_index[0]
        dst = edge_index[1]
        x_norm = _layernorm(x, ln_g, ln_b)
        q = x_norm @ Wq.T + bq
        k = x_norm @ Wk.T + bk
        v = x_norm @ Wv.T + bv
        dk = jax.nn.silu(edge_attr @ Wdk.T + bdk)
        dv = jax.nn.silu(edge_attr @ Wdv.T + bdv)
        q_i = q[dst]
        k_j = k[src]
        v_j = v[src]
        attn = jnp.sum(q_i * k_j * dk, axis=1)
        attn = jax.nn.silu(attn) * _cosine_cutoff(edge_weight)
        msg = v_j * dv * attn[:, None]
        agg = jax.ops.segment_sum(msg, dst, num_segments=x.shape[0])
        out = agg @ Wo.T + bo
        return x + out

    def _L1_gnn_ref(x, rbf, Wf1, bf1, Wf2, bf2, Wu1, bu1, Wu2, bu2, gamma, beta, ei):
        import jax, jax.numpy as jnp
        import numpy as np
        N, E, HDIM, NG = (1250, 40000, 256, 20)
        BN_EPS = 1e-05
        row, col = (ei[0], ei[1])
        filt = jax.nn.silu(rbf @ Wf1 + bf1) @ Wf2 + bf2
        msg = x[col] * filt
        agg = jax.ops.segment_sum(msg, row, num_segments=x.shape[0])
        h = jax.nn.silu(agg @ Wu1 + bu1) @ Wu2 + bu2
        mean = jnp.mean(h, axis=0)
        var = jnp.mean(jnp.square(h - mean), axis=0)
        bn = gamma * (h - mean) * jax.lax.rsqrt(var + BN_EPS) + beta
        return x + bn

    def _L2_gnn_ref(x, edge_index, W, b):
        import jax, jax.numpy as jnp
        import numpy as np
        N_NODES = 12500
        N_EDGES = 400000
        D_IN = 256
        D_OUT = 256
        N = x.shape[0]
        h = x @ W
        loop = jnp.arange(N, dtype=edge_index.dtype)
        src = jnp.concatenate([edge_index[0], loop])
        dst = jnp.concatenate([edge_index[1], loop])
        deg = jax.ops.segment_sum(jnp.ones(dst.shape, dtype=h.dtype), dst, num_segments=N)
        dinv = jnp.where(deg > 0, jax.lax.rsqrt(deg), 0.0)
        norm = dinv[src] * dinv[dst]
        out = jax.ops.segment_sum(norm[:, None] * h[src], dst, num_segments=N) + b
        return jax.nn.leaky_relu(out, negative_slope=0.2)

    def _L3_gnn_ref(h, W, Wl, Wr, b, edge_index):
        import jax, jax.numpy as jnp
        import numpy as np
        N_NODES = 6250
        N_EDGES = 200000
        IN_DIM, OUT_DIM, N_HEADS = (256, 64, 4)
        EPS = 1e-12
        N = h.shape[0]
        H = Wl.shape[0]
        x = h @ W
        el = x @ Wl.T
        er = x @ Wr.T
        src, dst = (edge_index[0], edge_index[1])
        e = el[src] + er[dst]
        e = jnp.exp(jax.nn.leaky_relu(e, negative_slope=0.2))
        rowsum = jax.ops.segment_sum(e, src, num_segments=N)
        w = e / jnp.maximum(rowsum, EPS)[src]
        heads = [jax.ops.segment_sum(w[:, hd:hd + 1] * x[dst], src, num_segments=N) for hd in range(H)]
        out = jnp.stack(heads, axis=1)
        out = jax.nn.elu(out + b)
        return out.reshape(N, H * x.shape[1])
    edge_index = jnp.stack([src, dst])
    x = _layernorm(x + _L0_gnn_ref(x, edge_index, edge_weight, edge_attr_64, L0_gnn_ln_g, L0_gnn_ln_b, L0_gnn_Wq, L0_gnn_bq, L0_gnn_Wk, L0_gnn_bk, L0_gnn_Wv, L0_gnn_bv, L0_gnn_Wo, L0_gnn_bo, L0_gnn_Wdk, L0_gnn_bdk, L0_gnn_Wdv, L0_gnn_bdv), axis=-1)
    x = _layernorm(x + _L1_gnn_ref(x, edge_attr_20, L1_gnn_Wf1, L1_gnn_bf1, L1_gnn_Wf2, L1_gnn_bf2, L1_gnn_Wu1, L1_gnn_bu1, L1_gnn_Wu2, L1_gnn_bu2, L1_gnn_gamma, L1_gnn_beta, edge_index), axis=-1)
    x = _layernorm(x + _L2_gnn_ref(x, edge_index, L2_gnn_W, L2_gnn_b), axis=-1)
    x = _layernorm(x + _L3_gnn_ref(x, L3_gnn_W, L3_gnn_Wl, L3_gnn_Wr, L3_gnn_b, edge_index), axis=-1)
    return x

_drawn_inputs = setup_inputs


def setup_inputs(seed=0):
    import zlib

    import numpy as np

    out = dict(_drawn_inputs(seed))
    spreads = {'L0_gnn_ln_g': (1.0, 0.2),
     'L0_gnn_ln_b': (0.0, 0.1),
     'L0_gnn_bq': (0.0, 0.1),
     'L0_gnn_bk': (0.0, 0.1),
     'L0_gnn_bv': (0.0, 0.1),
     'L0_gnn_bo': (0.0, 0.1),
     'L0_gnn_bdk': (0.0, 0.1),
     'L0_gnn_bdv': (0.0, 0.1),
     'L1_gnn_bf1': (0.0, 0.1),
     'L1_gnn_bf2': (0.0, 0.1),
     'L1_gnn_bu1': (0.0, 0.379),
     'L1_gnn_bu2': (0.0, 0.8),
     'L1_gnn_gamma': (1.0, 0.2),
     'L1_gnn_beta': (0.0, 0.1),
     'L2_gnn_b': (0.0, 0.1),
     'L3_gnn_b': (0.0, 0.1)}
    factors = {'L3_gnn_Wl': 3.73}
    for name, (base, spread) in spreads.items():
        noise = np.random.default_rng([zlib.crc32(name.encode()), seed]).standard_normal(out[name].shape)
        drawn = base * np.exp(spread * noise) if base else spread * noise
        out[name] = jnp.asarray(drawn.astype(out[name].dtype))
    for name, factor in factors.items():
        out[name] = (out[name] * factor).astype(out[name].dtype)
    return out
```

```python
import numpy as np
import concourse.bass as bass
from concourse import mybir
from contextlib import ExitStack

F32 = mybir.dt.float32
I32 = mybir.dt.int32
BF16 = mybir.dt.bfloat16
ALU = mybir.AluOpType
ACT = mybir.ActivationFunctionType
AX = mybir.AxisListType

P = 128
N = 6250
E = 106250
H = 256
R64 = 64
R20 = 20
HEADS = 4
DOUT = 64
XR = DOUT + HEADS
PAY = HEADS * DOUT + HEADS
NT = -(-N // P) + 1
NP = NT * P
TRASH = NP - P
ET = 832
EP = ET * P
G = 8
NG = ET // G
NB = 5
KACC = 4
LN_EPS = 1e-5
TWO_PI = 2.0 * np.pi
ROUND = 12582912.0
ds = bass.ds


def bcast_rows(ap, n):
    return ap.partition_broadcast(n)


class Phase:

    def __init__(self, nc, name):
        self.nc, self.name, self.ctx, self.used = nc, name, ExitStack(), []

    def __enter__(self):
        self.ctx.__enter__()
        return self

    def __exit__(self, *a):
        r = self.ctx.__exit__(*a)
        if self.used:
            self.nc.clear_and_free_semaphores(self.used)
            self.nc.all_engine_barrier()
        return r

    def sb(self, name, shape, dt=F32):
        return self.ctx.enter_context(self.nc.sbuf_tensor(f"{self.name}_{name}", shape, dt))

    def ps(self, name, shape, dt=F32):
        return self.ctx.enter_context(self.nc.psum_tensor(f"{self.name}_{name}", shape, dt))

    def sem(self, name):
        self.used.append(self.nc.alloc_semaphore(f"{self.name}_{name}"))
        return self.used[-1]

    def sems(self, name, n):
        return [self.sem(f"{name}{i}") for i in range(n)]

    def block(self):
        return self.ctx.enter_context(self.nc.Block())


def layernorm_batch(nc, dve, x, xhat, stats, mv, rstd, s_stats, s_var, s_sqrt, s_rinv, s_norm, s_go, it):
    for u in range(NB):
        nc.vector.bn_stats(stats[:, u, :], x[:, u, :]).then_inc(s_stats, 1)
    dve.wait_ge(s_stats, (it + 1) * 2 * NB - NB)
    dve.sem_inc(s_go, 1)
    for u in range(NB):
        nc.vector.bn_aggr(mv[:, u, :], stats[:, u, :]).then_inc(s_stats, 1)
    dve.wait_ge(s_stats, (it + 1) * 2 * NB)
    nc.vector.tensor_scalar(rstd[:, 0, :], mv[:, :, 1], LN_EPS, None, ALU.add).then_inc(s_var, 1)
    dve.wait_ge(s_sqrt, it + 1)
    nc.vector.reciprocal(rstd[:, 2, :], rstd[:, 1, :]).then_inc(s_rinv, 1)
    dve.wait_ge(s_rinv, it + 1)
    for u in range(NB):
        nc.vector.tensor_scalar(xhat[:, u, :], x[:, u, :], mv[:, u, 0:1], rstd[:, 2, u:u + 1],
                                ALU.subtract, ALU.mult).then_inc(s_norm, 1)
    dve.wait_ge(s_norm, (it + 1) * NB)
    dve.sem_inc(s_go, 1)


def layernorm_root(nc, act, rstd, s_var, s_sqrt, it):
    act.wait_ge(s_var, it + 1)
    nc.scalar.activation(rstd[:, 1, :], rstd[:, 0, :], ACT.Sqrt).then_inc(s_sqrt, 1)


def gnn_kernel(nc, A, out):
    ctx = ExitStack()
    with ctx, nc.allow_non_contiguous_dma(reason="small tables of weights and indices"):
        def dram(name, shape, dt=F32):
            return nc.dram_tensor(name, shape, dt, kind="Internal").ap()

        def keep(name, shape, dt=F32):
            return ctx.enter_context(nc.sbuf_tensor(name, shape, dt))

        q_tab = dram("q_tab", [NP, H])
        kv_tab = dram("kv_tab", [NP, 2 * H])
        x1_tab = dram("x1_tab", [NP, H])
        x2_tab = dram("x2_tab", [NP, H])
        x3_tab = dram("x3_tab", [NP, H])
        hs_tab = dram("hs_tab", [NP, H])
        xr_tab = dram("xr_tab", [NP, XR])
        el_tab = dram("el_tab", [NP, HEADS])
        srcu_cols = dram("srcu_cols", [P, ET], I32)
        dstu_cols = dram("dstu_cols", [P, ET], I32)
        acc0 = dram("acc0", [NP, H])
        acc1 = [dram(f"acc1_{k}", [NP, H]) for k in range(KACC)]
        acc2 = dram("acc2", [NP, H])
        acc3 = [dram(f"acc3_{k}", [NP, PAY]) for k in range(KACC)]

        def tiles(ap):
            return ap.rearrange("(t p) d -> p t d", p=P)

        ident = keep("ident", [P, P])
        iota_row = keep("iota_row", [P, P])
        src_f = keep("src_f", [P, ET])
        dst_f = keep("dst_f", [P, ET])
        cut = keep("cut", [P, ET])
        dinv = keep("dinv", [P, NT])
        ones_row = keep("ones_row", [1, P])
        zeros = keep("zeros", [P, PAY])

        edge_indices(nc, A, ident, iota_row, src_f, dst_f, cut, dinv, ones_row,
                     srcu_cols, dstu_cols, zeros)
        node_qkv(nc, A, ident, ones_row, tiles, q_tab, kv_tab)
        edge_layer0(nc, A, dst_f, cut, dstu_cols, q_tab, kv_tab, acc0, zeros)
        node_after0(nc, A, ident, ones_row, tiles, acc0, x1_tab)
        edge_layer1(nc, A, src_f, srcu_cols, x1_tab, acc1, ones_row, zeros)
        node_after1(nc, A, ident, ones_row, tiles, acc1, x1_tab, x2_tab, hs_tab, dinv)
        edge_layer2(nc, A, dst_f, dstu_cols, hs_tab, acc2, zeros)
        node_after2(nc, A, ident, ones_row, tiles, acc2, hs_tab, x2_tab, x3_tab, xr_tab, el_tab, dinv)
        edge_layer3(nc, A, src_f, srcu_cols, xr_tab, el_tab, acc3, zeros)
        node_after3(nc, A, tiles, acc3, x3_tab, out)


def edge_indices(nc, A, ident, iota_row, src_f, dst_f, cut, dinv, ones_row,
                 srcu_cols, dstu_cols, zeros):
    with Phase(nc, "ix") as ph:
        src_i = ph.sb("src_i", [P, ET], I32)
        dst_i = ph.sb("dst_i", [P, ET], I32)
        hi_i = ph.sb("hi_i", [P, ET], I32)
        lo_i = ph.sb("lo_i", [P, ET], I32)
        hi_f = ph.sb("hi_f", [P, ET])
        lo_f = ph.sb("lo_f", [P, ET])
        ew = ph.sb("ew", [P, ET])
        turn = ph.sb("turn", [P, ET])
        turn_r = ph.sb("turn_r", [P, ET])
        inside = ph.sb("inside", [P, ET])
        again = [ph.sb("again_s", [P, ET]), ph.sb("again_d", [P, ET])]
        room = [ph.sb("room_s", [P, ET]), ph.sb("room_d", [P, ET])]
        uniq = [ph.sb("uniq_s", [P, ET], I32), ph.sb("uniq_d", [P, ET], I32)]
        earlier = ph.sb("earlier", [P, P])
        trash = ph.sb("trash", [P, 1])
        half_pi = ph.sb("half_pi", [P, 1])
        rows = [ph.sb("rows_s", [P, G, P], I32), ph.sb("rows_d", [P, G, P], I32)]
        cols = ph.sb("cols", [P, 4, G])
        same = ph.sb("same", [P, 2, G, P], BF16)
        count = ph.sb("count", [P, 2, G])
        hot_lo = ph.sb("hot_lo", [P, G, P], BF16)
        hot_hi = ph.sb("hot_hi", [P, G, NT], BF16)
        none = ph.sb("none", [P, P], BF16)
        deg = ph.sb("deg", [P, NT])
        root = ph.sb("root", [P, NT])
        ps_deg = ph.ps("ps_deg", [P, NT])
        in_s = ph.sem("in")
        s_const = ph.sem("const")
        s_split = ph.sem("split")
        s_turn = ph.sem("turn")
        s_sin = ph.sem("sin")
        s_rows = ph.sem("rows")
        s_read = ph.sem("read")
        s_cols = ph.sem("cols")
        s_same = ph.sem("same")
        s_count = ph.sem("count")
        s_hot = ph.sem("hot")
        s_deg = ph.sem("deg")
        s_dsum = ph.sem("dsum")
        s_root = ph.sem("root")
        s_uniq = ph.sem("uniq")
        s_out = ph.sem("out")
        block = ph.block()

        @block.gpsimd
        def _(pool):
            nc.gpsimd.memset(ident[:], 0.0).then_inc(s_const, 1)
            nc.gpsimd.memset(earlier[:], 1.0).then_inc(s_const, 1)
            pool.wait_ge(s_const, 2)
            nc.gpsimd.affine_select(out=ident[:], in_=ident[:], compare_op=ALU.not_equal, fill=1.0, base=0,
                                    pattern=[[-1, P]], channel_multiplier=1).then_inc(s_const, 1)
            nc.gpsimd.affine_select(out=earlier[:], in_=earlier[:], compare_op=ALU.is_gt, fill=0.0, base=0,
                                    pattern=[[-1, P]], channel_multiplier=1).then_inc(s_const, 1)
            nc.gpsimd.iota(iota_row[:], [[1, P]], base=0, channel_multiplier=0,
                           allow_small_or_imprecise_dtypes=True).then_inc(s_const, 1)
            nc.gpsimd.iota(trash[:], [[1, 1]], base=TRASH, channel_multiplier=1,
                           allow_small_or_imprecise_dtypes=True).then_inc(s_const, 1)

        @block.scalar
        def _(act):
            act.wait_ge(s_turn, 4)
            nc.scalar.activation(cut[:], turn_r[:], ACT.Sin, bias=half_pi[:], scale=-TWO_PI).then_inc(s_sin, 1)
            act.wait_ge(s_dsum, 1)
            nc.scalar.activation(root[:], deg[:], ACT.Sqrt).then_inc(s_root, 1)

        @block.vector
        def _(dve):
            nc.vector.memset(zeros[:], 0.0)
            dve.sem_inc(s_read, 1)
            nc.vector.memset(half_pi[:], np.pi / 2)
            nc.vector.memset(none[:], 0.0)
            nc.vector.memset(ones_row[:], 1.0).then_inc(s_split, 1)
            dve.wait_ge(in_s, 48)
            nc.vector.tensor_copy(src_f[:], src_i[:])
            nc.vector.tensor_copy(dst_f[:], dst_i[:])
            nc.vector.tensor_scalar(hi_i[:], dst_i[:], 7, None, ALU.logical_shift_right)
            nc.vector.tensor_scalar(lo_i[:], dst_i[:], P - 1, None, ALU.bitwise_and).then_inc(s_split, 1)
            nc.vector.tensor_scalar(turn[:], ew[:], 0.1, None, ALU.mult).then_inc(s_turn, 1)
            dve.wait_ge(s_split, 2)
            nc.vector.tensor_copy(hi_f[:], hi_i[:])
            nc.vector.tensor_copy(lo_f[:], lo_i[:]).then_inc(s_split, 1)
            dve.wait_ge(s_turn, 1)
            nc.vector.tensor_scalar(turn_r[:], turn[:], ROUND, ROUND, ALU.add, ALU.subtract).then_inc(s_turn, 1)
            dve.wait_ge(s_turn, 2)
            nc.vector.tensor_tensor(turn[:], turn[:], turn_r[:], ALU.subtract).then_inc(s_turn, 1)
            dve.wait_ge(s_turn, 3)
            nc.vector.scalar_tensor_tensor(turn_r[:], turn[:], -1.0, turn[:], ALU.mult, ALU.max).then_inc(s_turn, 1)
            nc.vector.tensor_scalar(inside[:], ew[:], 5.0, 0.5, ALU.is_lt, ALU.mult).then_inc(s_turn, 1)
            dve.wait_ge(s_sin, 1)
            dve.wait_ge(s_turn, 5)
            nc.vector.scalar_tensor_tensor(cut[:], cut[:], 1.0, inside[:], ALU.add, ALU.mult).then_inc(s_turn, 1)
            dve.wait_ge(s_split, 3)
            dve.wait_ge(s_const, 6)
            with dve.Fori(0, NG) as g:
                for k, col in enumerate((src_f, dst_f, lo_f, hi_f)):
                    nc.vector.tensor_copy(cols[:, k, :], col[:, ds(g * G, G)]).then_inc(s_cols, 1)
                dve.wait_ge(s_rows, (g + 1) * 32)
                dve.wait_ge(s_cols, (g + 1) * 4)
                for k in range(2):
                    for u in range(G):
                        nc.vector.scalar_tensor_tensor(same[:, k, u, :], rows[k][:, u, :], cols[:, k, u:u + 1],
                                                       earlier[:], ALU.is_equal, ALU.mult,
                                                       accum_out=count[:, k, u:u + 1]).then_inc(s_same, 1)
                dve.wait_ge(s_same, (g + 1) * 2 * G)
                for k in range(2):
                    nc.vector.tensor_scalar(again[k][:, ds(g * G, G)], count[:, k, :], 1.0, None,
                                            ALU.min).then_inc(s_count, 1)
                dve.sem_inc(s_read, 1)
                dve.wait_ge(s_deg, g * G + 1)
                for u in range(G):
                    nc.vector.tensor_scalar(hot_lo[:, u, :], iota_row[:], cols[:, 2, u:u + 1], None,
                                            ALU.is_equal)
                    nc.vector.tensor_scalar(hot_hi[:, u, :], iota_row[:, 0:NT], cols[:, 3, u:u + 1], None,
                                            ALU.is_equal).then_inc(s_hot, 1)
                dve.wait_ge(s_hot, (g + 1) * G)
                dve.wait_ge(s_count, (g + 1) * 2)
            for k, col in enumerate((src_f, dst_f)):
                nc.vector.tensor_scalar(room[k][:], col[:], trash[:], -1.0, ALU.subtract,
                                        ALU.mult).then_inc(s_uniq, 1)
            dve.wait_ge(s_uniq, 2)
            for k in range(2):
                nc.vector.tensor_tensor(room[k][:], room[k][:], again[k][:], ALU.mult).then_inc(s_uniq, 1)
            dve.wait_ge(s_uniq, 4)
            for k, col in enumerate((src_f, dst_f)):
                nc.vector.tensor_tensor(uniq[k][:], room[k][:], col[:], ALU.add).then_inc(s_uniq, 1)
            dve.wait_ge(s_deg, ET + 1)
            nc.vector.tensor_scalar(deg[:], ps_deg[:], 1.0, None, ALU.add).then_inc(s_dsum, 1)
            dve.wait_ge(s_root, 1)
            nc.vector.reciprocal(dinv[:], root[:])

        @block.tensor
        def _(pe):
            pe.wait_ge(s_split, 1)
            nc.tensor.matmul(ps_deg[:], none[:], none[:, 0:NT], start=True, stop=False,
                             skip_group_check=True).then_inc(s_deg, 1)
            with pe.Fori(0, NG) as g:
                for u in range(G):
                    pe.wait_ge(s_hot, g * G + u + 1)
                    nc.tensor.matmul(ps_deg[:], hot_lo[:, u, :], hot_hi[:, u, :], start=False, stop=False,
                                     skip_group_check=True).then_inc(s_deg, 1)

        @block.sync
        def _(sp):
            sp.dma_start(src_i[:], A["src_cols"]).then_inc(in_s, 16)
            sp.dma_start(dst_i[:], A["dst_cols"]).then_inc(in_s, 16)
            sp.dma_start(ew[:], A["ew_cols"]).then_inc(in_s, 16)
            with sp.Fori(0, NG) as g:
                sp.wait_ge(s_read, g + 1)
                for k, name in enumerate(("src_rows", "dst_rows")):
                    sp.dma_start(rows[k][:].rearrange("p u f -> p (u f)"),
                                 bcast_rows(A[name][ds(g * G * P, G * P)], P)).then_inc(s_rows, 16)
            sp.wait_ge(s_uniq, 6)
            sp.dma_start(srcu_cols, uniq[0][:]).then_inc(s_out, 16)
            sp.dma_start(dstu_cols, uniq[1][:]).then_inc(s_out, 16)
            sp.wait_ge(s_out, 32)


def node_qkv(nc, A, ident, ones_row, tiles, q_tab, kv_tab):
    with Phase(nc, "qkv") as ph:
        w = ph.sb("w", [P, 2, 3 * H])
        bias = ph.sb("bias", [1, 3 * H])
        gb = ph.sb("gb", [P, 2, 2])
        x = ph.sb("x", [P, 2, NB, H])
        xhat = ph.sb("xhat", [P, NB, H])
        xT = ph.sb("xT", [P, 2, 2, P])
        y = ph.sb("y", [P, NB, 3 * H])
        stats = ph.sb("stats", [P, NB, 6])
        mv = ph.sb("mv", [P, NB, 2])
        rstd = ph.sb("rstd", [P, 3, NB])
        ps_t = ph.ps("ps_t", [P, 2, 4, P])
        ps_y = ph.ps("ps_y", [P, 2, 1024])
        s_w = ph.sem("w")
        s_x = ph.sems("x", 2)
        s_xfree = ph.sem("xfree")
        s_stats, s_var, s_sqrt, s_rinv, s_norm = (ph.sem(n) for n in ("stats", "var", "sqrt", "rinv", "norm"))
        s_t = ph.sem("t")
        s_xT = ph.sem("xT")
        s_y = ph.sem("y")
        s_ys = ph.sem("ys")
        s_st = ph.sem("st")
        s_yfree = ph.sem("yfree")
        s_go = ph.sem("go")
        block = ph.block()
        xt = tiles(A["x"])
        IT = NT // (2 * NB)

        @block.sync
        def _(sp):
            sp.dma_start(w[:, :, 0:H], A["WqT"].rearrange("(c p) n -> p c n", p=P)).then_inc(s_w, 16)
            sp.dma_start(w[:, :, H:2 * H], A["WkT"].rearrange("(c p) n -> p c n", p=P)).then_inc(s_w, 16)
            sp.dma_start(w[:, :, 2 * H:], A["WvT"].rearrange("(c p) n -> p c n", p=P)).then_inc(s_w, 16)
            for k, b in enumerate(("bq", "bk", "bv")):
                sp.dma_start(bias[0:1, k * H:(k + 1) * H], A[b].rearrange("(a n) -> a n", a=1)).then_inc(s_w, 16)
            sp.dma_start(gb[:, 0, :], A["ln_g"].rearrange("(c p) -> p c", p=P)).then_inc(s_w, 16)
            sp.dma_start(gb[:, 1, :], A["ln_b"].rearrange("(c p) -> p c", p=P)).then_inc(s_w, 16)
            with sp.Fori(0, IT) as b:
                for h in range(2):
                    it = b * 2 + h
                    sp.wait_ge(s_xfree, it + 1)
                    sp.dma_start(x[:, h, :, :], xt[:, ds(it * NB, NB), :]).then_inc(s_x[h], 16)

        @block.vector
        def _(dve):
            dve.sem_inc(s_xfree, 2)
            with dve.Fori(0, IT) as b:
                for h in range(2):
                    it = b * 2 + h
                    dve.wait_ge(s_x[h], (b + 1) * 16)
                    dve.wait_ge(s_t, it * 2 * NB + 1)
                    layernorm_batch(nc, dve, x[:, h], xhat, stats, mv, rstd,
                                    s_stats, s_var, s_sqrt, s_rinv, s_norm, s_go, it)
                    dve.wait_ge(s_norm, (it + 1) * NB)
                    dve.sem_inc(s_xfree, 1)

        @block.tensor
        def _(pe):
            pe.sem_inc(s_t, 1)
            pe.wait_ge(s_w, 16 * 8)
            with pe.Fori(0, IT) as b:
                for h in range(2):
                    it = b * 2 + h
                    for u in range(NB):
                        n = it * NB + u
                        v = (h * NB + u) % 2
                        pe.wait_ge(s_norm, n + 1)
                        pe.wait_ge(s_xT, n * 2 + 1)
                        for c in range(2):
                            nc.tensor.transpose(ps_t[:, v, c, :], xhat[:, u, c * P:(c + 1) * P],
                                                ident[:]).then_inc(s_t, 1)
                        pe.wait_ge(s_xT, n * 2 + 3)
                        pe.wait_ge(s_ys, n + 1)
                        for a, z in ((0, 512), (512, 768)):
                            o = ps_y[:, v, a:z]
                            nc.tensor.matmul(o, xT[:, v, 0, :], w[:, 0, a:z], start=True, stop=False)
                            nc.tensor.matmul(o, xT[:, v, 1, :], w[:, 1, a:z], start=False, stop=False)
                            nc.tensor.matmul(o, ones_row[:], bias[0:1, a:z], start=False,
                                             stop=True).then_inc(s_y, 1)

        @block.scalar
        def _(act):
            act.sem_inc(s_xT, 1)
            act.sem_inc(s_ys, 2)
            act.wait_ge(s_w, 16 * 8)
            with act.Fori(0, IT) as b:
                for h in range(2):
                    it = b * 2 + h
                    layernorm_root(nc, act, rstd, s_var, s_sqrt, it)
                    act.wait_ge(s_yfree, it + 1)
                    for u in range(NB):
                        n = it * NB + u
                        v = (h * NB + u) % 2
                        act.wait_ge(s_t, n * 2 + 3)
                        for c in range(2):
                            nc.scalar.activation(xT[:, v, c, :], ps_t[:, v, c, :], ACT.Identity,
                                                 bias=gb[:, 1, c:c + 1], scale=gb[:, 0, c:c + 1]).then_inc(s_xT, 1)
                        act.wait_ge(s_y, n * 2 + 2)
                        nc.scalar.activation(y[:, u, :], ps_y[:, v, 0:3 * H], ACT.Copy).then_inc(s_ys, 1)

        @block.gpsimd
        def _(pool):
            pool.sem_inc(s_yfree, 1)
            with pool.Fori(0, NT // NB) as it:
                pool.wait_ge(s_ys, (it + 1) * NB + 2)
                pool.sem_inc(s_go, 1)
                pool.dma_start(tiles(q_tab)[:, ds(it * NB, NB), :], y[:, :, 0:H]).then_inc(s_st, 16)
                pool.dma_start(tiles(kv_tab)[:, ds(it * NB, NB), :], y[:, :, H:3 * H]).then_inc(s_st, 16)
                pool.wait_ge(s_st, (it + 1) * 32)
                pool.sem_inc(s_yfree, 1)


def zero_accumulators(pool, accs, zeros, s_add):
    for acc, s in zip(accs, s_add):
        flat = acc.rearrange("(p t) d -> p t d", p=P)
        d = flat.shape[2]
        pool.dma_start(flat, zeros[:, None, 0:d].to_broadcast([P, NT, d])).then_inc(s, 16)


def edge_layer0(nc, A, dst_f, cut, dstu_cols, q_tab, kv_tab, acc0, zeros):
    with Phase(nc, "e0") as ph:
        w = ph.sb("w", [R64 + 1, 2 * H])
        ea = ph.sb("ea", [R64 + 1, 2, G * P])
        rows = ph.sb("rows", [P, 2, G, P], I32)
        isrc = ph.sb("isrc", [P, 2, G], I32)
        idst = ph.sb("idst", [P, 2, G], I32)
        iout = ph.sb("iout", [P, 2, G], I32)
        kv = ph.sb("kv", [P, G, 2 * H])
        q = ph.sb("q", [P, G, H])
        qk = ph.sb("qk", [P, 2, H])
        junk = ph.sb("junk", [P, G, H], BF16)
        vd = ph.sb("vd", [P, G, H])
        raw = ph.sb("raw", [P, G])
        att = ph.sb("att", [P, 2, G])
        cols = ph.sb("cols", [P, 2, G])
        same = ph.sb("same", [P, G, P])
        msg = ph.sb("msg", [P, 2, H])
        ps_d = ph.ps("ps_d", [P, 2, 512])
        ps_m = ph.ps("ps_m", [P, 2, 512])
        s_w, s_one = ph.sem("w"), ph.sem("one")
        s_ld = ph.sems("ld", 2)
        s_ldfree = ph.sem("ldfree")
        s_ge = ph.sems("ge", G)
        s_gfree = ph.sem("gfree")
        s_go = ph.sem("go")
        s_dl, s_si, s_cols, s_qk, s_raw, s_vd = (ph.sem(n) for n in ("dl", "si", "cols", "qk", "raw", "vd"))
        s_rs, s_att, s_same, s_sum, s_msg = (ph.sem(n) for n in ("rs", "att", "same", "sum", "msg"))
        s_add = ph.sem("add")
        block = ph.block()

        @block.sync
        def _(sp):
            sp.dma_start(w[0:R64, 0:H], A["WdkT"]).then_inc(s_w, 16)
            sp.dma_start(w[0:R64, H:2 * H], A["WdvT"]).then_inc(s_w, 16)
            sp.dma_start(w[R64:R64 + 1, 0:H], A["bdk"].rearrange("(a n) -> a n", a=1)).then_inc(s_w, 16)
            sp.dma_start(w[R64:R64 + 1, H:2 * H], A["bdv"].rearrange("(a n) -> a n", a=1)).then_inc(s_w, 16)
            with sp.Fori(0, NG // 2) as b:
                for h in range(2):
                    g = b * 2 + h
                    sp.wait_ge(s_ldfree, g + 1)
                    sp.dma_start(ea[0:R64, h, :], A["ea64T"][:, ds(g * G * P, G * P)]).then_inc(s_ld[h], 16)
                    sp.dma_start(rows[:, h].rearrange("p u f -> p (u f)"),
                                 bcast_rows(A["dst_rows"][ds(g * G * P, G * P)], P)).then_inc(s_ld[h], 16)
                    sp.dma_start(isrc[:, h, :], A["src_cols"][:, ds(g * G, G)]).then_inc(s_ld[h], 16)
                    sp.dma_start(idst[:, h, :], A["dst_cols"][:, ds(g * G, G)]).then_inc(s_ld[h], 16)
                    sp.dma_start(iout[:, h, :], dstu_cols[:, ds(g * G, G)]).then_inc(s_ld[h], 16)

        @block.gpsimd
        def _(pool):
            nc.gpsimd.memset(ea[R64:R64 + 1, :, :], 1.0).then_inc(s_one, 1)
            pool.sem_inc(s_ldfree, 2)
            zero_accumulators(pool, [acc0], zeros, [s_add])
            with pool.Fori(0, NG // 2) as b:
                for h in range(2):
                    g = b * 2 + h
                    pool.wait_ge(s_ld[h], (b + 1) * 80)
                    for u in range(G):
                        pool.wait_ge(s_gfree, g * G + u + 1)
                        pool.sem_inc(s_go, 1)
                        pool.indirect_dma_start(kv[:, u, :], None, kv_tab,
                                                bass.IndirectOffsetOnAxis(isrc[:, h, u:u + 1], 0)).then_inc(s_ge[u], 16)
                        pool.indirect_dma_start(q[:, u, :], None, q_tab,
                                                bass.IndirectOffsetOnAxis(idst[:, h, u:u + 1], 0)).then_inc(s_ge[u], 16)
                    for u in range(G):
                        pool.wait_ge(s_msg, g * G + u + 3)
                        pool.wait_ge(s_add, (g * G + u + 1) * 16)
                        pool.sem_inc(s_go, 1)
                        pool.indirect_dma_start(acc0, bass.IndirectOffsetOnAxis(iout[:, h, u:u + 1], 0),
                                                msg[:, u % 2, :], None, compute_op=ALU.add).then_inc(s_add, 16)
                    pool.wait_ge(s_add, (g * G + G + 1) * 16)
                    pool.sem_inc(s_ldfree, 1)

        @block.tensor
        def _(pe):
            pe.wait_ge(s_w, 64)
            pe.wait_ge(s_one, 1)
            with pe.Fori(0, NG // 2) as b:
                for h in range(2):
                    g = b * 2 + h
                    pe.wait_ge(s_ld[h], (b + 1) * 80)
                    for u in range(G):
                        pe.wait_ge(s_vd, g * G + u + 1)
                        nc.tensor.matmul(ps_d[:, u % 2, :], ea[:, h, u * P:(u + 1) * P], w[:], start=True,
                                         stop=True).then_inc(s_dl, 1)
                    for u in range(G):
                        pe.wait_ge(s_same, g * G + u + 1)
                        pe.wait_ge(s_msg, g * G + u + 1)
                        nc.tensor.matmul(ps_m[:, u % 2, 0:H], same[:, u, :], vd[:, u, :], start=True,
                                         stop=True).then_inc(s_sum, 1)

        @block.scalar
        def _(act):
            act.sem_inc(s_msg, 2)
            with act.Fori(0, NG) as g:
                for u in range(G):
                    act.wait_ge(s_dl, g * G + u + 1)
                    nc.scalar.activation(ps_d[:, u % 2, :], ps_d[:, u % 2, :], ACT.Silu).then_inc(s_si, 1)
                act.wait_ge(s_raw, (g + 1) * G)
                nc.scalar.activation(att[:, 0, :], raw[:], ACT.Silu).then_inc(s_rs, 1)
                for u in range(G):
                    act.wait_ge(s_sum, g * G + u + 1)
                    act.wait_ge(s_add, g * G * 16 + max(u, 1) * 16)
                    nc.scalar.activation(msg[:, u % 2, :], ps_m[:, u % 2, 0:H], ACT.Copy).then_inc(s_msg, 1)

        @block.vector
        def _(dve):
            dve.sem_inc(s_gfree, G)
            dve.sem_inc(s_vd, 2)
            with dve.Fori(0, NG // 2) as b:
                for h in range(2):
                    g = b * 2 + h
                    nc.vector.tensor_copy(cols[:, 0, :], dst_f[:, ds(g * G, G)]).then_inc(s_cols, 1)
                    nc.vector.tensor_copy(cols[:, 1, :], cut[:, ds(g * G, G)]).then_inc(s_cols, 1)
                    for u in range(G):
                        n = g * G + u
                        dve.wait_ge(s_ge[u], (g + 1) * 32)
                        nc.vector.tensor_tensor(qk[:, u % 2, :], q[:, u, :], kv[:, u, 0:H], ALU.mult).then_inc(s_qk, 1)
                        dve.wait_ge(s_si, n + 1)
                        nc.vector.tensor_tensor(vd[:, u, :], kv[:, u, H:2 * H], ps_d[:, u % 2, H:2 * H],
                                                ALU.mult).then_inc(s_gfree, 1)
                        dve.wait_ge(s_qk, n + 1)
                        nc.vector.tensor_tensor_reduce(out=junk[:, u, :], in0=qk[:, u % 2, :], in1=ps_d[:, u % 2, 0:H],
                                                       scale=1.0, scalar=0.0, op0=ALU.mult, op1=ALU.add,
                                                       accum_out=raw[:, u:u + 1]).then_inc(s_raw, 1)
                        dve.wait_ge(s_raw, n + 1)
                        dve.sem_inc(s_vd, 1)
                    dve.wait_ge(s_rs, g + 1)
                    dve.wait_ge(s_cols, (g + 1) * 2)
                    nc.vector.tensor_tensor(att[:, 1, :], att[:, 0, :], cols[:, 1, :], ALU.mult).then_inc(s_att, 1)
                    dve.wait_ge(s_att, g + 1)
                    for u in range(G):
                        nc.vector.tensor_scalar(same[:, u, :], rows[:, h, u, :], cols[:, 0, u:u + 1],
                                                att[:, 1, u:u + 1], ALU.is_equal, ALU.mult).then_inc(s_same, 1)
                    dve.wait_ge(s_sum, (g + 1) * G)


def edge_layer1(nc, A, src_f, srcu_cols, x1_tab, acc1, ones_row, zeros):
    with Phase(nc, "e1") as ph:
        w1 = ph.sb("w1", [R20, H])
        b1 = ph.sb("b1", [P, 2])
        w2 = ph.sb("w2", [P, 2, H])
        b2 = ph.sb("b2", [1, H])
        ea = ph.sb("ea", [R20, 2, G * P])
        rows = ph.sb("rows", [P, 2, G, P], I32)
        idst = ph.sb("idst", [P, 2, G], I32)
        iout = ph.sb("iout", [P, 2, G], I32)
        hid = ph.sb("hid", [P, 2, 2, 512])
        xd = ph.sb("xd", [P, 2, G, H])
        cols = ph.sb("cols", [P, G])
        same = ph.sb("same", [P, 4, P])
        prod = ph.sb("prod", [P, 4, H])
        msg = ph.sb("msg", [P, KACC, H])
        ps_h = ph.ps("ps_h", [P, 2, 512])
        ps_f = ph.ps("ps_f", [P, 2, 512])
        ps_m = ph.ps("ps_m", [P, 2, 512])
        s_w = ph.sem("w")
        s_ld = ph.sems("ld", 2)
        s_rowfree, s_dyn = ph.sem("rowfree"), ph.sem("dyn")
        s_ge = [ph.sems(f"ge{h}_", G) for h in range(2)]
        s_gfree, s_go, s_cols, s_h, s_hid, s_f, s_prod, s_same, s_sum, s_msg = (
            ph.sem(n) for n in ("gfree", "go", "cols", "h", "hid", "f", "prod", "same", "sum", "msg"))
        s_add = ph.sems("add", KACC)
        block = ph.block()

        @block.sync
        def _(sp):
            sp.dma_start(w1[:], A["Wf1"]).then_inc(s_w, 16)
            sp.dma_start(w2[:], A["Wf2"].rearrange("(c p) n -> p c n", p=P)).then_inc(s_w, 16)
            sp.dma_start(b1[:], A["bf1"].rearrange("(c p) -> p c", p=P)).then_inc(s_w, 16)
            sp.dma_start(b2[:], A["bf2"].rearrange("(a n) -> a n", a=1)).then_inc(s_w, 16)
            with sp.Fori(0, NG // 2) as b:
                for h in range(2):
                    g = b * 2 + h
                    sp.wait_ge(s_rowfree, g + 1)
                    sp.dma_start(ea[:, h, :], A["ea20T"][:, ds(g * G * P, G * P)]).then_inc(s_ld[h], 16)
                    sp.dma_start(rows[:, h].rearrange("p u f -> p (u f)"),
                                 bcast_rows(A["src_rows"][ds(g * G * P, G * P)], P)).then_inc(s_ld[h], 16)
                    sp.dma_start(idst[:, h, :], A["dst_cols"][:, ds(g * G, G)]).then_inc(s_ld[h], 16)
                    sp.dma_start(iout[:, h, :], srcu_cols[:, ds(g * G, G)]).then_inc(s_ld[h], 16)

        @block.gpsimd
        def _(pool):
            pool.sem_inc(s_rowfree, 2)
            zero_accumulators(pool, acc1, zeros, s_add)
            with pool.Fori(0, NG // 2) as b:
                for h in range(2):
                    g = b * 2 + h
                    pool.wait_ge(s_ld[h], (b + 1) * 64)
                    pool.wait_ge(s_gfree, g + 1)
                    pool.sem_inc(s_go, 1)
                    for u in range(G):
                        pool.indirect_dma_start(xd[:, h, u, :], None, x1_tab,
                                                bass.IndirectOffsetOnAxis(idst[:, h, u:u + 1], 0)).then_inc(s_ge[h][u], 16)
                    for u in range(G):
                        pool.wait_ge(s_msg, g * G + u + 3)
                        pool.wait_ge(s_add[u % KACC], (g * (G // KACC) + u // KACC + 1) * 16)
                        pool.sem_inc(s_go, 1)
                        pool.indirect_dma_start(acc1[u % KACC], bass.IndirectOffsetOnAxis(iout[:, h, u:u + 1], 0),
                                                msg[:, u % KACC, :], None,
                                                compute_op=ALU.add).then_inc(s_add[u % KACC], 16)
                    for k in range(KACC):
                        pool.wait_ge(s_add[k], ((g + 1) * (G // KACC) + 1) * 16)
                    pool.sem_inc(s_rowfree, 1)

        @block.tensor
        def _(pe):
            pe.wait_ge(s_w, 64)
            pe.sem_inc(s_dyn, 1)
            with pe.Fori(0, NG // 2) as b:
                for h in range(2):
                    g = b * 2 + h
                    pe.wait_ge(s_ld[h], (b + 1) * 64)
                    for q in range(2):
                        m = g * 2 + q
                        for c in range(2):
                            pe.wait_ge(s_hid, m * 2 + c + 1)
                            nc.tensor.matmul(ps_h[:, c, :], w1[:, c * P:(c + 1) * P],
                                             ea[:, h, q * 512:(q + 1) * 512], start=True, stop=True).then_inc(s_h, 1)
                        pe.wait_ge(s_hid, m * 2 + 4)
                        for v in range(4):
                            u = q * 4 + v
                            n = g * G + u
                            pe.wait_ge(s_prod, n + 1)
                            o = ps_f[:, u % 2, 0:H]
                            nc.tensor.matmul(o, hid[:, q, 0, v * P:(v + 1) * P], w2[:, 0, :], start=True, stop=False)
                            nc.tensor.matmul(o, hid[:, q, 1, v * P:(v + 1) * P], w2[:, 1, :], start=False, stop=False)
                            nc.tensor.matmul(o, ones_row[:], b2[:], start=False, stop=True).then_inc(s_f, 1)
                            pe.wait_ge(s_prod, n + 3)
                            pe.wait_ge(s_same, n + 1)
                            pe.wait_ge(s_msg, n + 1)
                            nc.tensor.matmul(ps_m[:, u % 2, 0:H], same[:, v, :], prod[:, v, :], start=True,
                                             stop=True).then_inc(s_sum, 1)

        @block.scalar
        def _(act):
            act.sem_inc(s_msg, 2)
            act.sem_inc(s_hid, 2)
            act.wait_ge(s_w, 64)
            act.sem_inc(s_dyn, 1)
            with act.Fori(0, NG) as g:
                for q in range(2):
                    for c in range(2):
                        act.wait_ge(s_h, g * 4 + q * 2 + c + 1)
                        nc.scalar.activation(hid[:, q, c, :], ps_h[:, c, :], ACT.Silu,
                                             bias=b1[:, c:c + 1]).then_inc(s_hid, 1)
                    for v in range(4):
                        u = q * 4 + v
                        k = u % KACC
                        act.wait_ge(s_sum, g * G + u + 1)
                        act.wait_ge(s_add[k], (g * (G // KACC) + u // KACC + 1) * 16)
                        nc.scalar.activation(msg[:, k, :], ps_m[:, u % 2, 0:H], ACT.Copy).then_inc(s_msg, 1)

        @block.vector
        def _(dve):
            dve.sem_inc(s_gfree, 2)
            dve.sem_inc(s_prod, 2)
            with dve.Fori(0, NG // 2) as b:
                for h in range(2):
                    g = b * 2 + h
                    nc.vector.tensor_copy(cols[:], src_f[:, ds(g * G, G)]).then_inc(s_cols, 1)
                    dve.wait_ge(s_ld[h], (b + 1) * 64)
                    dve.wait_ge(s_cols, g + 1)
                    for u in range(G):
                        n = g * G + u
                        if u >= 4:
                            dve.wait_ge(s_sum, n - 3)
                        nc.vector.tensor_scalar(same[:, u % 4, :], rows[:, h, u, :], cols[:, u:u + 1], None,
                                                ALU.is_equal).then_inc(s_same, 1)
                        dve.wait_ge(s_ge[h][u], (b + 1) * 16)
                        dve.wait_ge(s_f, n + 1)
                        nc.vector.tensor_tensor(prod[:, u % 4, :], xd[:, h, u, :], ps_f[:, u % 2, 0:H],
                                                ALU.mult).then_inc(s_prod, 1)
                    dve.wait_ge(s_sum, (g + 1) * G)
                    dve.sem_inc(s_gfree, 1)


def edge_layer2(nc, A, dst_f, dstu_cols, hs_tab, acc2, zeros):
    with Phase(nc, "e2") as ph:
        rows = ph.sb("rows", [P, 2, G, P], I32)
        isrc = ph.sb("isrc", [P, 2, G], I32)
        iout = ph.sb("iout", [P, 2, G], I32)
        xs = ph.sb("xs", [P, 2, G, H])
        cols = ph.sb("cols", [P, G])
        same = ph.sb("same", [P, G, P])
        msg = ph.sb("msg", [P, 2, H])
        ps_m = ph.ps("ps_m", [P, 2, 512])
        s_ld = ph.sems("ld", 2)
        s_ge = [ph.sems(f"ge{h}_", G) for h in range(2)]
        s_ldfree, s_gfree, s_go, s_cols, s_same, s_sum, s_msg, s_add = (
            ph.sem(n) for n in ("ldfree", "gfree", "go", "cols", "same", "sum", "msg", "add"))
        block = ph.block()

        @block.sync
        def _(sp):
            with sp.Fori(0, NG // 2) as b:
                for h in range(2):
                    g = b * 2 + h
                    sp.wait_ge(s_ldfree, g + 1)
                    sp.dma_start(rows[:, h].rearrange("p u f -> p (u f)"),
                                 bcast_rows(A["dst_rows"][ds(g * G * P, G * P)], P)).then_inc(s_ld[h], 16)
                    sp.dma_start(isrc[:, h, :], A["src_cols"][:, ds(g * G, G)]).then_inc(s_ld[h], 16)
                    sp.dma_start(iout[:, h, :], dstu_cols[:, ds(g * G, G)]).then_inc(s_ld[h], 16)

        @block.gpsimd
        def _(pool):
            pool.sem_inc(s_ldfree, 2)
            zero_accumulators(pool, [acc2], zeros, [s_add])
            with pool.Fori(0, NG // 2) as b:
                for h in range(2):
                    g = b * 2 + h
                    pool.wait_ge(s_ld[h], (b + 1) * 48)
                    pool.wait_ge(s_gfree, g + 1)
                    pool.sem_inc(s_go, 1)
                    for u in range(G):
                        pool.indirect_dma_start(xs[:, h, u, :], None, hs_tab,
                                                bass.IndirectOffsetOnAxis(isrc[:, h, u:u + 1], 0)).then_inc(s_ge[h][u], 16)
                    for u in range(G):
                        pool.wait_ge(s_msg, g * G + u + 3)
                        pool.wait_ge(s_add, (g * G + u + 1) * 16)
                        pool.sem_inc(s_go, 1)
                        pool.indirect_dma_start(acc2, bass.IndirectOffsetOnAxis(iout[:, h, u:u + 1], 0),
                                                msg[:, u % 2, :], None, compute_op=ALU.add).then_inc(s_add, 16)
                    pool.wait_ge(s_add, (g * G + G + 1) * 16)
                    pool.sem_inc(s_ldfree, 1)

        @block.tensor
        def _(pe):
            with pe.Fori(0, NG // 2) as b:
                for h in range(2):
                    for u in range(G):
                        n = (b * 2 + h) * G + u
                        pe.wait_ge(s_ge[h][u], (b + 1) * 16)
                        pe.wait_ge(s_same, n + 1)
                        pe.wait_ge(s_msg, n + 1)
                        nc.tensor.matmul(ps_m[:, u % 2, 0:H], same[:, u, :], xs[:, h, u, :], start=True,
                                         stop=True).then_inc(s_sum, 1)

        @block.scalar
        def _(act):
            act.sem_inc(s_msg, 2)
            with act.Fori(0, NG) as g:
                for u in range(G):
                    act.wait_ge(s_sum, g * G + u + 1)
                    act.wait_ge(s_add, g * G * 16 + max(u, 1) * 16)
                    nc.scalar.activation(msg[:, u % 2, :], ps_m[:, u % 2, 0:H], ACT.Copy).then_inc(s_msg, 1)

        @block.vector
        def _(dve):
            dve.sem_inc(s_gfree, 2)
            with dve.Fori(0, NG // 2) as b:
                for h in range(2):
                    g = b * 2 + h
                    nc.vector.tensor_copy(cols[:], dst_f[:, ds(g * G, G)]).then_inc(s_cols, 1)
                    dve.wait_ge(s_ld[h], (b + 1) * 48)
                    dve.wait_ge(s_cols, g + 1)
                    for u in range(G):
                        nc.vector.tensor_scalar(same[:, u, :], rows[:, h, u, :], cols[:, u:u + 1], None,
                                                ALU.is_equal).then_inc(s_same, 1)
                    dve.wait_ge(s_sum, (g + 1) * G)
                    dve.sem_inc(s_gfree, 1)


def edge_layer3(nc, A, src_f, srcu_cols, xr_tab, el_tab, acc3, zeros):
    with Phase(nc, "e3") as ph:
        rows = ph.sb("rows", [P, 2, G, P], I32)
        isrc = ph.sb("isrc", [P, 2, G], I32)
        idst = ph.sb("idst", [P, 2, G], I32)
        iout = ph.sb("iout", [P, 2, G], I32)
        xr = ph.sb("xr", [P, 2, G, XR])
        el = ph.sb("el", [P, 2, G, HEADS])
        z = ph.sb("z", [P, 2, G, HEADS])
        pay = ph.sb("pay", [P, G, PAY])
        cols = ph.sb("cols", [P, G])
        same = ph.sb("same", [P, G, P])
        msg = ph.sb("msg", [P, KACC, PAY])
        ps_m = ph.ps("ps_m", [P, 2, 512])
        s_ld = ph.sems("ld", 2)
        s_ge = ph.sems("ge", 2)
        s_ldfree, s_gfree, s_go, s_cols, s_z, s_exp, s_pay, s_same, s_sum, s_msg = (
            ph.sem(n) for n in ("ldfree", "gfree", "go", "cols", "z", "exp", "pay", "same", "sum", "msg"))
        s_add = ph.sems("add", KACC)
        block = ph.block()

        @block.sync
        def _(sp):
            with sp.Fori(0, NG // 2) as b:
                for h in range(2):
                    g = b * 2 + h
                    sp.wait_ge(s_ldfree, g + 1)
                    sp.dma_start(rows[:, h].rearrange("p u f -> p (u f)"),
                                 bcast_rows(A["src_rows"][ds(g * G * P, G * P)], P)).then_inc(s_ld[h], 16)
                    sp.dma_start(isrc[:, h, :], A["src_cols"][:, ds(g * G, G)]).then_inc(s_ld[h], 16)
                    sp.dma_start(idst[:, h, :], A["dst_cols"][:, ds(g * G, G)]).then_inc(s_ld[h], 16)
                    sp.dma_start(iout[:, h, :], srcu_cols[:, ds(g * G, G)]).then_inc(s_ld[h], 16)

        @block.gpsimd
        def _(pool):
            pool.sem_inc(s_ldfree, 2)
            zero_accumulators(pool, acc3, zeros, s_add)
            with pool.Fori(0, NG // 2) as b:
                for h in range(2):
                    g = b * 2 + h
                    pool.wait_ge(s_ld[h], (b + 1) * 64)
                    pool.wait_ge(s_gfree, g + 1)
                    pool.sem_inc(s_go, 1)
                    for u in range(G):
                        pool.indirect_dma_start(xr[:, h, u, :], None, xr_tab,
                                                bass.IndirectOffsetOnAxis(idst[:, h, u:u + 1], 0)).then_inc(s_ge[h], 16)
                        pool.indirect_dma_start(el[:, h, u, :], None, el_tab,
                                                bass.IndirectOffsetOnAxis(isrc[:, h, u:u + 1], 0)).then_inc(s_ge[h], 16)
                    for u in range(G):
                        pool.wait_ge(s_msg, g * G + u + 3)
                        pool.wait_ge(s_add[u % KACC], (g * (G // KACC) + u // KACC + 1) * 16)
                        pool.sem_inc(s_go, 1)
                        pool.indirect_dma_start(acc3[u % KACC], bass.IndirectOffsetOnAxis(iout[:, h, u:u + 1], 0),
                                                msg[:, u % KACC, :], None,
                                                compute_op=ALU.add).then_inc(s_add[u % KACC], 16)
                    for k in range(KACC):
                        pool.wait_ge(s_add[k], ((g + 1) * (G // KACC) + 1) * 16)
                    pool.sem_inc(s_ldfree, 1)

        @block.tensor
        def _(pe):
            with pe.Fori(0, NG // 2) as b:
                for h in range(2):
                    for u in range(G):
                        n = (b * 2 + h) * G + u
                        pe.wait_ge(s_pay, n * 2 + 2)
                        pe.wait_ge(s_msg, n + 1)
                        nc.tensor.matmul(ps_m[:, u % 2, 0:PAY], same[:, u, :], pay[:, u, :], start=True,
                                         stop=True).then_inc(s_sum, 1)

        @block.scalar
        def _(act):
            act.sem_inc(s_msg, 2)
            with act.Fori(0, NG) as g:
                act.wait_ge(s_z, (g + 1) * 2)
                nc.scalar.activation(pay[:, :, HEADS * DOUT:PAY], z[:, 1, :, :], ACT.Exp).then_inc(s_exp, 1)
                for u in range(G):
                    act.wait_ge(s_sum, g * G + u + 1)
                    act.wait_ge(s_add[u % KACC], (g * (G // KACC) + u // KACC + 1) * 16)
                    nc.scalar.activation(msg[:, u % KACC, :], ps_m[:, u % 2, 0:PAY], ACT.Copy).then_inc(s_msg, 1)

        @block.vector
        def _(dve):
            dve.sem_inc(s_gfree, 2)
            with dve.Fori(0, NG // 2) as b:
                for h in range(2):
                    g = b * 2 + h
                    nc.vector.tensor_copy(cols[:], src_f[:, ds(g * G, G)]).then_inc(s_cols, 1)
                    dve.wait_ge(s_ge[h], (b + 1) * 2 * G * 16)
                    nc.vector.tensor_tensor(z[:, 0, :, :], el[:, h, :, :], xr[:, h, :, DOUT:XR],
                                            ALU.add).then_inc(s_z, 1)
                    dve.wait_ge(s_z, g * 2 + 1)
                    nc.vector.scalar_tensor_tensor(z[:, 1, :, :], z[:, 0, :, :], 0.2, z[:, 0, :, :],
                                                   ALU.mult, ALU.max).then_inc(s_z, 1)
                    dve.wait_ge(s_ld[h], (b + 1) * 64)
                    dve.wait_ge(s_cols, g + 1)
                    for u in range(G):
                        nc.vector.tensor_scalar(same[:, u, :], rows[:, h, u, :], cols[:, u:u + 1], None,
                                                ALU.is_equal).then_inc(s_same, 1)
                    dve.wait_ge(s_exp, g + 1)
                    for u in range(G):
                        for e in range(2):
                            x2 = xr[:, h, u, None, 0:DOUT].to_broadcast([P, 2, DOUT])
                            e2 = pay[:, u, HEADS * DOUT + 2 * e:HEADS * DOUT + 2 * e + 2][:, :, None]
                            nc.vector.tensor_tensor(
                                pay[:, u, e * 2 * DOUT:(e + 1) * 2 * DOUT].rearrange("p (a d) -> p a d", a=2),
                                x2, e2.to_broadcast([P, 2, DOUT]), ALU.mult).then_inc(s_pay, 1)
                    dve.wait_ge(s_sum, (g + 1) * G)
                    dve.sem_inc(s_gfree, 1)


def node_after0(nc, A, ident, ones_row, tiles, acc0, x1_tab):
    with Phase(nc, "n0") as ph:
        w = ph.sb("w", [P, 2, H])
        bias = ph.sb("bias", [1, H])
        x = ph.sb("x", [P, NB, H])
        agg = ph.sb("agg", [P, NB, H])
        xT = ph.sb("xT", [P, 2, 2, P])
        y = ph.sb("y", [P, NB, H])
        yhat = ph.sb("yhat", [P, NB, H])
        stats = ph.sb("stats", [P, NB, 6])
        mv = ph.sb("mv", [P, NB, 2])
        rstd = ph.sb("rstd", [P, 3, NB])
        ps_t = ph.ps("ps_t", [P, 2, 4, P])
        ps_y = ph.ps("ps_y", [P, 2, 512])
        (s_w, s_ld, s_free, s_stats, s_var, s_sqrt, s_rinv, s_norm, s_t, s_xT, s_y, s_ys, s_go, s_st,
         s_yfree) = (ph.sem(n) for n in ("w", "ld", "free", "stats", "var", "sqrt", "rinv", "norm", "t", "xT", "y",
                                         "ys", "go", "st", "yfree"))
        block = ph.block()
        IT = NT // NB

        @block.sync
        def _(sp):
            sp.dma_start(w[:], A["WoT"].rearrange("(c p) n -> p c n", p=P)).then_inc(s_w, 16)
            sp.dma_start(bias[:], A["bo"].rearrange("(a n) -> a n", a=1)).then_inc(s_w, 16)
            with sp.Fori(0, IT) as it:
                sp.wait_ge(s_free, it + 1)
                sp.dma_start(x[:], tiles(A["x"])[:, ds(it * NB, NB), :]).then_inc(s_ld, 16)
                sp.dma_start(agg[:], tiles(acc0)[:, ds(it * NB, NB), :]).then_inc(s_ld, 16)

        @block.tensor
        def _(pe):
            pe.wait_ge(s_w, 32)
            with pe.Fori(0, IT) as it:
                pe.wait_ge(s_ld, (it + 1) * 32)
                for u in range(NB):
                    n = it * NB + u
                    pe.wait_ge(s_y, n + 1)
                    for c in range(2):
                        nc.tensor.transpose(ps_t[:, 0, c, :], agg[:, u, c * P:(c + 1) * P], ident[:]).then_inc(s_t, 1)
                    pe.wait_ge(s_xT, n + 1)
                    o = ps_y[:, 0, 0:H]
                    nc.tensor.matmul(o, xT[:, 0, 0, :], w[:, 0, :], start=True, stop=False)
                    nc.tensor.matmul(o, xT[:, 0, 1, :], w[:, 1, :], start=False, stop=False)
                    nc.tensor.matmul(o, ones_row[:], bias[:], start=False, stop=True).then_inc(s_ys, 1)

        @block.scalar
        def _(act):
            with act.Fori(0, IT) as it:
                for u in range(NB):
                    n = it * NB + u
                    act.wait_ge(s_t, n * 2 + 2)
                    nc.scalar.activation(xT[:, 0, :, :], ps_t[:, 0, 0:2, :], ACT.Copy).then_inc(s_xT, 1)
                layernorm_root(nc, act, rstd, s_var, s_sqrt, it)

        @block.vector
        def _(dve):
            dve.sem_inc(s_free, 1)
            dve.sem_inc(s_y, 1)
            with dve.Fori(0, IT) as it:
                for u in range(NB):
                    dve.wait_ge(s_ys, it * NB + u + 1)
                    nc.vector.scalar_tensor_tensor(y[:, u, :], x[:, u, :], 2.0, ps_y[:, 0, 0:H], ALU.mult,
                                                   ALU.add).then_inc(s_y, 1)
                dve.wait_ge(s_y, (it + 1) * NB + 1)
                dve.sem_inc(s_free, 1)
                dve.wait_ge(s_yfree, it + 1)
                layernorm_batch(nc, dve, y, yhat, stats, mv, rstd, s_stats, s_var, s_sqrt, s_rinv, s_norm, s_go, it)

        store_batches(nc, block, [(tiles(x1_tab), yhat)], s_norm, NB, 0, s_go, s_st, s_yfree)


def store_batches(nc, block, pairs, s_ready, per, extra, s_go, s_st, s_free):
    @block.gpsimd
    def _(pool):
        pool.sem_inc(s_free, 1)
        with pool.Fori(0, NT // NB) as it:
            pool.wait_ge(s_ready, (it + 1) * per + extra)
            pool.sem_inc(s_go, 1)
            for dst, buf in pairs:
                pool.dma_start(dst[:, ds(it * NB, NB), :], buf[:]).then_inc(s_st, 16)
            pool.wait_ge(s_st, (it + 1) * 16 * len(pairs))
            pool.sem_inc(s_free, 1)


def node_after1(nc, A, ident, ones_row, tiles, acc1, x1_tab, x2_tab, hs_tab, dinv):
    IT = NT // NB
    with Phase(nc, "n1") as outer:
        hT = outer.sb("hT", [P, 2, NP])
        with Phase(nc, "n1a") as ph:
            w1 = ph.sb("w1", [P, 2, H])
            w2 = ph.sb("w2", [P, 2, H])
            b1 = ph.sb("b1", [P, 2])
            b2 = ph.sb("b2", [P, 2])
            part = ph.sb("part", [P, KACC, NB, H])
            agg = ph.sb("agg", [P, NB, H])
            aT = ph.sb("aT", [P, 2, P])
            hid = ph.sb("hid", [P, 2, P])
            ps_t = ph.ps("ps_t", [P, 512])
            ps_u = ph.ps("ps_u", [P, 2, 512])
            ps_h = ph.ps("ps_h", [P, 2, 512])
            s_w, s_ld, s_free, s_sum, s_t, s_aT, s_u, s_hid, s_h, s_hT, s_dyn = (
                ph.sem(n) for n in ("w", "ld", "free", "sum", "t", "aT", "u", "hid", "h", "hT", "dyn"))
            block = ph.block()

            @block.sync
            def _(sp):
                sp.dma_start(w1[:], A["Wu1"].rearrange("(c p) n -> p c n", p=P)).then_inc(s_w, 16)
                sp.dma_start(w2[:], A["Wu2"].rearrange("(c p) n -> p c n", p=P)).then_inc(s_w, 16)
                sp.dma_start(b1[:], A["bu1"].rearrange("(c p) -> p c", p=P)).then_inc(s_w, 16)
                sp.dma_start(b2[:], A["bu2"].rearrange("(c p) -> p c", p=P)).then_inc(s_w, 16)
                with sp.Fori(0, IT) as it:
                    sp.wait_ge(s_free, it + 1)
                    for k in range(KACC):
                        sp.dma_start(part[:, k], tiles(acc1[k])[:, ds(it * NB, NB), :]).then_inc(s_ld, 16)

            @block.tensor
            def _(pe):
                pe.wait_ge(s_w, 64)
                pe.sem_inc(s_dyn, 1)
                with pe.Fori(0, IT) as it:
                    for u in range(NB):
                        n = it * NB + u
                        pe.wait_ge(s_sum, (it + 1) * 3)
                        for c in range(2):
                            nc.tensor.transpose(ps_t[:, c * P:(c + 1) * P], agg[:, u, c * P:(c + 1) * P],
                                                ident[:]).then_inc(s_t, 1)
                        pe.wait_ge(s_aT, n + 1)
                        for c in range(2):
                            for k in range(2):
                                nc.tensor.matmul(ps_u[:, c, 0:P], w1[:, k, c * P:(c + 1) * P], aT[:, k, :],
                                                 start=(k == 0), stop=(k == 1)).then_inc(s_u, 1)
                        pe.wait_ge(s_hid, n * 2 + 2)
                        pe.wait_ge(s_hT, n * 2 + 1)
                        for c in range(2):
                            for k in range(2):
                                nc.tensor.matmul(ps_h[:, c, 0:P], w2[:, k, c * P:(c + 1) * P], hid[:, k, :],
                                                 start=(k == 0), stop=(k == 1)).then_inc(s_h, 1)

            @block.scalar
            def _(act):
                act.wait_ge(s_w, 64)
                act.sem_inc(s_dyn, 1)
                with act.Fori(0, NT) as n:
                    act.wait_ge(s_t, n * 2 + 2)
                    nc.scalar.activation(aT[:].rearrange("p a b -> p (a b)"), ps_t[:, 0:2 * P], ACT.Copy).then_inc(s_aT, 1)
                    act.wait_ge(s_u, n * 4 + 4)
                    for c in range(2):
                        nc.scalar.activation(hid[:, c, :], ps_u[:, c, 0:P], ACT.Silu,
                                             bias=b1[:, c:c + 1]).then_inc(s_hid, 1)

            @block.vector
            def _(dve):
                dve.sem_inc(s_hT, 1)
                dve.sem_inc(s_free, 1)
                with dve.Fori(0, IT) as it:
                    dve.wait_ge(s_ld, (it + 1) * 16 * KACC)
                    nc.vector.tensor_tensor(part[:, 0], part[:, 0], part[:, 1], ALU.add).then_inc(s_sum, 1)
                    nc.vector.tensor_tensor(part[:, 2], part[:, 2], part[:, 3], ALU.add).then_inc(s_sum, 1)
                    dve.wait_ge(s_sum, it * 3 + 2)
                    nc.vector.tensor_tensor(agg[:], part[:, 0], part[:, 2], ALU.add).then_inc(s_sum, 1)
                    dve.wait_ge(s_sum, it * 3 + 3)
                    dve.sem_inc(s_free, 1)
                    for u in range(NB):
                        n = it * NB + u
                        dve.wait_ge(s_h, n * 4 + 4)
                        for c in range(2):
                            nc.vector.tensor_scalar(hT[:, c, ds(n * P, P)], ps_h[:, c, 0:P], b2[:, c:c + 1], None,
                                                    ALU.add).then_inc(s_hT, 1)

        with Phase(nc, "n1b") as ph:
            w = ph.sb("w", [P, 2, H])
            gamma = ph.sb("gamma", [P, 2])
            beta = ph.sb("beta", [P, 2])
            chunks = [(c, min(512, N - c)) for c in range(0, N, 512)]
            bstats = ph.sb("bstats", [P, 2, len(chunks), 6])
            bmv = ph.sb("bmv", [P, 2, 2])
            bn = ph.sb("bn", [P, 5, 2])
            hb = ph.sb("hb", [P, 2, P])
            x = ph.sb("x", [P, NB, H])
            y = ph.sb("y", [P, NB, H])
            yhat = ph.sb("yhat", [P, NB, H])
            xT = ph.sb("xT", [P, 2, P])
            hs = ph.sb("hs", [P, NB, H])
            dcol = ph.sb("dcol", [P, NB])
            stats = ph.sb("stats", [P, NB, 6])
            mv = ph.sb("mv", [P, NB, 2])
            rstd = ph.sb("rstd", [P, 3, NB])
            ps_b = ph.ps("ps_b", [P, 512])
            ps_t = ph.ps("ps_t", [P, 512])
            ps_y = ph.ps("ps_y", [P, 512])
            (s_w, s_ld, s_free, s_stats, s_var, s_sqrt, s_rinv, s_norm, s_t, s_xT, s_y, s_ys, s_go, s_st,
             s_yfree, s_hb, s_b, s_bn, s_bsq, s_hs, s_dc) = (
                ph.sem(n) for n in ("w", "ld", "free", "stats", "var", "sqrt", "rinv", "norm", "t", "xT", "y",
                                    "ys", "go", "st", "yfree", "hb", "b", "bn", "bsq", "hs", "dc"))
            block = ph.block()

            @block.sync
            def _(sp):
                sp.dma_start(w[:], A["W2"].rearrange("(c p) n -> p c n", p=P)).then_inc(s_w, 16)
                sp.dma_start(gamma[:], A["gamma"].rearrange("(c p) -> p c", p=P)).then_inc(s_w, 16)
                sp.dma_start(beta[:], A["beta"].rearrange("(c p) -> p c", p=P)).then_inc(s_w, 16)
                with sp.Fori(0, IT) as it:
                    sp.wait_ge(s_free, it + 1)
                    sp.dma_start(x[:], tiles(x1_tab)[:, ds(it * NB, NB), :]).then_inc(s_ld, 16)

            @block.tensor
            def _(pe):
                pe.wait_ge(s_w, 48)
                with pe.Fori(0, IT) as it:
                    for u in range(NB):
                        n = it * NB + u
                        pe.wait_ge(s_hb, n * 2 + 2)
                        pe.wait_ge(s_y, n + 1)
                        for c in range(2):
                            nc.tensor.transpose(ps_b[:, c * P:(c + 1) * P], hb[:, c, :], ident[:]).then_inc(s_b, 1)
                    for u in range(NB):
                        n = it * NB + u
                        pe.wait_ge(s_norm, n + 1)
                        for c in range(2):
                            nc.tensor.transpose(ps_t[:, c * P:(c + 1) * P], yhat[:, u, c * P:(c + 1) * P],
                                                ident[:]).then_inc(s_t, 1)
                        pe.wait_ge(s_xT, n + 1)
                        pe.wait_ge(s_hs, n + 1)
                        nc.tensor.matmul(ps_y[:, 0:H], xT[:, 0, :], w[:, 0, :], start=True, stop=False)
                        nc.tensor.matmul(ps_y[:, 0:H], xT[:, 1, :], w[:, 1, :], start=False, stop=True).then_inc(s_ys, 1)

            @block.scalar
            def _(act):
                act.wait_ge(s_bn, 1)
                nc.scalar.activation(bn[:, 1, :], bn[:, 0, :], ACT.Sqrt).then_inc(s_bsq, 1)
                act.sem_inc(s_hs, 1)
                with act.Fori(0, IT) as it:
                    layernorm_root(nc, act, rstd, s_var, s_sqrt, it)
                    act.wait_ge(s_dc, it + 1)
                    act.wait_ge(s_yfree, it + 1)
                    act.sem_inc(s_go, 1)
                    for u in range(NB):
                        n = it * NB + u
                        act.wait_ge(s_t, n * 2 + 2)
                        nc.scalar.activation(xT[:].rearrange("p a b -> p (a b)"), ps_t[:, 0:2 * P], ACT.Copy).then_inc(s_xT, 1)
                        act.wait_ge(s_ys, n + 1)
                        nc.scalar.activation(hs[:, u, :], ps_y[:, 0:H], ACT.Copy, scale=dcol[:, u:u + 1]).then_inc(s_hs, 1)

            @block.vector
            def _(dve):
                for c in range(2):
                    for k, (a, m) in enumerate(chunks):
                        nc.vector.bn_stats(bstats[:, c, k, :], hT[:, c, a:a + m]).then_inc(s_stats, 1)
                nb = 2 * len(chunks)
                dve.wait_ge(s_stats, nb)
                for c in range(2):
                    nc.vector.bn_aggr(bmv[:, c, :], bstats[:, c, :, :]).then_inc(s_dc, 1)
                dve.wait_ge(s_dc, 2)
                nc.vector.tensor_scalar(bn[:, 0, :], bmv[:, :, 1], LN_EPS, None, ALU.add).then_inc(s_bn, 1)
                dve.wait_ge(s_bsq, 1)
                nc.vector.reciprocal(bn[:, 2, :], bn[:, 1, :]).then_inc(s_bn, 1)
                dve.wait_ge(s_bn, 2)
                dve.wait_ge(s_w, 48)
                nc.vector.tensor_tensor(bn[:, 3, :], bn[:, 2, :], gamma[:], ALU.mult).then_inc(s_bn, 1)
                dve.wait_ge(s_bn, 3)
                nc.vector.tensor_tensor(bn[:, 4, :], bn[:, 3, :], bmv[:, :, 0], ALU.mult).then_inc(s_bn, 1)
                dve.wait_ge(s_bn, 4)
                nc.vector.tensor_tensor(bn[:, 4, :], beta[:], bn[:, 4, :], ALU.subtract).then_inc(s_bn, 1)
                dve.wait_ge(s_bn, 5)
                dve.sem_inc(s_free, 1)
                dve.sem_inc(s_y, 1)
                with dve.Fori(0, IT) as it:
                    dve.wait_ge(s_ld, (it + 1) * 16)
                    for u in range(NB):
                        n = it * NB + u
                        for c in range(2):
                            nc.vector.tensor_scalar(hb[:, c, :], hT[:, c, ds(n * P, P)], bn[:, 3, c:c + 1],
                                                    bn[:, 4, c:c + 1], ALU.mult, ALU.add).then_inc(s_hb, 1)
                        dve.wait_ge(s_b, n * 2 + 2)
                        nc.vector.scalar_tensor_tensor(y[:, u, :], x[:, u, :], 2.0, ps_b[:, 0:H], ALU.mult,
                                                       ALU.add).then_inc(s_y, 1)
                    dve.wait_ge(s_y, (it + 1) * NB + 1)
                    dve.sem_inc(s_free, 1)
                    dve.wait_ge(s_yfree, it + 1)
                    dve.wait_ge(s_hs, it * NB + 1)
                    dve.sem_inc(s_go, 1)
                    nc.vector.tensor_copy(dcol[:], dinv[:, ds(it * NB, NB)]).then_inc(s_dc, 1)
                    stats_from(nc, dve, y, yhat, stats, mv, rstd, s_stats, s_var, s_sqrt, s_rinv, s_norm, s_go, it, nb)

            @block.gpsimd
            def _(pool):
                pool.sem_inc(s_yfree, 1)
                with pool.Fori(0, IT) as it:
                    pool.wait_ge(s_norm, (it + 1) * NB)
                    pool.sem_inc(s_go, 1)
                    pool.dma_start(tiles(x2_tab)[:, ds(it * NB, NB), :], yhat[:]).then_inc(s_st, 16)
                    pool.wait_ge(s_hs, (it + 1) * NB + 1)
                    pool.sem_inc(s_go, 1)
                    pool.dma_start(tiles(hs_tab)[:, ds(it * NB, NB), :], hs[:]).then_inc(s_st, 16)
                    pool.wait_ge(s_st, (it + 1) * 32)
                    pool.sem_inc(s_yfree, 1)


def stats_from(nc, dve, y, yhat, stats, mv, rstd, s_stats, s_var, s_sqrt, s_rinv, s_norm, s_go, it, before):
    for u in range(NB):
        nc.vector.bn_stats(stats[:, u, :], y[:, u, :]).then_inc(s_stats, 1)
    dve.wait_ge(s_stats, (it + 1) * 2 * NB - NB + before)
    dve.sem_inc(s_go, 1)
    for u in range(NB):
        nc.vector.bn_aggr(mv[:, u, :], stats[:, u, :]).then_inc(s_stats, 1)
    dve.wait_ge(s_stats, (it + 1) * 2 * NB + before)
    nc.vector.tensor_scalar(rstd[:, 0, :], mv[:, :, 1], LN_EPS, None, ALU.add).then_inc(s_var, 1)
    dve.wait_ge(s_sqrt, it + 1)
    nc.vector.reciprocal(rstd[:, 2, :], rstd[:, 1, :]).then_inc(s_rinv, 1)
    dve.wait_ge(s_rinv, it + 1)
    for u in range(NB):
        nc.vector.tensor_scalar(yhat[:, u, :], y[:, u, :], mv[:, u, 0:1], rstd[:, 2, u:u + 1],
                                ALU.subtract, ALU.mult).then_inc(s_norm, 1)
    dve.wait_ge(s_norm, (it + 1) * NB)
    dve.sem_inc(s_go, 1)


def node_after2(nc, A, ident, ones_row, tiles, acc2, hs_tab, x2_tab, x3_tab, xr_tab, el_tab, dinv):
    IT = NT // NB
    WC = DOUT + 2 * HEADS
    with Phase(nc, "n2") as ph:
        w = ph.sb("w", [P, 2, WC])
        wT = ph.sb("wT", [DOUT, 2, P])
        wlr = ph.sb("wlr", [DOUT, 2 * HEADS])
        bias = ph.sb("bias", [P, H])
        dcol = ph.sb("dcol", [P, NB])
        x = ph.sb("x", [P, 3, NB, H])
        t = ph.sb("t", [P, 3, NB, H])
        y = ph.sb("y", [P, NB, H])
        yhat = ph.sb("yhat", [P, NB, H])
        xT = ph.sb("xT", [P, 2, P])
        xr = ph.sb("xr", [P, NB, WC])
        stats = ph.sb("stats", [P, NB, 6])
        mv = ph.sb("mv", [P, NB, 2])
        rstd = ph.sb("rstd", [P, 3, NB])
        ps_w = ph.ps("ps_w", [P, 512])
        ps_t = ph.ps("ps_t", [P, 512])
        ps_y = ph.ps("ps_y", [P, 512])
        (s_w, s_ld, s_free, s_stats, s_var, s_sqrt, s_rinv, s_norm, s_t, s_xT, s_e, s_ys, s_go, s_st,
         s_yfree, s_wp, s_wc, s_xr) = (
            ph.sem(n) for n in ("w", "ld", "free", "stats", "var", "sqrt", "rinv", "norm", "t", "xT", "e",
                                "ys", "go", "st", "yfree", "wp", "wc", "xr"))
        block = ph.block()

        @block.sync
        def _(sp):
            sp.dma_start(w[:, :, 0:DOUT], A["W3"].rearrange("(c p) n -> p c n", p=P)).then_inc(s_w, 16)
            sp.dma_start(wT[:], A["W3T"].rearrange("k (c n) -> k c n", c=2)).then_inc(s_w, 16)
            sp.dma_start(wlr[:, 0:HEADS], A["WrT"]).then_inc(s_w, 16)
            sp.dma_start(wlr[:, HEADS:], A["WlT"]).then_inc(s_w, 16)
            sp.dma_start(bias[:], bcast_rows(A["b2"], P)).then_inc(s_w, 16)
            with sp.Fori(0, IT) as it:
                sp.wait_ge(s_free, it + 1)
                for k, tab in enumerate((acc2, hs_tab, x2_tab)):
                    sp.dma_start(x[:, k], tiles(tab)[:, ds(it * NB, NB), :]).then_inc(s_ld, 16)

        @block.tensor
        def _(pe):
            pe.wait_ge(s_w, 80)
            for c in range(2):
                nc.tensor.matmul(ps_w[:, c * 8:c * 8 + 8], wT[:, c, :], wlr[:], start=True, stop=True).then_inc(s_wp, 1)
            pe.wait_ge(s_wc, 1)
            pe.sem_inc(s_go, 1)
            with pe.Fori(0, IT) as it:
                for u in range(NB):
                    n = it * NB + u
                    pe.wait_ge(s_norm, n + 1)
                    for c in range(2):
                        nc.tensor.transpose(ps_t[:, c * P:(c + 1) * P], yhat[:, u, c * P:(c + 1) * P],
                                            ident[:]).then_inc(s_t, 1)
                    pe.wait_ge(s_xT, n + 1)
                    pe.wait_ge(s_xr, n + 1)
                    nc.tensor.matmul(ps_y[:, 0:WC], xT[:, 0, :], w[:, 0, :], start=True, stop=False)
                    nc.tensor.matmul(ps_y[:, 0:WC], xT[:, 1, :], w[:, 1, :], start=False, stop=True).then_inc(s_ys, 1)

        @block.scalar
        def _(act):
            act.wait_ge(s_wp, 2)
            nc.scalar.activation(w[:, :, DOUT:WC], ps_w[:, 0:16].rearrange("p (c n) -> p c n", c=2),
                                 ACT.Copy).then_inc(s_wc, 1)
            act.sem_inc(s_xr, 1)
            with act.Fori(0, IT) as it:
                layernorm_root(nc, act, rstd, s_var, s_sqrt, it)
                act.wait_ge(s_yfree, it + 1)
                act.sem_inc(s_go, 1)
                for u in range(NB):
                    n = it * NB + u
                    act.wait_ge(s_t, n * 2 + 2)
                    nc.scalar.activation(xT[:].rearrange("p a b -> p (a b)"), ps_t[:, 0:2 * P], ACT.Copy).then_inc(s_xT, 1)
                    act.wait_ge(s_ys, n + 1)
                    nc.scalar.activation(xr[:, u, :], ps_y[:, 0:WC], ACT.Copy).then_inc(s_xr, 1)

        @block.vector
        def _(dve):
            dve.sem_inc(s_free, 1)
            S = 3 + NB
            with dve.Fori(0, IT) as it:
                dve.wait_ge(s_ld, (it + 1) * 48)
                nc.vector.tensor_tensor(t[:, 0], x[:, 0], x[:, 1], ALU.add)
                nc.vector.tensor_copy(dcol[:], dinv[:, ds(it * NB, NB)]).then_inc(s_e, 1)
                dve.wait_ge(s_e, it * S + 1)
                for u in range(NB):
                    nc.vector.scalar_tensor_tensor(t[:, 1, u, :], t[:, 0, u, :], dcol[:, u:u + 1], bias[:], ALU.mult,
                                                   ALU.add).then_inc(s_e, 1)
                dve.wait_ge(s_e, it * S + 1 + NB)
                nc.vector.scalar_tensor_tensor(t[:, 2], t[:, 1], 0.2, t[:, 1], ALU.mult, ALU.max).then_inc(s_e, 1)
                dve.wait_ge(s_e, it * S + 2 + NB)
                nc.vector.tensor_tensor(y[:], t[:, 2], x[:, 2], ALU.add).then_inc(s_e, 1)
                dve.wait_ge(s_e, it * S + S)
                dve.sem_inc(s_free, 1)
                dve.wait_ge(s_yfree, it + 1)
                layernorm_batch(nc, dve, y, yhat, stats, mv, rstd, s_stats, s_var, s_sqrt, s_rinv, s_norm, s_go, it)

        @block.gpsimd
        def _(pool):
            pool.sem_inc(s_yfree, 1)
            with pool.Fori(0, IT) as it:
                pool.wait_ge(s_norm, (it + 1) * NB)
                pool.sem_inc(s_go, 1)
                pool.dma_start(tiles(x3_tab)[:, ds(it * NB, NB), :], yhat[:]).then_inc(s_st, 16)
                pool.wait_ge(s_xr, (it + 1) * NB + 1)
                pool.sem_inc(s_go, 1)
                pool.dma_start(tiles(xr_tab)[:, ds(it * NB, NB), :], xr[:, :, 0:XR]).then_inc(s_st, 16)
                pool.dma_start(tiles(el_tab)[:, ds(it * NB, NB), :], xr[:, :, XR:WC]).then_inc(s_st, 16)
                pool.wait_ge(s_st, (it + 1) * 48)
                pool.sem_inc(s_yfree, 1)


def node_after3(nc, A, tiles, acc3, x3_tab, out):
    IT = NT // NB
    HD = HEADS * DOUT
    with Phase(nc, "n3") as ph:
        bias = ph.sb("bias", [P, HD])
        part = ph.sb("part", [P, KACC, NB, PAY])
        x = ph.sb("x", [P, NB, H])
        den = ph.sb("den", [P, 2, NB, HEADS])
        z = ph.sb("z", [P, NB, HD])
        neg = ph.sb("neg", [P, NB, HD])
        ex = ph.sb("ex", [P, NB, HD])
        pos = ph.sb("pos", [P, NB, HD])
        y = ph.sb("y", [P, NB, H])
        yhat = ph.sb("yhat", [P, NB, H])
        stats = ph.sb("stats", [P, NB, 6])
        mv = ph.sb("mv", [P, NB, 2])
        rstd = ph.sb("rstd", [P, 3, NB])
        (s_w, s_ld, s_free, s_stats, s_var, s_sqrt, s_rinv, s_norm, s_e, s_neg, s_ex, s_go, s_st,
         s_yfree) = (
            ph.sem(n) for n in ("w", "ld", "free", "stats", "var", "sqrt", "rinv", "norm", "e", "neg", "ex",
                                "go", "st", "yfree"))
        block = ph.block()

        @block.sync
        def _(sp):
            for hd in range(HEADS):
                sp.dma_start(bias[:, hd * DOUT:(hd + 1) * DOUT], bcast_rows(A["b3"], P)).then_inc(s_w, 16)
            with sp.Fori(0, IT) as it:
                sp.wait_ge(s_free, it + 1)
                for k in range(KACC):
                    sp.dma_start(part[:, k], tiles(acc3[k])[:, ds(it * NB, NB), :]).then_inc(s_ld, 16)
                sp.dma_start(x[:], tiles(x3_tab)[:, ds(it * NB, NB), :]).then_inc(s_ld, 16)

        @block.scalar
        def _(act):
            with act.Fori(0, IT) as it:
                act.wait_ge(s_neg, it + 1)
                nc.scalar.activation(ex[:], neg[:], ACT.Exp).then_inc(s_ex, 1)
                layernorm_root(nc, act, rstd, s_var, s_sqrt, it)

        @block.vector
        def _(dve):
            dve.sem_inc(s_free, 1)
            dve.wait_ge(s_w, 64)
            nc.vector.memset(rstd[:], 0.0)
            S = 5 + NB * HEADS + 2 + 1
            with dve.Fori(0, IT) as it:
                e = it * S
                dve.wait_ge(s_ld, (it + 1) * 16 * (KACC + 1))
                nc.vector.tensor_tensor(part[:, 0], part[:, 0], part[:, 1], ALU.add).then_inc(s_e, 1)
                nc.vector.tensor_tensor(part[:, 2], part[:, 2], part[:, 3], ALU.add).then_inc(s_e, 1)
                dve.wait_ge(s_e, e + 2)
                nc.vector.tensor_tensor(part[:, 0], part[:, 0], part[:, 2], ALU.add).then_inc(s_e, 1)
                dve.wait_ge(s_e, e + 3)
                nc.vector.tensor_scalar(den[:, 0], part[:, 0, :, HD:PAY], 1e-12, None, ALU.max).then_inc(s_e, 1)
                dve.wait_ge(s_e, e + 4)
                nc.vector.reciprocal(den[:, 1], den[:, 0]).then_inc(s_e, 1)
                dve.wait_ge(s_e, e + 5)
                for u in range(NB):
                    for hd in range(HEADS):
                        cc = slice(hd * DOUT, (hd + 1) * DOUT)
                        nc.vector.scalar_tensor_tensor(z[:, u, cc], part[:, 0, u, cc], den[:, 1, u, hd:hd + 1],
                                                       bias[:, cc], ALU.mult, ALU.add).then_inc(s_e, 1)
                dve.wait_ge(s_e, e + 5 + NB * HEADS)
                nc.vector.tensor_scalar(neg[:], z[:], 0.0, None, ALU.min).then_inc(s_neg, 1)
                nc.vector.scalar_tensor_tensor(pos[:], z[:], 0.0, x[:], ALU.max, ALU.add).then_inc(s_e, 1)
                dve.wait_ge(s_ex, it + 1)
                dve.wait_ge(s_e, e + 6 + NB * HEADS)
                nc.vector.scalar_tensor_tensor(y[:], ex[:], -1.0, pos[:], ALU.add, ALU.add).then_inc(s_e, 1)
                dve.wait_ge(s_e, e + 7 + NB * HEADS)
                dve.sem_inc(s_free, 1)
                dve.wait_ge(s_yfree, it + 1)
                nc.vector.tensor_scalar(y[:, 0, 0:1], y[:, 0, 0:1], 0.0, None, ALU.add).then_inc(s_e, 1)
                dve.wait_ge(s_e, e + S)
                layernorm_batch(nc, dve, y, yhat, stats, mv, rstd, s_stats, s_var, s_sqrt, s_rinv, s_norm, s_go, it)

        store_batches(nc, block, [(tiles(out), yhat)], s_norm, NB, 0, s_go, s_st, s_yfree)


_INS = ["x", "src_cols", "src_rows", "dst_cols", "dst_rows", "ew_cols", "ea20T", "ea64T", "ln_g", "ln_b",
        "WqT", "bq", "WkT", "bk", "WvT", "bv", "WoT", "bo", "WdkT", "bdk", "WdvT", "bdv",
        "Wf1", "bf1", "Wf2", "bf2", "Wu1", "bu1", "Wu2", "bu2", "gamma", "beta", "W2", "b2",
        "W3", "W3T", "WlT", "WrT", "b3"]


def lay_out(i):
    a = {k: np.asarray(v) for k, v in i.items()}
    pad_n, pad_e = NP - N, EP - E
    x = np.concatenate([a["x"], np.zeros((pad_n, H), np.float32)])
    spare = np.full((pad_e,), N, np.int32)
    src = np.concatenate([a["src"], spare])
    dst = np.concatenate([a["dst"], spare])
    ew = np.concatenate([a["edge_weight"], np.zeros((pad_e,), np.float32)])
    e20 = np.concatenate([a["edge_attr_20"], np.zeros((pad_e, R20), np.float32)])
    e64 = np.concatenate([a["edge_attr_64"], np.zeros((pad_e, R64), np.float32)])
    d = {"x": x, "src_cols": src.reshape(ET, P).T, "src_rows": src, "dst_cols": dst.reshape(ET, P).T,
         "dst_rows": dst, "ew_cols": ew.reshape(ET, P).T, "ea20T": e20.T, "ea64T": e64.T,
         "ln_g": a["L0_gnn_ln_g"], "ln_b": a["L0_gnn_ln_b"]}
    for n in ("Wq", "Wk", "Wv", "Wo", "Wdk", "Wdv"):
        d[n + "T"] = a["L0_gnn_" + n].T
    for n in ("bq", "bk", "bv", "bo", "bdk", "bdv"):
        d[n] = a["L0_gnn_" + n]
    for n in ("Wf1", "bf1", "Wf2", "bf2", "Wu1", "bu1", "Wu2", "bu2", "gamma", "beta"):
        d[n] = a["L1_gnn_" + n]
    d["W2"], d["b2"] = a["L2_gnn_W"], a["L2_gnn_b"]
    d["W3"], d["W3T"], d["b3"] = a["L3_gnn_W"], a["L3_gnn_W"].T, a["L3_gnn_b"]
    d["WlT"], d["WrT"] = a["L3_gnn_Wl"].T, a["L3_gnn_Wr"].T
    return {k: np.ascontiguousarray(d[k]) for k in _INS}


def kernel(**inputs):
    import concourse.bacc as _bacc
    from concourse.bass_utils import run_bass_kernel_spmd as _run

    nc = _bacc.Bacc("TRN2", target_bir_lowering=False, num_devices=1)
    arrays, A = {}, {}
    for name, a in lay_out(inputs).items():
        arrays[f"in_{name}_dram"] = a
        A[name] = nc.dram_tensor(f"in_{name}_dram", a.shape, mybir.dt.from_np(a.dtype), kind="ExternalInput").ap()
    out = nc.dram_tensor("out_0_dram", (NP, H), F32, kind="ExternalOutput").ap()
    gnn_kernel(nc, A, out)
    r = _run(nc, [arrays], core_ids=[0])
    return r.results[0]["out_0_dram"][:N]
```

```python
import numpy as np
import concourse.bass as bass
from concourse import mybir
from contextlib import ExitStack

F32 = mybir.dt.float32
F32R = mybir.dt.float32r
I32 = mybir.dt.int32
BF16 = mybir.dt.bfloat16
ALU = mybir.AluOpType
ACT = mybir.ActivationFunctionType
AX = mybir.AxisListType

P = 128
N = 6250
E = 106250
H = 256
R64 = 64
R20 = 20
R20P = 32
B2R = 2 * R20P + 1
HEADS = 4
DOUT = 64
XR = DOUT + HEADS
PAY = HEADS * DOUT + HEADS
NT = -(-N // P) + 1
NP = NT * P
TRASH = NP - P
ET = 832
EP = ET * P
G = 8
NG = ET // G
NB = 5
KACC = 4
LN_EPS = 1e-5
TWO_PI = 2.0 * np.pi
ROUND = 12582912.0
ds = bass.ds


def bcast_rows(ap, n):
    return ap.partition_broadcast(n)


class Phase:

    def __init__(self, nc, name):
        self.nc, self.name, self.ctx, self.used = nc, name, ExitStack(), []

    def __enter__(self):
        self.ctx.__enter__()
        return self

    def __exit__(self, *a):
        r = self.ctx.__exit__(*a)
        if self.used:
            self.nc.clear_and_free_semaphores(self.used)
            self.nc.all_engine_barrier()
        return r

    def sb(self, name, shape, dt=F32):
        return self.ctx.enter_context(self.nc.sbuf_tensor(f"{self.name}_{name}", shape, dt))

    def ps(self, name, shape, dt=F32):
        return self.ctx.enter_context(self.nc.psum_tensor(f"{self.name}_{name}", shape, dt))

    def sem(self, name):
        self.used.append(self.nc.alloc_semaphore(f"{self.name}_{name}"))
        return self.used[-1]

    def sems(self, name, n):
        return [self.sem(f"{name}{i}") for i in range(n)]

    def block(self):
        return self.ctx.enter_context(self.nc.Block())


def layernorm_batch(nc, dve, x, xhat, stats, mv, rstd, s_stats, s_var, s_sqrt, s_rinv, s_norm, s_go, it):
    for u in range(NB):
        nc.vector.bn_stats(stats[:, u, :], x[:, u, :]).then_inc(s_stats, 1)
    dve.wait_ge(s_stats, (it + 1) * 2 * NB - NB)
    dve.sem_inc(s_go, 1)
    for u in range(NB):
        nc.vector.bn_aggr(mv[:, u, :], stats[:, u, :]).then_inc(s_stats, 1)
    dve.wait_ge(s_stats, (it + 1) * 2 * NB)
    nc.vector.tensor_scalar(rstd[:, 0, :], mv[:, :, 1], LN_EPS, None, ALU.add).then_inc(s_var, 1)
    dve.wait_ge(s_sqrt, it + 1)
    nc.vector.reciprocal(rstd[:, 2, :], rstd[:, 1, :]).then_inc(s_rinv, 1)
    dve.wait_ge(s_rinv, it + 1)
    for u in range(NB):
        nc.vector.tensor_scalar(xhat[:, u, :], x[:, u, :], mv[:, u, 0:1], rstd[:, 2, u:u + 1],
                                ALU.subtract, ALU.mult).then_inc(s_norm, 1)
    dve.wait_ge(s_norm, (it + 1) * NB)
    dve.sem_inc(s_go, 1)


def layernorm_root(nc, act, rstd, s_var, s_sqrt, it):
    act.wait_ge(s_var, it + 1)
    nc.scalar.activation(rstd[:, 1, :], rstd[:, 0, :], ACT.Sqrt).then_inc(s_sqrt, 1)


class Tables:
    pass


def gnn_kernel(nc, A, out):
    ctx = ExitStack()
    with ctx, nc.allow_non_contiguous_dma(reason="small tables of weights and indices"):
        def dram(name, shape, dt=F32):
            return nc.dram_tensor(name, shape, dt, kind="Internal").ap()

        def keep(name, shape, dt=F32):
            return ctx.enter_context(nc.sbuf_tensor(name, shape, dt))

        T = Tables()
        T.q_tab = dram("q_tab", [NP, H])
        T.qs_tab = dram("qs_tab", [NP, 2 * H])
        T.kv_tab = dram("kv_tab", [NP, 2 * H])
        T.x1_tab = dram("x1_tab", [NP, H])
        T.x1s_tab = dram("x1s_tab", [NP, 2 * H])
        T.x2_tab = dram("x2_tab", [NP, H])
        T.x3_tab = dram("x3_tab", [NP, H])
        T.hs_tab = dram("hs_tab", [NP, H])
        T.xr_tab = dram("xr_tab", [NP, XR])
        T.el_tab = dram("el_tab", [NP, HEADS])
        T.src_rows = dram("srcf_rows", [EP])
        T.dst_rows = dram("dstf_rows", [EP])
        T.lo_rows = dram("lof_rows", [EP])
        T.srcu_cols = dram("srcu_cols", [P, ET], I32)
        T.dstu_cols = dram("dstu_cols", [P, ET], I32)
        T.acc0 = dram("acc0", [NP, H + 1])
        T.acc1 = [dram(f"acc1_{k}", [NP, H]) for k in range(KACC)]
        T.acc2 = dram("acc2", [NP, H])
        T.acc3 = [dram(f"acc3_{k}", [NP, PAY]) for k in range(KACC)]

        def tiles(ap):
            return ap.rearrange("(t p) d -> p t d", p=P)

        T.ident = keep("ident", [P, P])
        T.iota_row = keep("iota_row", [P, P])
        T.iota_col = keep("iota_col", [P, 1])
        T.iota_hi = keep("iota_hi", [P, NT, HEADS])
        T.earlier = keep("earlier", [P, P])
        T.trash = keep("trash", [P, 1])
        T.src_f = keep("src_f", [P, ET])
        T.dst_f = keep("dst_f", [P, ET])
        T.off_f = keep("off_f", [P, ET])
        T.hi_f = keep("hi_f", [P, ET])
        T.window = keep("window", [P, NG])
        T.base = keep("base", [1, NG], I32)
        T.far = keep("far", [1, 1], I32)
        T.cut = keep("cut", [P, ET])
        T.deg = keep("deg", [P, NT])
        T.dinv = keep("dinv", [P, NT])
        T.ones_row = keep("ones_row", [1, P])
        T.zeros = keep("zeros", [P, PAY])
        T.el_res = keep("el_res", [P, NT, HEADS])

        edge_indices(nc, A, T)
        edge_indices_far(nc, A, T)
        node_qkv(nc, A, T.ident, T.ones_row, tiles, T.q_tab, T.qs_tab, T.kv_tab)
        edge_layer0(nc, A, T)
        node_after0(nc, A, T.ident, T.ones_row, tiles, T.acc0, T.x1_tab, T.x1s_tab, T.deg)
        edge_layer1(nc, A, T)
        node_after1(nc, A, T.ident, T.ones_row, tiles, T.acc1, T.x1_tab, T.x2_tab, T.hs_tab, T.deg, T.dinv)
        edge_layer2(nc, A, T)
        node_after2(nc, A, T.ident, T.ones_row, tiles, T.acc2, T.hs_tab, T.x2_tab, T.x3_tab, T.xr_tab,
                    T.el_tab, T.el_res, T.dinv)
        edge_layer3(nc, A, T)
        node_after3(nc, A, tiles, T.acc3, T.x3_tab, out)


def if_near(eng, T, near, far):
    outside = eng.value_load(T.far[0:1, 0:1], min_val=0, max_val=EP)
    with eng.If(outside < 1):
        near()
    with eng.Else():
        far()


def if_far(eng, T, far):
    outside = eng.value_load(T.far[0:1, 0:1], min_val=0, max_val=EP)
    with eng.If(outside >= 1):
        far()


def edge_indices(nc, A, T):
    with Phase(nc, "ix") as ph:
        src_i = ph.sb("src_i", [P, ET], I32)
        dst_i = ph.sb("dst_i", [P, ET], I32)
        row_i = ph.sb("row_i", [P, 2, ET], I32)
        hi_i = ph.sb("hi_i", [P, ET], I32)
        lo_i = ph.sb("lo_i", [P, ET], I32)
        row_f = ph.sb("row_f", [P, 3, ET])
        ew = ph.sb("ew", [P, ET])
        turn = ph.sb("turn", [P, ET])
        turn_r = ph.sb("turn_r", [P, ET])
        inside = ph.sb("inside", [P, ET])
        half_pi = ph.sb("half_pi", [P, 1])
        first = ph.sb("first", [P, P])
        ones = ph.sb("ones", [P, P])
        beyond = ph.sb("beyond", [P, 2, ET])
        count = ph.sb("count", [P, 2])
        ps_base = ph.ps("ps_base", [P, NG])
        ps_far = ph.ps("ps_far", [P, 2])
        (s_in, s_const, s_f, s_bits, s_rowf, s_turn, s_sin, s_base, s_win, s_off, s_beyond, s_far, s_flag,
         s_out) = (ph.sem(n) for n in ("in", "const", "f", "bits", "rowf", "turn", "sin", "base", "win", "off",
                                       "beyond", "far", "flag", "out"))
        block = ph.block()

        @block.sync
        def _(sp):
            sp.dma_start(src_i[:], A["src_cols"]).then_inc(s_in, 16)
            sp.dma_start(dst_i[:], A["dst_cols"]).then_inc(s_in, 16)
            sp.dma_start(ew[:], A["ew_cols"]).then_inc(s_in, 16)
            sp.dma_start(row_i[:, 0, :], A["src_rows"].rearrange("(p k) -> p k", p=P)).then_inc(s_in, 16)
            sp.dma_start(row_i[:, 1, :], A["dst_rows"].rearrange("(p k) -> p k", p=P)).then_inc(s_in, 16)
            sp.wait_ge(s_rowf, 3)
            for k, tab in enumerate((T.src_rows, T.dst_rows, T.lo_rows)):
                sp.dma_start(tab.rearrange("(p k) -> p k", p=P), row_f[:, k, :]).then_inc(s_out, 16)
            sp.wait_ge(s_out, 48)

        @block.gpsimd
        def _(pool):
            nc.gpsimd.memset(T.ident[:], 0.0).then_inc(s_const, 1)
            nc.gpsimd.memset(T.earlier[:], 1.0).then_inc(s_const, 1)
            nc.gpsimd.memset(ones[:], 1.0).then_inc(s_const, 1)
            nc.gpsimd.memset(first[:], 0.0).then_inc(s_const, 1)
            pool.wait_ge(s_const, 4)
            nc.gpsimd.affine_select(out=T.ident[:], in_=T.ident[:], compare_op=ALU.not_equal, fill=1.0, base=0,
                                    pattern=[[-1, P]], channel_multiplier=1).then_inc(s_const, 1)
            nc.gpsimd.affine_select(out=T.earlier[:], in_=T.earlier[:], compare_op=ALU.is_ge, fill=0.0, base=0,
                                    pattern=[[-1, P]], channel_multiplier=1).then_inc(s_const, 1)
            nc.gpsimd.memset(first[0:1, :], 1.0).then_inc(s_const, 1)
            nc.gpsimd.iota(T.iota_row[:], [[1, P]], base=0, channel_multiplier=0,
                           allow_small_or_imprecise_dtypes=True).then_inc(s_const, 1)
            nc.gpsimd.iota(T.iota_col[:], [[1, 1]], base=0, channel_multiplier=1,
                           allow_small_or_imprecise_dtypes=True).then_inc(s_const, 1)
            nc.gpsimd.iota(T.iota_hi[:], [[1, NT], [0, HEADS]], base=0, channel_multiplier=0,
                           allow_small_or_imprecise_dtypes=True).then_inc(s_const, 1)
            nc.gpsimd.iota(T.trash[:], [[1, 1]], base=TRASH, channel_multiplier=1,
                           allow_small_or_imprecise_dtypes=True).then_inc(s_const, 1)

        @block.scalar
        def _(act):
            act.wait_ge(s_turn, 4)
            nc.scalar.activation(T.cut[:], turn_r[:], ACT.Sin, bias=half_pi[:], scale=-TWO_PI).then_inc(s_sin, 1)

        @block.tensor
        def _(pe):
            pe.wait_ge(s_const, 11)
            pe.wait_ge(s_f, 1)
            nc.tensor.matmul(ps_base[:], first[:], T.dst_f[:].rearrange("p (g u) -> p g u", u=G)[:, :, 0],
                             start=True, stop=True).then_inc(s_base, 1)
            pe.wait_ge(s_far, 2)
            nc.tensor.matmul(ps_far[:], ones[:], count[:], start=True, stop=True).then_inc(s_flag, 1)

        @block.vector
        def _(dve):
            nc.vector.memset(half_pi[:], np.pi / 2)
            nc.vector.memset(T.zeros[:], 0.0)
            nc.vector.memset(T.deg[:], 0.0)
            nc.vector.memset(T.ones_row[:], 1.0)
            dve.wait_ge(s_in, 80)
            nc.vector.tensor_copy(T.dst_f[:], dst_i[:]).then_inc(s_f, 1)
            nc.vector.tensor_copy(T.src_f[:], src_i[:])
            nc.vector.tensor_scalar(hi_i[:], src_i[:], 7, None, ALU.logical_shift_right)
            nc.vector.tensor_scalar(lo_i[:], row_i[:, 0, :], P - 1, None, ALU.bitwise_and).then_inc(s_bits, 1)
            nc.vector.tensor_copy(row_f[:, 0, :], row_i[:, 0, :]).then_inc(s_rowf, 1)
            nc.vector.tensor_copy(row_f[:, 1, :], row_i[:, 1, :]).then_inc(s_rowf, 1)
            nc.vector.tensor_scalar(turn[:], ew[:], 0.1, None, ALU.mult).then_inc(s_turn, 1)
            dve.wait_ge(s_bits, 1)
            nc.vector.tensor_copy(T.hi_f[:], hi_i[:])
            nc.vector.tensor_copy(row_f[:, 2, :], lo_i[:]).then_inc(s_rowf, 1)
            dve.wait_ge(s_turn, 1)
            nc.vector.tensor_scalar(turn_r[:], turn[:], ROUND, ROUND, ALU.add, ALU.subtract).then_inc(s_turn, 1)
            dve.wait_ge(s_turn, 2)
            nc.vector.tensor_tensor(turn[:], turn[:], turn_r[:], ALU.subtract).then_inc(s_turn, 1)
            dve.wait_ge(s_turn, 3)
            nc.vector.scalar_tensor_tensor(turn_r[:], turn[:], -1.0, turn[:], ALU.mult, ALU.max).then_inc(s_turn, 1)
            nc.vector.tensor_scalar(inside[:], ew[:], 5.0, 0.5, ALU.is_lt, ALU.mult).then_inc(s_turn, 1)
            dve.wait_ge(s_base, 1)
            dve.wait_ge(s_const, 11)
            nc.vector.tensor_scalar(T.window[:], ps_base[:], T.iota_col[:], None, ALU.add).then_inc(s_win, 1)
            nc.vector.tensor_copy(T.base[:], ps_base[0:1, :]).then_inc(s_win, 1)
            dst_g = T.dst_f[:].rearrange("p (g u) -> p g u", u=G)
            nc.vector.tensor_tensor(T.off_f[:].rearrange("p (g u) -> p g u", u=G), dst_g,
                                    ps_base[:, :, None].to_broadcast([P, NG, G]), ALU.subtract).then_inc(s_off, 1)
            dve.wait_ge(s_off, 1)
            nc.vector.tensor_scalar(beyond[:, 0, :], T.off_f[:], 0.0, None, ALU.is_lt).then_inc(s_beyond, 1)
            nc.vector.tensor_scalar(beyond[:, 1, :], T.off_f[:], float(P - 1), None, ALU.is_gt).then_inc(s_beyond, 1)
            dve.wait_ge(s_beyond, 2)
            for k in range(2):
                nc.vector.reduce_sum(count[:, k:k + 1], beyond[:, k, :], axis=AX.X).then_inc(s_far, 1)
            dve.wait_ge(s_sin, 1)
            dve.wait_ge(s_turn, 5)
            nc.vector.scalar_tensor_tensor(T.cut[:], T.cut[:], 1.0, inside[:], ALU.add, ALU.mult).then_inc(s_turn, 1)
            dve.wait_ge(s_flag, 1)
            nc.vector.reduce_sum(count[0:1, 0:1], ps_far[0:1, :], axis=AX.X).then_inc(s_flag, 1)
            dve.wait_ge(s_flag, 2)
            nc.vector.tensor_copy(T.far[:], count[0:1, 0:1])


def edge_indices_far(nc, A, T):
    with Phase(nc, "fx") as ph:
        dst_i = ph.sb("dst_i", [P, ET], I32)
        hi_i = ph.sb("hi_i", [P, ET], I32)
        lo_i = ph.sb("lo_i", [P, ET], I32)
        hi_f = ph.sb("hi_f", [P, ET])
        lo_f = ph.sb("lo_f", [P, ET])
        again = [ph.sb("again_s", [P, ET]), ph.sb("again_d", [P, ET])]
        room = [ph.sb("room_s", [P, ET]), ph.sb("room_d", [P, ET])]
        uniq = [ph.sb("uniq_s", [P, ET], I32), ph.sb("uniq_d", [P, ET], I32)]
        rows = [ph.sb("rows_s", [P, G, P]), ph.sb("rows_d", [P, G, P])]
        cols = ph.sb("cols", [P, 4, G])
        same = ph.sb("same", [P, 2, G, P], BF16)
        count = ph.sb("count", [P, 2, G])
        hot_lo = ph.sb("hot_lo", [P, G, P], BF16)
        hot_hi = ph.sb("hot_hi", [P, G, NT], BF16)
        none = ph.sb("none", [P, P], BF16)
        ps_deg = ph.ps("ps_deg", [P, NT])
        (s_in, s_split, s_rows, s_read, s_cols, s_same, s_count, s_hot, s_deg, s_uniq, s_out) = (
            ph.sem(n) for n in ("in", "split", "rows", "read", "cols", "same", "count", "hot", "deg", "uniq", "out"))
        block = ph.block()

        @block.sync
        def _(sp):
            def far():
                sp.dma_start(dst_i[:], A["dst_cols"]).then_inc(s_in, 16)
                with sp.Fori(0, NG) as g:
                    sp.wait_ge(s_read, g + 1)
                    for k, tab in enumerate((T.src_rows, T.dst_rows)):
                        sp.dma_start(rows[k][:].rearrange("p u f -> p (u f)"),
                                     bcast_rows(tab[ds(g * G * P, G * P)], P)).then_inc(s_rows, 16)
                sp.wait_ge(s_uniq, 6)
                sp.dma_start(T.srcu_cols, uniq[0][:]).then_inc(s_out, 16)
                sp.dma_start(T.dstu_cols, uniq[1][:]).then_inc(s_out, 16)
                sp.wait_ge(s_out, 32)
                sp.sem_inc(s_in, 1)
            if_far(sp, T, far)

        @block.tensor
        def _(pe):
            def far():
                pe.wait_ge(s_split, 1)
                nc.tensor.matmul(ps_deg[:], none[:], none[:, 0:NT], start=True, stop=False,
                                 skip_group_check=True).then_inc(s_deg, 1)
                with pe.Fori(0, NG) as g:
                    for u in range(G):
                        pe.wait_ge(s_hot, g * G + u + 1)
                        nc.tensor.matmul(ps_deg[:], hot_lo[:, u, :], hot_hi[:, u, :], start=False, stop=False,
                                         skip_group_check=True).then_inc(s_deg, 1)
            if_far(pe, T, far)

        @block.vector
        def _(dve):
            def far():
                nc.vector.memset(none[:], 0.0).then_inc(s_split, 1)
                dve.wait_ge(s_in, 16)
                nc.vector.tensor_scalar(hi_i[:], dst_i[:], 7, None, ALU.logical_shift_right)
                nc.vector.tensor_scalar(lo_i[:], dst_i[:], P - 1, None, ALU.bitwise_and).then_inc(s_split, 1)
                dve.wait_ge(s_split, 2)
                nc.vector.tensor_copy(hi_f[:], hi_i[:])
                nc.vector.tensor_copy(lo_f[:], lo_i[:]).then_inc(s_split, 1)
                dve.wait_ge(s_split, 3)
                dve.sem_inc(s_read, 1)
                with dve.Fori(0, NG) as g:
                    for k, col in enumerate((T.src_f, T.dst_f, lo_f, hi_f)):
                        nc.vector.tensor_copy(cols[:, k, :], col[:, ds(g * G, G)]).then_inc(s_cols, 1)
                    dve.wait_ge(s_rows, (g + 1) * 32)
                    dve.wait_ge(s_cols, (g + 1) * 4)
                    for k in range(2):
                        for u in range(G):
                            nc.vector.scalar_tensor_tensor(same[:, k, u, :], rows[k][:, u, :], cols[:, k, u:u + 1],
                                                           T.earlier[:], ALU.is_equal, ALU.mult,
                                                           accum_out=count[:, k, u:u + 1]).then_inc(s_same, 1)
                    dve.wait_ge(s_same, (g + 1) * 2 * G)
                    for k in range(2):
                        nc.vector.tensor_scalar(again[k][:, ds(g * G, G)], count[:, k, :], 2.0, -1.0,
                                                ALU.min, ALU.add).then_inc(s_count, 1)
                    dve.sem_inc(s_read, 1)
                    dve.wait_ge(s_deg, g * G + 1)
                    for u in range(G):
                        nc.vector.tensor_scalar(hot_lo[:, u, :], T.iota_row[:], cols[:, 2, u:u + 1], None,
                                                ALU.is_equal)
                        nc.vector.tensor_scalar(hot_hi[:, u, :], T.iota_row[:, 0:NT], cols[:, 3, u:u + 1], None,
                                                ALU.is_equal).then_inc(s_hot, 1)
                    dve.wait_ge(s_hot, (g + 1) * G)
                    dve.wait_ge(s_count, (g + 1) * 2)
                    dve.sem_inc(s_in, 1)
                for k, col in enumerate((T.src_f, T.dst_f)):
                    nc.vector.tensor_scalar(room[k][:], col[:], T.trash[:], -1.0, ALU.subtract,
                                            ALU.mult).then_inc(s_uniq, 1)
                dve.wait_ge(s_uniq, 2)
                for k in range(2):
                    nc.vector.tensor_tensor(room[k][:], room[k][:], again[k][:], ALU.mult).then_inc(s_uniq, 1)
                dve.wait_ge(s_uniq, 4)
                for k, col in enumerate((T.src_f, T.dst_f)):
                    nc.vector.tensor_tensor(uniq[k][:], room[k][:], col[:], ALU.add).then_inc(s_uniq, 1)
                dve.wait_ge(s_deg, ET + 1)
                nc.vector.tensor_copy(T.deg[:], ps_deg[:])
            if_far(dve, T, far)


def node_qkv(nc, A, ident, ones_row, tiles, q_tab, qs_tab, kv_tab):
    with Phase(nc, "qkv") as ph:
        w = ph.sb("w", [P, 2, 3 * H])
        bias = ph.sb("bias", [1, 3 * H])
        gb = ph.sb("gb", [P, 2, 2])
        x = ph.sb("x", [P, 2, NB, H])
        xhat = ph.sb("xhat", [P, NB, H])
        xT = ph.sb("xT", [P, 2, 2, P])
        y = ph.sb("y", [P, NB, 3 * H])
        ys = ph.sb("ys", [P, NB, 2, H], F32R)
        stats = ph.sb("stats", [P, NB, 6])
        mv = ph.sb("mv", [P, NB, 2])
        rstd = ph.sb("rstd", [P, 3, NB])
        ps_t = ph.ps("ps_t", [P, 2, 4, P])
        ps_y = ph.ps("ps_y", [P, 2, 1024])
        s_w = ph.sem("w")
        s_x = ph.sems("x", 2)
        s_xfree = ph.sem("xfree")
        s_stats, s_var, s_sqrt, s_rinv, s_norm = (ph.sem(n) for n in ("stats", "var", "sqrt", "rinv", "norm"))
        s_t = ph.sem("t")
        s_xT = ph.sem("xT")
        s_y = ph.sem("y")
        s_ys = ph.sem("ys")
        s_st = ph.sem("st")
        s_yfree = ph.sem("yfree")
        s_go = ph.sem("go")
        s_hi, s_lo = ph.sem("hi"), ph.sem("lo")
        block = ph.block()
        xt = tiles(A["x"])
        IT = NT // (2 * NB)

        @block.sync
        def _(sp):
            sp.dma_start(w[:, :, 0:H], A["WqT"].rearrange("(c p) n -> p c n", p=P)).then_inc(s_w, 16)
            sp.dma_start(w[:, :, H:2 * H], A["WkT"].rearrange("(c p) n -> p c n", p=P)).then_inc(s_w, 16)
            sp.dma_start(w[:, :, 2 * H:], A["WvT"].rearrange("(c p) n -> p c n", p=P)).then_inc(s_w, 16)
            for k, b in enumerate(("bq", "bk", "bv")):
                sp.dma_start(bias[0:1, k * H:(k + 1) * H], A[b].rearrange("(a n) -> a n", a=1)).then_inc(s_w, 16)
            sp.dma_start(gb[:, 0, :], A["ln_g"].rearrange("(c p) -> p c", p=P)).then_inc(s_w, 16)
            sp.dma_start(gb[:, 1, :], A["ln_b"].rearrange("(c p) -> p c", p=P)).then_inc(s_w, 16)
            with sp.Fori(0, IT) as b:
                for h in range(2):
                    it = b * 2 + h
                    sp.wait_ge(s_xfree, it + 1)
                    sp.dma_start(x[:, h, :, :], xt[:, ds(it * NB, NB), :]).then_inc(s_x[h], 16)

        @block.vector
        def _(dve):
            dve.sem_inc(s_xfree, 2)
            with dve.Fori(0, IT) as b:
                for h in range(2):
                    it = b * 2 + h
                    dve.wait_ge(s_x[h], (b + 1) * 16)
                    dve.wait_ge(s_t, it * 2 * NB + 1)
                    layernorm_batch(nc, dve, x[:, h], xhat, stats, mv, rstd,
                                    s_stats, s_var, s_sqrt, s_rinv, s_norm, s_go, it)
                    dve.wait_ge(s_norm, (it + 1) * NB)
                    dve.sem_inc(s_xfree, 1)
                    for u in range(NB):
                        dve.wait_ge(s_ys, it * NB + u + 3)
                        nc.vector.tensor_tensor(ys[:, u, 1, :], y[:, u, 0:H], ys[:, u, 0, :],
                                                ALU.subtract).then_inc(s_lo, 1)

        @block.tensor
        def _(pe):
            pe.sem_inc(s_t, 1)
            pe.wait_ge(s_w, 16 * 8)
            with pe.Fori(0, IT) as b:
                for h in range(2):
                    it = b * 2 + h
                    for u in range(NB):
                        n = it * NB + u
                        v = (h * NB + u) % 2
                        pe.wait_ge(s_norm, n + 1)
                        pe.wait_ge(s_xT, n * 2 + 1)
                        for c in range(2):
                            nc.tensor.transpose(ps_t[:, v, c, :], xhat[:, u, c * P:(c + 1) * P],
                                                ident[:]).then_inc(s_t, 1)
                        pe.wait_ge(s_xT, n * 2 + 3)
                        pe.wait_ge(s_ys, n + 1)
                        for a, z in ((0, 512), (512, 768)):
                            o = ps_y[:, v, a:z]
                            nc.tensor.matmul(o, xT[:, v, 0, :], w[:, 0, a:z], start=True, stop=False)
                            nc.tensor.matmul(o, xT[:, v, 1, :], w[:, 1, a:z], start=False, stop=False)
                            nc.tensor.matmul(o, ones_row[:], bias[0:1, a:z], start=False,
                                             stop=True).then_inc(s_y, 1)

        @block.scalar
        def _(act):
            act.sem_inc(s_xT, 1)
            act.sem_inc(s_ys, 2)
            act.wait_ge(s_w, 16 * 8)
            with act.Fori(0, IT) as b:
                for h in range(2):
                    it = b * 2 + h
                    layernorm_root(nc, act, rstd, s_var, s_sqrt, it)
                    act.wait_ge(s_yfree, it + 1)
                    for u in range(NB):
                        n = it * NB + u
                        v = (h * NB + u) % 2
                        act.wait_ge(s_t, n * 2 + 3)
                        for c in range(2):
                            nc.scalar.activation(xT[:, v, c, :], ps_t[:, v, c, :], ACT.Identity,
                                                 bias=gb[:, 1, c:c + 1], scale=gb[:, 0, c:c + 1]).then_inc(s_xT, 1)
                        act.wait_ge(s_y, n * 2 + 2)
                        nc.scalar.activation(ys[:, u, 0, :], ps_y[:, v, 0:H], ACT.Copy).then_inc(s_hi, 1)
                        nc.scalar.activation(y[:, u, :], ps_y[:, v, 0:3 * H], ACT.Copy).then_inc(s_ys, 1)

        @block.gpsimd
        def _(pool):
            pool.sem_inc(s_yfree, 1)
            with pool.Fori(0, NT // NB) as it:
                pool.wait_ge(s_ys, (it + 1) * NB + 2)
                pool.sem_inc(s_go, 1)
                pool.dma_start(tiles(q_tab)[:, ds(it * NB, NB), :], y[:, :, 0:H]).then_inc(s_st, 16)
                pool.dma_start(tiles(kv_tab)[:, ds(it * NB, NB), :], y[:, :, H:3 * H]).then_inc(s_st, 16)
                pool.wait_ge(s_lo, (it + 1) * NB)
                pool.sem_inc(s_go, 1)
                pool.dma_start(tiles(qs_tab)[:, ds(it * NB, NB), :],
                               ys[:].rearrange("p n a d -> p n (a d)").bitcast(F32)).then_inc(s_st, 16)
                pool.wait_ge(s_st, (it + 1) * 48)
                pool.sem_inc(s_yfree, 1)


def zero_accumulators(pool, accs, zeros, s_add):
    for acc, s in zip(accs, s_add):
        flat = acc.rearrange("(p t) d -> p t d", p=P)
        d = flat.shape[2]
        pool.dma_start(flat, zeros[:, None, 0:d].to_broadcast([P, NT, d])).then_inc(s, 16)


class Near:

    def __init__(self, ph, slots=2, gathers=True):
        self.ge = [ph.sems(f"near{h}_", G) for h in range(slots)] if gathers else None


def edge_layer0(nc, A, T):
    with Phase(nc, "e0") as ph:
        w = ph.sb("w", [R64 + 1, 2 * H])
        ea = ph.sb("ea", [R64 + 1, 2, G * P])
        rows = ph.sb("rows", [P, 2, G, P])
        isrc = ph.sb("isrc", [P, 2, G], I32)
        idst = ph.sb("idst", [P, 2, G], I32)
        iout = ph.sb("iout", [P, 2, G], I32)
        kv = ph.sb("kv", [P, G, 2 * H])
        q = ph.sb("q", [P, G, H])
        qk = ph.sb("qk", [P, 2, H])
        junk = ph.sb("junk", [P, G, H], BF16)
        vd = ph.sb("vd", [P, G, H])
        raw = ph.sb("raw", [P, G])
        att = ph.sb("att", [P, 2, G])
        cols = ph.sb("cols", [P, 2, G])
        same = ph.sb("same", [P, G, P])
        msg = ph.sb("msg", [P, 2, H + 1])
        ps_d = ph.ps("ps_d", [P, 2, 512])
        ps_m = ph.ps("ps_m", [P, 2, 512])
        s_w, s_one = ph.sem("w"), ph.sem("one")
        s_ld = ph.sems("ld", 2)
        s_ldfree = ph.sem("ldfree")
        s_ge = ph.sems("ge", G)
        s_gfree = ph.sem("gfree")
        s_go = ph.sem("go")
        s_dl, s_si, s_cols, s_qk, s_raw, s_vd = (ph.sem(n) for n in ("dl", "si", "cols", "qk", "raw", "vd"))
        s_rs, s_att, s_same, s_sum, s_msg = (ph.sem(n) for n in ("rs", "att", "same", "sum", "msg"))
        s_add = ph.sem("add")


        def far_sp(sp):
            with sp.Fori(0, NG // 2) as b:
                for h in range(2):
                    g = b * 2 + h
                    sp.wait_ge(s_ldfree, g + 1)
                    sp.dma_start(ea[0:R64, h, :], A["ea64T"][:, ds(g * G * P, G * P)]).then_inc(s_ld[h], 16)
                    sp.dma_start(rows[:, h].rearrange("p u f -> p (u f)"),
                                 bcast_rows(T.dst_rows[ds(g * G * P, G * P)], P)).then_inc(s_ld[h], 16)
                    sp.dma_start(isrc[:, h, :], A["src_cols"][:, ds(g * G, G)]).then_inc(s_ld[h], 16)
                    sp.dma_start(idst[:, h, :], A["dst_cols"][:, ds(g * G, G)]).then_inc(s_ld[h], 16)
                    sp.dma_start(iout[:, h, :], T.dstu_cols[:, ds(g * G, G)]).then_inc(s_ld[h], 16)

        def far_pool(pool):
            pool.sem_inc(s_ldfree, 2)
            zero_accumulators(pool, [T.acc0], T.zeros, [s_add])
            with pool.Fori(0, NG // 2) as b:
                for h in range(2):
                    g = b * 2 + h
                    pool.wait_ge(s_ld[h], (b + 1) * 80)
                    for u in range(G):
                        pool.wait_ge(s_gfree, g * G + u + 1)
                        pool.sem_inc(s_go, 1)
                        pool.indirect_dma_start(kv[:, u, :], None, T.kv_tab,
                                                bass.IndirectOffsetOnAxis(isrc[:, h, u:u + 1], 0)).then_inc(s_ge[u], 16)
                        pool.indirect_dma_start(q[:, u, :], None, T.q_tab,
                                                bass.IndirectOffsetOnAxis(idst[:, h, u:u + 1], 0)).then_inc(s_ge[u], 16)
                    for u in range(G):
                        pool.wait_ge(s_msg, g * G + u + 3)
                        pool.wait_ge(s_add, (g * G + u + 1) * 16)
                        pool.sem_inc(s_go, 1)
                        pool.indirect_dma_start(T.acc0, bass.IndirectOffsetOnAxis(iout[:, h, u:u + 1], 0),
                                                msg[:, u % 2, :], None, compute_op=ALU.add).then_inc(s_add, 16)
                    pool.wait_ge(s_add, (g * G + G + 1) * 16)
                    pool.sem_inc(s_ldfree, 1)

        def far_pe(pe):
            with pe.Fori(0, NG // 2) as b:
                for h in range(2):
                    g = b * 2 + h
                    pe.wait_ge(s_ld[h], (b + 1) * 80)
                    for u in range(G):
                        pe.wait_ge(s_vd, g * G + u + 1)
                        nc.tensor.matmul(ps_d[:, u % 2, :], ea[:, h, u * P:(u + 1) * P], w[:], start=True,
                                         stop=True).then_inc(s_dl, 1)
                    for u in range(G):
                        pe.wait_ge(s_same, g * G + u + 1)
                        pe.wait_ge(s_msg, g * G + u + 1)
                        nc.tensor.matmul(ps_m[:, u % 2, 0:H], same[:, u, :], vd[:, u, :], start=True,
                                         stop=True).then_inc(s_sum, 1)

        def far_act(act):
            nc.scalar.activation(msg[:, :, H:H + 1], T.zeros[:, None, 0:1].to_broadcast([P, 2, 1]), ACT.Copy)
            act.sem_inc(s_msg, 2)
            with act.Fori(0, NG) as g:
                for u in range(G):
                    act.wait_ge(s_dl, g * G + u + 1)
                    nc.scalar.activation(ps_d[:, u % 2, :], ps_d[:, u % 2, :], ACT.Silu).then_inc(s_si, 1)
                act.wait_ge(s_raw, (g + 1) * G)
                nc.scalar.activation(att[:, 0, :], raw[:], ACT.Silu).then_inc(s_rs, 1)
                for u in range(G):
                    act.wait_ge(s_sum, g * G + u + 1)
                    act.wait_ge(s_add, g * G * 16 + max(u, 1) * 16)
                    nc.scalar.activation(msg[:, u % 2, 0:H], ps_m[:, u % 2, 0:H], ACT.Copy).then_inc(s_msg, 1)

        def far_dve(dve):
            dve.sem_inc(s_gfree, G)
            dve.sem_inc(s_vd, 2)
            with dve.Fori(0, NG // 2) as b:
                for h in range(2):
                    g = b * 2 + h
                    nc.vector.tensor_copy(cols[:, 0, :], T.dst_f[:, ds(g * G, G)]).then_inc(s_cols, 1)
                    nc.vector.tensor_copy(cols[:, 1, :], T.cut[:, ds(g * G, G)]).then_inc(s_cols, 1)
                    for u in range(G):
                        n = g * G + u
                        dve.wait_ge(s_ge[u], (g + 1) * 32)
                        nc.vector.tensor_tensor(qk[:, u % 2, :], q[:, u, :], kv[:, u, 0:H], ALU.mult).then_inc(s_qk, 1)
                        dve.wait_ge(s_si, n + 1)
                        nc.vector.tensor_tensor(vd[:, u, :], kv[:, u, H:2 * H], ps_d[:, u % 2, H:2 * H],
                                                ALU.mult).then_inc(s_gfree, 1)
                        dve.wait_ge(s_qk, n + 1)
                        nc.vector.tensor_tensor_reduce(out=junk[:, u, :], in0=qk[:, u % 2, :], in1=ps_d[:, u % 2, 0:H],
                                                       scale=1.0, scalar=0.0, op0=ALU.mult, op1=ALU.add,
                                                       accum_out=raw[:, u:u + 1]).then_inc(s_raw, 1)
                        dve.wait_ge(s_raw, n + 1)
                        dve.sem_inc(s_vd, 1)
                    dve.wait_ge(s_rs, g + 1)
                    dve.wait_ge(s_cols, (g + 1) * 2)
                    nc.vector.tensor_tensor(att[:, 1, :], att[:, 0, :], cols[:, 1, :], ALU.mult).then_inc(s_att, 1)
                    dve.wait_ge(s_att, g + 1)
                    for u in range(G):
                        nc.vector.tensor_scalar(same[:, u, :], rows[:, h, u, :], cols[:, 0, u:u + 1],
                                                att[:, 1, u:u + 1], ALU.is_equal, ALU.mult).then_inc(s_same, 1)
                    dve.wait_ge(s_sum, (g + 1) * G)

        nw = Near(ph)
        hotT = ph.sb("hotT", [P, 2, G * P], F32R)
        win = ph.sb("win", [P, 2, 2 * H], F32R)
        kv2 = ph.sb("kv2", [P, 2, G, 2 * H])
        qk2 = ph.sb("qk2", [P, 2, 2, H])
        vd2 = ph.sb("vd2", [P, 2, G, H])
        att2 = ph.sb("att2", [P, 2, 3, G])
        hot = ph.sb("hot", [P, 2, G, P])
        count = ph.sb("count", [P, 2])
        cut2 = ph.sb("cut2", [P, 2, G])
        off2 = ph.sb("off2", [P, 2, G])
        agg = ph.sb("agg", [P, 2, H + 1])
        ps_q = ph.ps("ps_q", [P, 2, 2, H])
        ps_k = ph.ps("ps_k", [P, 2, 2, H])
        ps_a = ps_m
        banks = [ps_d[:, 0, :], ps_d[:, 1, :], ps_k[:, 0].rearrange("p a d -> p (a d)"),
                 ps_k[:, 1].rearrange("p a d -> p (a d)")]
        dkv = [ps_d[:].rearrange("p t (a d) -> p t a d", a=2), ps_k[:]]
        s_hotT, s_q, s_pair, s_hotA, s_red, s_agg, s_vp = (
            ph.sem(n) for n in ("hotT", "q", "pair", "hotA", "red", "agg", "vp"))
        LAST = NG // 2 - 1

        def near_sp(sp):
            with sp.Fori(0, NG // 2) as b:
                for h in range(2):
                    g = b * 2 + h
                    first = sp.value_load(T.base[0:1, ds(g, 1)], min_val=0, max_val=NP - P)
                    sp.wait_ge(s_gfree, g + 1)
                    sp.dma_start(ea[0:R64, h, :], A["ea64T"][:, ds(g * G * P, G * P)]).then_inc(s_ld[h], 16)
                    sp.dma_start(rows[:, h].rearrange("p u f -> p (u f)"),
                                 bcast_rows(T.dst_rows[ds(g * G * P, G * P)], P)).then_inc(s_ld[h], 16)
                    sp.dma_start(isrc[:, h, :], A["src_cols"][:, ds(g * G, G)]).then_inc(s_ld[h], 16)
                    sp.dma_start(win[:, h, :].bitcast(F32), T.qs_tab[ds(first, P), :]).then_inc(s_ld[h], 16)

        def near_pool(pool):
            zero_accumulators(pool, [T.acc0], T.zeros, [s_add])

            def gathers(g, b, h):
                pool.wait_ge(s_ld[h], (b + 1) * 64)
                pool.wait_ge(s_gfree, g + 1)
                pool.sem_inc(s_go, 1)
                for u in range(G):
                    pool.indirect_dma_start(kv2[:, h, u, :], None, T.kv_tab,
                                            bass.IndirectOffsetOnAxis(isrc[:, h, u:u + 1], 0)).then_inc(nw.ge[h][u], 16)

            def add(g, h):
                first = pool.value_load(T.base[0:1, ds(g, 1)], min_val=0, max_val=NP - P)
                pool.wait_ge(s_agg, g + 3)
                pool.wait_ge(s_add, (g + 1) * 16)
                pool.sem_inc(s_go, 1)
                pool.dma_start(T.acc0[ds(first, P), :], agg[:, h, :], accum_op=ALU.add).then_inc(s_add, 16)

            gathers(0, 0, 0)
            gathers(1, 0, 1)
            with pool.Fori(0, LAST) as b:
                gathers(b * 2 + 2, b + 1, 0)
                add(b * 2, 0)
                gathers(b * 2 + 3, b + 1, 1)
                add(b * 2 + 1, 1)
            add(NG - 2, 0)
            add(NG - 1, 1)
            pool.wait_ge(s_add, (NG + 1) * 16)

        def near_pe(pe):
            def pair(g, b, h, i):
                if i == 0:
                    pe.wait_ge(s_ld[h], (b + 1) * 64)
                n = g * 4 + i
                pe.wait_ge(s_vp, n + 1)
                for v in range(2):
                    u = 2 * i + v
                    nc.tensor.matmul(banks[u % 4], ea[:, h, u * P:(u + 1) * P], w[:], start=True,
                                     stop=True).then_inc(s_dl, 1)
                pe.wait_ge(s_pair, n + 1)
                if i == 0:
                    pe.wait_ge(s_hotT, g + 1)
                for v in range(2):
                    e = hotT[:, h, (2 * i + v) * P:(2 * i + v + 1) * P]
                    nc.tensor.matmul(ps_q[:, i % 2, v, :], e, win[:, h, 0:H], start=True, stop=False)
                    nc.tensor.matmul(ps_q[:, i % 2, v, :], e, win[:, h, H:2 * H], start=False,
                                     stop=True).then_inc(s_q, 1)

            def reduce(g, h, us):
                for u in us:
                    pe.wait_ge(s_hotA, g * G + u + 1)
                    nc.tensor.matmul(ps_a[:, h, 0:H], hot[:, h, u, :], vd2[:, h, u, :], start=(u == 0),
                                     stop=(u == G - 1)).then_inc(s_red, 1)

            def group(g, b, h, start=False):
                pair(g, b, h, 0)
                pair(g, b, h, 1)
                if not start:
                    reduce(g - 1, 1 - h, range(0, G // 2))
                pair(g, b, h, 2)
                if not start:
                    reduce(g - 1, 1 - h, range(G // 2, G))
                pair(g, b, h, 3)

            group(0, 0, 0, start=True)
            group(1, 0, 1)
            with pe.Fori(1, NG // 2) as b:
                group(b * 2, b, 0)
                group(b * 2 + 1, b, 1)
            reduce(NG - 1, 1, range(G))

        def near_act(act):
            act.sem_inc(s_agg, 2)

            def filt(g, i):
                act.wait_ge(s_dl, g * G + 2 * i + 2)
                o = dkv[i % 2].rearrange("p t a d -> p (t a d)")
                nc.scalar.activation(o, o, ACT.Silu).then_inc(s_si, 1)

            def sums(g, h):
                act.wait_ge(s_red, (g + 1) * G)
                act.wait_ge(s_add, (g + 1) * 16)
                act.sem_inc(s_go, 1)
                nc.scalar.activation(agg[:, h, H:H + 1], count[:, h:h + 1], ACT.Copy)
                nc.scalar.activation(agg[:, h, 0:H], ps_a[:, h, 0:H], ACT.Copy).then_inc(s_agg, 1)

            def group(g, h, start=False):
                filt(g, 0)
                filt(g, 1)
                filt(g, 2)
                if not start:
                    sums(g - 1, 1 - h)
                filt(g, 3)
                act.wait_ge(s_raw, (g + 1) * G)
                nc.scalar.activation(att2[:, h, 1, :], att2[:, h, 0, :], ACT.Silu).then_inc(s_rs, 1)

            group(0, 0, start=True)
            group(1, 1)
            with act.Fori(1, NG // 2) as b:
                group(b * 2, 0)
                group(b * 2 + 1, 1)
            sums(NG - 1, 1)

        def near_dve(dve):
            dve.sem_inc(s_gfree, 2)
            dve.sem_inc(s_pair, 2)
            dve.sem_inc(s_vp, 2)

            def onehots(g, b, h):
                dve.wait_ge(s_ld[h], (b + 1) * 64)
                dve.wait_ge(s_agg, g + 1)
                dve.sem_inc(s_go, 1)
                nc.vector.tensor_copy(cut2[:, h, :], T.cut[:, ds(g * G, G)]).then_inc(s_cols, 1)
                nc.vector.tensor_copy(off2[:, h, :], T.off_f[:, ds(g * G, G)]).then_inc(s_cols, 1)
                nc.vector.tensor_scalar(hotT[:, h, :], rows[:, h].rearrange("p u f -> p (u f)"),
                                        T.window[:, ds(g, 1)], None, ALU.is_equal, ALU.add,
                                        accum_out=count[:, h:h + 1]).then_inc(s_hotT, 1)

            def attention(g, b, h, pairs):
                for i in pairs:
                    n = g * 4 + i
                    u = 2 * i
                    for v in range(2):
                        dve.wait_ge(nw.ge[h][u + v], (b + 1) * 16)
                    dve.wait_ge(s_q, g * G + u + 2)
                    nc.vector.tensor_tensor(qk2[:, i % 2], ps_q[:, i % 2], kv2[:, h, u:u + 2, 0:H],
                                            ALU.mult).then_inc(s_pair, 1)
                    dve.wait_ge(s_si, n + 1)
                    nc.vector.tensor_tensor(vd2[:, h, u:u + 2, :], dkv[i % 2][:, :, 1, :], kv2[:, h, u:u + 2, H:2 * H],
                                            ALU.mult).then_inc(s_vd, 1)
                    dve.wait_ge(s_pair, n + 3)
                    for v in range(2):
                        nc.vector.tensor_tensor_reduce(out=junk[:, u + v, :], in0=qk2[:, i % 2, v, :],
                                                       in1=dkv[i % 2][:, v, 0, :], scale=1.0, scalar=0.0,
                                                       op0=ALU.mult, op1=ALU.add,
                                                       accum_out=att2[:, h, 0, u + v:u + v + 1]).then_inc(s_raw, 1)
                    dve.wait_ge(s_raw, g * G + u + 2)
                    dve.sem_inc(s_vp, 1)
                if i == 3:
                    dve.wait_ge(s_vd, g * 4 + 4)
                    dve.sem_inc(s_gfree, 1)

            def weigh(g, h):
                dve.wait_ge(s_rs, g + 1)
                dve.wait_ge(s_cols, (g + 1) * 2)
                nc.vector.tensor_tensor(att2[:, h, 2, :], att2[:, h, 1, :], cut2[:, h, :], ALU.mult).then_inc(s_att, 1)
                dve.wait_ge(s_att, g + 1)
                for u in range(G):
                    nc.vector.tensor_scalar(hot[:, h, u, :], T.iota_row[:], off2[:, h, u:u + 1],
                                            att2[:, h, 2, u:u + 1], ALU.is_equal, ALU.mult).then_inc(s_hotA, 1)

            def group(g, b, h, last=False):
                attention(g, b, h, range(3))
                if not last:
                    onehots(g + 1, b + h, 1 - h)
                attention(g, b, h, (3,))
                weigh(g, h)

            onehots(0, 0, 0)
            with dve.Fori(0, LAST) as b:
                group(b * 2, b, 0)
                group(b * 2 + 1, b, 1)
            group(NG - 2, LAST, 0)
            group(NG - 1, LAST, 1, last=True)

        block = ph.block()

        @block.sync
        def _(sp):
            sp.dma_start(w[0:R64, 0:H], A["WdkT"]).then_inc(s_w, 16)
            sp.dma_start(w[0:R64, H:2 * H], A["WdvT"]).then_inc(s_w, 16)
            sp.dma_start(w[R64:R64 + 1, 0:H], A["bdk"].rearrange("(a n) -> a n", a=1)).then_inc(s_w, 16)
            sp.dma_start(w[R64:R64 + 1, H:2 * H], A["bdv"].rearrange("(a n) -> a n", a=1)).then_inc(s_w, 16)
            if_near(sp, T, lambda: near_sp(sp), lambda: far_sp(sp))

        @block.gpsimd
        def _(pool):
            nc.gpsimd.memset(ea[R64:R64 + 1, :, :], 1.0).then_inc(s_one, 1)
            if_near(pool, T, lambda: near_pool(pool), lambda: far_pool(pool))

        @block.tensor
        def _(pe):
            pe.wait_ge(s_w, 64)
            pe.wait_ge(s_one, 1)
            if_near(pe, T, lambda: near_pe(pe), lambda: far_pe(pe))

        @block.scalar
        def _(act):
            if_near(act, T, lambda: near_act(act), lambda: far_act(act))

        @block.vector
        def _(dve):
            if_near(dve, T, lambda: near_dve(dve), lambda: far_dve(dve))


def edge_layer1(nc, A, T):
    with Phase(nc, "e1") as ph:
        w1 = ph.sb("w1", [P, H])
        b1 = ph.sb("b1", [P, 2])
        w2 = ph.sb("w2", [P, 2, H])
        b2 = ph.sb("b2", [B2R, H])
        ea = ph.sb("ea", [P, 2, G * P])
        rows = ph.sb("rows", [P, 2, G, P])
        idst = ph.sb("idst", [P, 2, G], I32)
        iout = ph.sb("iout", [P, 2, G], I32)
        hid = ph.sb("hid", [P, 2, 2, 512])
        xd = ph.sb("xd", [P, 2, G, H])
        cols = ph.sb("cols", [P, G])
        same = ph.sb("same", [P, 4, P])
        prod = ph.sb("prod", [P, 4, H])
        msg = ph.sb("msg", [P, KACC, H])
        ps_h = ph.ps("ps_h", [P, 2, 512])
        ps_f = ph.ps("ps_f", [P, 2, 512])
        ps_m = ph.ps("ps_m", [P, 2, 512])
        s_w = ph.sem("w")
        s_ld = ph.sems("ld", 2)
        s_rowfree, s_dyn = ph.sem("rowfree"), ph.sem("dyn")
        s_ge = [ph.sems(f"ge{h}_", G) for h in range(2)]
        s_gfree, s_go, s_cols, s_h, s_hid, s_f, s_prod, s_same, s_sum, s_msg = (
            ph.sem(n) for n in ("gfree", "go", "cols", "h", "hid", "f", "prod", "same", "sum", "msg"))
        s_add = ph.sems("add", KACC)


        def far_sp(sp):
            with sp.Fori(0, NG // 2) as b:
                for h in range(2):
                    g = b * 2 + h
                    sp.wait_ge(s_rowfree, g + 1)
                    sp.dma_start(ea[0:R20, h, :], A["ea20T"][0:R20, ds(g * G * P, G * P)]).then_inc(s_ld[h], 16)
                    sp.dma_start(rows[:, h].rearrange("p u f -> p (u f)"),
                                 bcast_rows(T.src_rows[ds(g * G * P, G * P)], P)).then_inc(s_ld[h], 16)
                    sp.dma_start(idst[:, h, :], A["dst_cols"][:, ds(g * G, G)]).then_inc(s_ld[h], 16)
                    sp.dma_start(iout[:, h, :], T.srcu_cols[:, ds(g * G, G)]).then_inc(s_ld[h], 16)

        def far_pool(pool):
            pool.sem_inc(s_rowfree, 2)
            zero_accumulators(pool, T.acc1, T.zeros, s_add)
            with pool.Fori(0, NG // 2) as b:
                for h in range(2):
                    g = b * 2 + h
                    pool.wait_ge(s_ld[h], (b + 1) * 64)
                    pool.wait_ge(s_gfree, g + 1)
                    pool.sem_inc(s_go, 1)
                    for u in range(G):
                        pool.indirect_dma_start(xd[:, h, u, :], None, T.x1_tab,
                                                bass.IndirectOffsetOnAxis(idst[:, h, u:u + 1], 0)).then_inc(s_ge[h][u], 16)
                    for u in range(G):
                        pool.wait_ge(s_msg, g * G + u + 3)
                        pool.wait_ge(s_add[u % KACC], (g * (G // KACC) + u // KACC + 1) * 16)
                        pool.sem_inc(s_go, 1)
                        pool.indirect_dma_start(T.acc1[u % KACC], bass.IndirectOffsetOnAxis(iout[:, h, u:u + 1], 0),
                                                msg[:, u % KACC, :], None,
                                                compute_op=ALU.add).then_inc(s_add[u % KACC], 16)
                    for k in range(KACC):
                        pool.wait_ge(s_add[k], ((g + 1) * (G // KACC) + 1) * 16)
                    pool.sem_inc(s_rowfree, 1)

        def far_pe(pe):
            pe.wait_ge(s_w, 112)
            pe.sem_inc(s_dyn, 1)
            with pe.Fori(0, NG // 2) as b:
                for h in range(2):
                    g = b * 2 + h
                    pe.wait_ge(s_ld[h], (b + 1) * 64)
                    for q in range(2):
                        m = g * 2 + q
                        for c in range(2):
                            pe.wait_ge(s_hid, m * 2 + c + 1)
                            nc.tensor.matmul(ps_h[:, c, :], w1[0:R20, c * P:(c + 1) * P],
                                             ea[0:R20, h, q * 512:(q + 1) * 512], start=True, stop=True).then_inc(s_h, 1)
                        pe.wait_ge(s_hid, m * 2 + 4)
                        for v in range(4):
                            u = q * 4 + v
                            n = g * G + u
                            pe.wait_ge(s_prod, n + 1)
                            o = ps_f[:, u % 2, 0:H]
                            nc.tensor.matmul(o, hid[:, q, 0, v * P:(v + 1) * P], w2[:, 0, :], start=True, stop=False)
                            nc.tensor.matmul(o, hid[:, q, 1, v * P:(v + 1) * P], w2[:, 1, :], start=False, stop=False)
                            nc.tensor.matmul(o, T.ones_row[:], b2[0:1, :], start=False, stop=True).then_inc(s_f, 1)
                            pe.wait_ge(s_prod, n + 3)
                            pe.wait_ge(s_same, n + 1)
                            pe.wait_ge(s_msg, n + 1)
                            nc.tensor.matmul(ps_m[:, u % 2, 0:H], same[:, v, :], prod[:, v, :], start=True,
                                             stop=True).then_inc(s_sum, 1)

        def far_act(act):
            act.sem_inc(s_msg, 2)
            act.sem_inc(s_hid, 2)
            act.wait_ge(s_w, 112)
            act.sem_inc(s_dyn, 1)
            with act.Fori(0, NG) as g:
                for q in range(2):
                    for c in range(2):
                        act.wait_ge(s_h, g * 4 + q * 2 + c + 1)
                        nc.scalar.activation(hid[:, q, c, :], ps_h[:, c, :], ACT.Silu,
                                             bias=b1[:, c:c + 1]).then_inc(s_hid, 1)
                    for v in range(4):
                        u = q * 4 + v
                        k = u % KACC
                        act.wait_ge(s_sum, g * G + u + 1)
                        act.wait_ge(s_add[k], (g * (G // KACC) + u // KACC + 1) * 16)
                        nc.scalar.activation(msg[:, k, :], ps_m[:, u % 2, 0:H], ACT.Copy).then_inc(s_msg, 1)

        def far_dve(dve):
            dve.sem_inc(s_gfree, 2)
            dve.sem_inc(s_prod, 2)
            with dve.Fori(0, NG // 2) as b:
                for h in range(2):
                    g = b * 2 + h
                    nc.vector.tensor_copy(cols[:], T.src_f[:, ds(g * G, G)]).then_inc(s_cols, 1)
                    dve.wait_ge(s_ld[h], (b + 1) * 64)
                    dve.wait_ge(s_cols, g + 1)
                    for u in range(G):
                        n = g * G + u
                        if u >= 4:
                            dve.wait_ge(s_sum, n - 3)
                        nc.vector.tensor_scalar(same[:, u % 4, :], rows[:, h, u, :], cols[:, u:u + 1], None,
                                                ALU.is_equal).then_inc(s_same, 1)
                        dve.wait_ge(s_ge[h][u], (b + 1) * 16)
                        dve.wait_ge(s_f, n + 1)
                        nc.vector.tensor_tensor(prod[:, u % 4, :], xd[:, h, u, :], ps_f[:, u % 2, 0:H],
                                                ALU.mult).then_inc(s_prod, 1)
                    dve.wait_ge(s_sum, (g + 1) * G)
                    dve.sem_inc(s_gfree, 1)

        nw = Near(ph, gathers=False)
        rowd = ph.sb("rowd", [P, 2, G * P])
        hotT = ph.sb("hotT", [P, 2, G * P], F32R)
        win = ph.sb("win", [P, 2, 2 * H], F32R)
        first_of = ph.sb("first_of", [P, 2, G, P], F32R)
        count = ph.sb("count", [P, 2, G])
        place = ph.sb("place", [P, 2, 3, G])
        uniq = ph.sb("uniq", [P, 2, G], I32)
        uniq_all = ph.sb("uniq_all", [P, ET], I32)
        src2 = ph.sb("src2", [P, 2, G])
        xs = ph.sb("xs", [P, 2, 2, H])
        prod2 = ph.sb("prod2", [P, 4, 2, H])
        msg2 = ph.sb("msg2", [P, 4, 2, H])
        prod_s = ph.sb("prod_s", [P, 4, 2, 2, H], F32R)
        part = ph.sb("part", [B2R, 2, H])
        cut3 = ph.sb("cut3", [B2R, 3, H], BF16)
        b2p = ph.sb("b2p", [B2R, H], BF16)
        ones_b = ph.sb("ones_b", [B2R, P], BF16)
        w1s = ph.sb("w1s", [P, H], F32R)
        eas = ph.sb("eas", [P, 2, G * P], F32R)
        ps_x = ph.ps("ps_x", [P, 2, 2, H])
        s_hotT, s_x, s_xs, s_fo, s_pl, s_id, s_b2, s_out, s_eah, s_eas, s_hi, s_lo = (
            ph.sem(n) for n in ("hotT", "x", "xs", "fo", "pl", "id", "b2", "out", "eah", "eas", "hi", "lo"))
        ps_f2 = ps_f[:].rearrange("p t (a d) -> p t a d", a=2)
        ps_m2 = ps_m[:].rearrange("p t (a d) -> p t a d", a=2)
        LAST = NG // 2 - 1

        def near_sp(sp):
            with sp.Fori(0, NG // 2) as b:
                for h in range(2):
                    g = b * 2 + h
                    first = sp.value_load(T.base[0:1, ds(g, 1)], min_val=0, max_val=NP - P)
                    sp.wait_ge(s_f, g * 4 + 4)
                    sp.sem_inc(s_dyn, 1)
                    sp.wait_ge(s_id, g + 1)
                    for r in range(0, P, R20P):
                        sp.dma_start(ea[r:r + R20P, h, :], A["ea20T"][:, ds(g * G * P, G * P)]).then_inc(s_ld[h], 16)
                    sp.dma_start(rows[:, h].rearrange("p u f -> p (u f)"),
                                 bcast_rows(T.src_rows[ds(g * G * P, G * P)], P)).then_inc(s_ld[h], 16)
                    sp.dma_start(rowd[:, h, :], bcast_rows(T.dst_rows[ds(g * G * P, G * P)], P)).then_inc(s_ld[h], 16)
                    sp.dma_start(win[:, h, :].bitcast(F32), T.x1s_tab[ds(first, P), :]).then_inc(s_ld[h], 16)
            sp.wait_ge(s_id, NG + 2)
            sp.dma_start(T.srcu_cols, uniq_all[:]).then_inc(s_out, 16)
            sp.wait_ge(s_out, 16)

        def near_pool(pool):
            zero_accumulators(pool, T.acc1, T.zeros, s_add)
            with pool.Fori(0, NG // 2) as b:
                for h in range(2):
                    g = b * 2 + h
                    for u in range(G):
                        k = u % KACC
                        if u == 0:
                            pool.wait_ge(s_id, g + 3)
                        pool.wait_ge(s_msg, g * 4 + u // 2 + 3)
                        pool.wait_ge(s_add[k], (g * (G // KACC) + u // KACC + 1) * 16)
                        pool.sem_inc(s_go, 1)
                        pool.indirect_dma_start(T.acc1[k], bass.IndirectOffsetOnAxis(uniq[:, h, u:u + 1], 0),
                                                msg2[:, u // 2, u % 2, :], None,
                                                compute_op=ALU.add).then_inc(s_add[k], 16)
            for k in range(KACC):
                pool.wait_ge(s_add[k], (NG * (G // KACC) + 1) * 16)

        def near_pe(pe):
            pe.sem_inc(s_f, 8)
            pe.sem_inc(s_sum, 8)
            pe.wait_ge(s_b2, 13)
            pe.sem_inc(s_dyn, 1)

            def hidden(m, b, h, q):
                if q == 0:
                    pe.wait_ge(s_ld[h], (b + 1) * 112)
                pe.wait_ge(s_eas, m + 1)
                for c in range(2):
                    pe.wait_ge(s_hid, m * 2 + c + 1)
                    nc.tensor.matmul(ps_h[:, c, :], w1s[:, c * P:(c + 1) * P], eas[:, h, q * 512:(q + 1) * 512],
                                     start=True, stop=True).then_inc(s_h, 1)

            def filters(g, h, i):
                n = g * 4 + i
                q = i // 2
                pe.wait_ge(s_hotT, g + 1)
                pe.wait_ge(s_xs, n + 1)
                for v in range(2):
                    e = hotT[:, h, (2 * i + v) * P:(2 * i + v + 1) * P]
                    nc.tensor.matmul(ps_x[:, i % 2, v, :], e, win[:, h, 0:H], start=True, stop=False)
                    nc.tensor.matmul(ps_x[:, i % 2, v, :], e, win[:, h, H:2 * H], start=False,
                                     stop=True).then_inc(s_x, 1)
                pe.wait_ge(s_hid, (g * 2 + q) * 2 + 4)
                pe.wait_ge(s_prod, n + 1)
                for v in range(2):
                    e = ((2 * i + v) % 4) * P
                    o = ps_f2[:, i % 2, v, :]
                    nc.tensor.matmul(o, hid[:, q, 0, e:e + P], w2[:, 0, :], start=True, stop=False)
                    nc.tensor.matmul(o, hid[:, q, 1, e:e + P], w2[:, 1, :], start=False, stop=False)
                    last = nc.tensor.matmul(o, ones_b[:], b2p[:], start=False, stop=True)
                last.then_inc(s_f, 1)

            def sums(g, h, i):
                n = g * 4 + i
                pe.wait_ge(s_lo, n + 1)
                pe.wait_ge(s_fo, (g + 1) * G)
                pe.wait_ge(s_msg, n + 1)
                for v in range(2):
                    for k in range(2):
                        last = nc.tensor.matmul(ps_m2[:, i % 2, v, :], first_of[:, h, 2 * i + v, :],
                                                prod_s[:, i, v, k, :], start=(k == 0), stop=(k == 1))
                last.then_inc(s_sum, 1)

            def group(g, b, h, start=False, last=False):
                hidden(g * 2 + 1, b, h, 1)
                for i in range(4):
                    if i == 3 and not last:
                        hidden(g * 2 + 2, b + h, 1 - h, 0)
                    filters(g, h, i)
                    if i >= 2:
                        sums(g, h, i - 2)
                    elif not start:
                        sums(g - 1, 1 - h, i + 2)

            hidden(0, 0, 0, 0)
            group(0, 0, 0, start=True)
            group(1, 0, 1)
            with pe.Fori(1, LAST) as b:
                group(b * 2, b, 0)
                group(b * 2 + 1, b, 1)
            group(NG - 2, LAST, 0)
            group(NG - 1, LAST, 1, last=True)
            sums(NG - 1, 1, 2)
            sums(NG - 1, 1, 3)

        def near_act(act):
            act.sem_inc(s_hid, 2)
            act.sem_inc(s_xs, 2)
            act.sem_inc(s_msg, 2)
            act.wait_ge(s_w, 112)
            act.sem_inc(s_dyn, 1)

            def hidden(m, q):
                for c in range(2):
                    act.wait_ge(s_h, m * 2 + c + 1)
                    nc.scalar.activation(hid[:, q, c, :], ps_h[:, c, :], ACT.Silu,
                                         bias=b1[:, c:c + 1]).then_inc(s_hid, 1)

            def features(g, i):
                act.wait_ge(s_x, g * G + 2 * i + 2)
                act.wait_ge(s_prod, g * 4 + i + 1)
                nc.scalar.activation(xs[:, i % 2], ps_x[:, i % 2], ACT.Copy).then_inc(s_xs, 1)

            def messages(g, i):
                n = g * 4 + i
                act.wait_ge(s_sum, n + 9)
                for v in range(2):
                    u = 2 * i + v
                    if not isinstance(g, int) or 2 * g + u // KACC:
                        act.wait_ge(s_add[u % KACC], (g * (G // KACC) + u // KACC) * 16)
                nc.scalar.activation(msg2[:, i], ps_m2[:, i % 2], ACT.Copy).then_inc(s_msg, 1)

            def rounded(m, b, h, q):
                if q == 0:
                    act.wait_ge(s_ld[h], (b + 1) * 112)
                cols_ = slice(q * 512, (q + 1) * 512)
                nc.scalar.activation(eas[:, h, cols_], ea[:, h, cols_], ACT.Copy).then_inc(s_eah, 1)

            def high(g, i):
                n = g * 4 + i
                act.wait_ge(s_prod, n + 3)
                act.wait_ge(s_sum, n + 5)
                nc.scalar.activation(prod_s[:, i, :, 0, :], prod2[:, i], ACT.Copy).then_inc(s_hi, 1)

            def group(g, b, h, start=False, last=False):
                hidden(g * 2 + 1, 1)
                for i in range(4):
                    if i == 3 and not last:
                        hidden(g * 2 + 2, 0)
                    features(g, i)
                    if i > 0:
                        high(g, i - 1)
                    elif not start:
                        high(g - 1, 3)
                    if i == 1 and not last:
                        rounded(g * 2 + 2, b + h, 1 - h, 0)
                        rounded(g * 2 + 3, b + h, 1 - h, 1)
                    if i == 3:
                        messages(g, 0)
                    elif not start:
                        messages(g - 1, i + 1)

            rounded(0, 0, 0, 0)
            rounded(1, 0, 0, 1)
            hidden(0, 0)
            group(0, 0, 0, start=True)
            group(1, 0, 1)
            with act.Fori(1, LAST) as b:
                group(b * 2, b, 0)
                group(b * 2 + 1, b, 1)
            group(NG - 2, LAST, 0)
            group(NG - 1, LAST, 1, last=True)
            high(NG - 1, 3)
            for i in range(1, 4):
                messages(NG - 1, i)

        def near_dve(dve):
            dve.sem_inc(s_prod, 2)
            dve.sem_inc(s_id, 2)
            nc.vector.memset(ones_b[:], 1.0).then_inc(s_b2, 1)
            nc.vector.memset(b2p[:], 0.0).then_inc(s_b2, 1)
            dve.wait_ge(s_w, 112)
            nc.vector.tensor_copy(w1s[:], w1[:]).then_inc(s_b2, 1)
            nc.vector.tensor_copy(cut3[:, 0, :], b2[:]).then_inc(s_b2, 1)
            dve.wait_ge(s_b2, 4)
            for r in (R20P, 3 * R20P):
                rr = slice(r, r + R20P)
                nc.vector.tensor_tensor(w1s[rr, :], w1[rr, :], w1s[rr, :], ALU.subtract).then_inc(s_b2, 1)
            nc.vector.tensor_tensor(part[:, 0, :], b2[:], cut3[:, 0, :], ALU.subtract).then_inc(s_b2, 1)
            dve.wait_ge(s_b2, 7)
            nc.vector.tensor_copy(cut3[:, 1, :], part[:, 0, :]).then_inc(s_b2, 1)
            dve.wait_ge(s_b2, 8)
            nc.vector.tensor_tensor(part[:, 1, :], part[:, 0, :], cut3[:, 1, :], ALU.subtract).then_inc(s_b2, 1)
            dve.wait_ge(s_b2, 9)
            nc.vector.tensor_copy(cut3[:, 2, :], part[:, 1, :]).then_inc(s_b2, 1)
            dve.wait_ge(s_b2, 10)
            for k in range(3):
                r = k * R20P
                nc.vector.tensor_copy(b2p[r:r + 1, :], cut3[r:r + 1, k, :]).then_inc(s_b2, 1)

            def leftover(m, h, q):
                dve.wait_ge(s_eah, m + 1)
                cols_ = slice(q * 512, (q + 1) * 512)
                nc.vector.tensor_tensor(eas[P // 2:P, h, cols_], ea[P // 2:P, h, cols_], eas[P // 2:P, h, cols_],
                                        ALU.subtract).then_inc(s_eas, 1)

            def low(g, i):
                dve.wait_ge(s_hi, g * 4 + i + 1)
                nc.vector.tensor_tensor(prod_s[:, i, :, 1, :], prod2[:, i], prod_s[:, i, :, 0, :],
                                        ALU.subtract).then_inc(s_lo, 1)

            def onehots(g, b, h):
                dve.wait_ge(s_ld[h], (b + 1) * 112)
                dve.wait_ge(s_f, g * 4 + 4)
                nc.vector.tensor_scalar(hotT[:, h, :], rowd[:, h, :], T.window[:, ds(g, 1)], None,
                                        ALU.is_equal).then_inc(s_hotT, 1)
                dve.wait_ge(s_id, g + 1)
                dve.sem_inc(s_dyn, 1)
                nc.vector.tensor_copy(src2[:, h, :], T.src_f[:, ds(g * G, G)]).then_inc(s_cols, 1)
                dve.wait_ge(s_cols, g + 1)
                dve.wait_ge(s_sum, g * 4 + 4)
                dve.sem_inc(s_dyn, 1)

            def firsts(g, h, us):
                for u in us:
                    nc.vector.scalar_tensor_tensor(first_of[:, h, u, :], rows[:, h, u, :], src2[:, h, u:u + 1],
                                                   T.earlier[:], ALU.is_equal, ALU.mult,
                                                   accum_out=count[:, h, u:u + 1]).then_inc(s_fo, 1)

            def places(g, h):
                dve.wait_ge(s_fo, (g + 1) * G)
                if not isinstance(g, int) or g >= 1:
                    for k in range(KACC):
                        dve.wait_ge(s_add[k], (g * (G // KACC) - 1) * 16)
                nc.vector.tensor_scalar(place[:, h, 0, :], count[:, h, :], 2.0, -1.0, ALU.min,
                                        ALU.add).then_inc(s_pl, 1)
                nc.vector.tensor_scalar(place[:, h, 1, :], src2[:, h, :], T.trash[:], -1.0, ALU.subtract,
                                        ALU.mult).then_inc(s_pl, 1)
                dve.wait_ge(s_pl, g * 3 + 2)
                nc.vector.tensor_tensor(place[:, h, 2, :], place[:, h, 0, :], place[:, h, 1, :],
                                        ALU.mult).then_inc(s_pl, 1)
                dve.wait_ge(s_pl, g * 3 + 3)
                nc.vector.tensor_tensor(uniq_all[:, ds(g * G, G)], place[:, h, 2, :], src2[:, h, :], ALU.add)
                nc.vector.tensor_tensor(uniq[:, h, :], place[:, h, 2, :], src2[:, h, :], ALU.add).then_inc(s_id, 1)

            def product(g, i):
                n = g * 4 + i
                dve.wait_ge(s_xs, n + 3)
                dve.wait_ge(s_f, n + 9)
                dve.wait_ge(s_sum, n + 5)
                nc.vector.tensor_tensor(prod2[:, i], ps_f2[:, i % 2], xs[:, i % 2], ALU.mult).then_inc(s_prod, 1)

            def group(g, b, h, start=False, last=False):
                product(g, 0)
                if not start:
                    low(g - 1, 3)
                product(g, 1)
                low(g, 0)
                if not last:
                    leftover(g * 2 + 2, 1 - h, 0)
                    onehots(g + 1, b + h, 1 - h)
                    firsts(g + 1, 1 - h, (0,))
                product(g, 2)
                low(g, 1)
                if not last:
                    leftover(g * 2 + 3, 1 - h, 1)
                    firsts(g + 1, 1 - h, (1, 2, 3))
                product(g, 3)
                low(g, 2)
                if not last:
                    firsts(g + 1, 1 - h, (4, 5, 6, 7))
                    places(g + 1, 1 - h)

            leftover(0, 0, 0)
            leftover(1, 0, 1)
            onehots(0, 0, 0)
            firsts(0, 0, range(G))
            places(0, 0)
            group(0, 0, 0, start=True)
            group(1, 0, 1)
            with dve.Fori(1, LAST) as b:
                group(b * 2, b, 0)
                group(b * 2 + 1, b, 1)
            group(NG - 2, LAST, 0)
            group(NG - 1, LAST, 1, last=True)
            low(NG - 1, 3)

        block = ph.block()

        @block.sync
        def _(sp):
            for r in range(0, P, R20P):
                sp.dma_start(w1[r:r + R20P, :], A["Wf1"]).then_inc(s_w, 16)
            sp.dma_start(w2[:], A["Wf2"].rearrange("(c p) n -> p c n", p=P)).then_inc(s_w, 16)
            sp.dma_start(b1[:], A["bf1"].rearrange("(c p) -> p c", p=P)).then_inc(s_w, 16)
            sp.dma_start(b2[:], bcast_rows(A["bf2"], B2R)).then_inc(s_w, 16)
            if_near(sp, T, lambda: near_sp(sp), lambda: far_sp(sp))

        @block.gpsimd
        def _(pool):
            if_near(pool, T, lambda: near_pool(pool), lambda: far_pool(pool))

        @block.tensor
        def _(pe):
            if_near(pe, T, lambda: near_pe(pe), lambda: far_pe(pe))

        @block.scalar
        def _(act):
            if_near(act, T, lambda: near_act(act), lambda: far_act(act))

        @block.vector
        def _(dve):
            if_near(dve, T, lambda: near_dve(dve), lambda: far_dve(dve))


def edge_layer2(nc, A, T):
    with Phase(nc, "e2") as ph:
        rows = ph.sb("rows", [P, 2, G, P])
        isrc = ph.sb("isrc", [P, 2, G], I32)
        iout = ph.sb("iout", [P, 2, G], I32)
        xs = ph.sb("xs", [P, 2, G, H])
        cols = ph.sb("cols", [P, G])
        same = ph.sb("same", [P, G, P])
        msg = ph.sb("msg", [P, 2, H])
        ps_m = ph.ps("ps_m", [P, 2, 512])
        s_ld = ph.sems("ld", 2)
        s_ge = [ph.sems(f"ge{h}_", G) for h in range(2)]
        s_ldfree, s_gfree, s_go, s_cols, s_same, s_sum, s_msg, s_add = (
            ph.sem(n) for n in ("ldfree", "gfree", "go", "cols", "same", "sum", "msg", "add"))


        def far_sp(sp):
            with sp.Fori(0, NG // 2) as b:
                for h in range(2):
                    g = b * 2 + h
                    sp.wait_ge(s_ldfree, g + 1)
                    sp.dma_start(rows[:, h].rearrange("p u f -> p (u f)"),
                                 bcast_rows(T.dst_rows[ds(g * G * P, G * P)], P)).then_inc(s_ld[h], 16)
                    sp.dma_start(isrc[:, h, :], A["src_cols"][:, ds(g * G, G)]).then_inc(s_ld[h], 16)
                    sp.dma_start(iout[:, h, :], T.dstu_cols[:, ds(g * G, G)]).then_inc(s_ld[h], 16)

        def far_pool(pool):
            pool.sem_inc(s_ldfree, 2)
            zero_accumulators(pool, [T.acc2], T.zeros, [s_add])
            with pool.Fori(0, NG // 2) as b:
                for h in range(2):
                    g = b * 2 + h
                    pool.wait_ge(s_ld[h], (b + 1) * 48)
                    pool.wait_ge(s_gfree, g + 1)
                    pool.sem_inc(s_go, 1)
                    for u in range(G):
                        pool.indirect_dma_start(xs[:, h, u, :], None, T.hs_tab,
                                                bass.IndirectOffsetOnAxis(isrc[:, h, u:u + 1], 0)).then_inc(s_ge[h][u], 16)
                    for u in range(G):
                        pool.wait_ge(s_msg, g * G + u + 3)
                        pool.wait_ge(s_add, (g * G + u + 1) * 16)
                        pool.sem_inc(s_go, 1)
                        pool.indirect_dma_start(T.acc2, bass.IndirectOffsetOnAxis(iout[:, h, u:u + 1], 0),
                                                msg[:, u % 2, :], None, compute_op=ALU.add).then_inc(s_add, 16)
                    pool.wait_ge(s_add, (g * G + G + 1) * 16)
                    pool.sem_inc(s_ldfree, 1)

        def far_pe(pe):
            with pe.Fori(0, NG // 2) as b:
                for h in range(2):
                    for u in range(G):
                        n = (b * 2 + h) * G + u
                        pe.wait_ge(s_ge[h][u], (b + 1) * 16)
                        pe.wait_ge(s_same, n + 1)
                        pe.wait_ge(s_msg, n + 1)
                        nc.tensor.matmul(ps_m[:, u % 2, 0:H], same[:, u, :], xs[:, h, u, :], start=True,
                                         stop=True).then_inc(s_sum, 1)

        def far_act(act):
            act.sem_inc(s_msg, 2)
            with act.Fori(0, NG) as g:
                for u in range(G):
                    act.wait_ge(s_sum, g * G + u + 1)
                    act.wait_ge(s_add, g * G * 16 + max(u, 1) * 16)
                    nc.scalar.activation(msg[:, u % 2, :], ps_m[:, u % 2, 0:H], ACT.Copy).then_inc(s_msg, 1)

        def far_dve(dve):
            dve.sem_inc(s_gfree, 2)
            with dve.Fori(0, NG // 2) as b:
                for h in range(2):
                    g = b * 2 + h
                    nc.vector.tensor_copy(cols[:], T.dst_f[:, ds(g * G, G)]).then_inc(s_cols, 1)
                    dve.wait_ge(s_ld[h], (b + 1) * 48)
                    dve.wait_ge(s_cols, g + 1)
                    for u in range(G):
                        nc.vector.tensor_scalar(same[:, u, :], rows[:, h, u, :], cols[:, u:u + 1], None,
                                                ALU.is_equal).then_inc(s_same, 1)
                    dve.wait_ge(s_sum, (g + 1) * G)
                    dve.sem_inc(s_gfree, 1)

        nw = Near(ph, slots=4)
        isrc4 = ph.sb("isrc4", [P, 4, G], I32)
        xs4 = ph.sb("xs4", [P, 4, G, H])
        hot = ph.sb("hot", [P, 2, G, P])
        off2 = ph.sb("off2", [P, 2, G])
        agg = ph.sb("agg", [P, 2, H])
        ps_a = ps_m
        s_ix = ph.sems("ix", 4)
        s_hot, s_red, s_agg = (ph.sem(n) for n in ("hot", "red", "agg"))
        Q = NG // 4

        def near_sp(sp):
            with sp.Fori(0, Q) as b:
                for h in range(4):
                    sp.wait_ge(s_agg, b * 4 + h + 1)
                    sp.dma_start(isrc4[:, h, :], A["src_cols"][:, ds((b * 4 + h) * G, G)]).then_inc(s_ix[h], 16)

        def near_pool(pool):
            zero_accumulators(pool, [T.acc2], T.zeros, [s_add])

            def gathers(g, b, h):
                pool.wait_ge(s_ix[h], (b + 1) * 16)
                pool.sem_inc(s_go, 1)
                for u in range(G):
                    pool.indirect_dma_start(xs4[:, h, u, :], None, T.hs_tab,
                                            bass.IndirectOffsetOnAxis(isrc4[:, h, u:u + 1], 0)).then_inc(nw.ge[h][u], 16)

            def add(g, h):
                first = pool.value_load(T.base[0:1, ds(g, 1)], min_val=0, max_val=NP - P)
                pool.wait_ge(s_agg, g + 5)
                pool.wait_ge(s_add, (g + 1) * 16)
                pool.sem_inc(s_go, 1)
                pool.dma_start(T.acc2[ds(first, P), :], agg[:, h % 2, :], accum_op=ALU.add).then_inc(s_add, 16)

            gathers(0, 0, 0)
            gathers(1, 0, 1)
            with pool.Fori(0, Q - 1) as b:
                for h in range(4):
                    gathers(b * 4 + h + 2, b + (h + 2) // 4, (h + 2) % 4)
                    add(b * 4 + h, h)
            for h in range(4):
                if h < 2:
                    gathers(NG - 2 + h, Q - 1, 2 + h)
                add(NG - 4 + h, h)
            pool.wait_ge(s_add, (NG + 1) * 16)

        def near_pe(pe):
            with pe.Fori(0, Q) as b:
                for h in range(4):
                    for u in range(G):
                        pe.wait_ge(nw.ge[h][u], (b + 1) * 16)
                        pe.wait_ge(s_hot, (b * 4 + h) * G + u + 1)
                        nc.tensor.matmul(ps_a[:, h % 2, 0:H], hot[:, h % 2, u, :], xs4[:, h, u, :], start=(u == 0),
                                         stop=(u == G - 1)).then_inc(s_red, 1)

        def near_act(act):
            act.sem_inc(s_agg, 4)
            with act.Fori(0, Q) as b:
                for h in range(4):
                    g = b * 4 + h
                    act.wait_ge(s_red, (g + 1) * G)
                    act.wait_ge(s_add, (g + 1) * 16)
                    nc.scalar.activation(agg[:, h % 2, :], ps_a[:, h % 2, 0:H], ACT.Copy).then_inc(s_agg, 1)

        def near_dve(dve):
            with dve.Fori(0, NG // 2) as b:
                for h in range(2):
                    g = b * 2 + h
                    dve.wait_ge(s_agg, g + 3)
                    dve.sem_inc(s_ldfree, 1)
                    nc.vector.tensor_copy(off2[:, h, :], T.off_f[:, ds(g * G, G)]).then_inc(s_cols, 1)
                    dve.wait_ge(s_cols, g + 1)
                    for u in range(G):
                        nc.vector.tensor_scalar(hot[:, h, u, :], T.iota_row[:], off2[:, h, u:u + 1], None,
                                                ALU.is_equal).then_inc(s_hot, 1)

        block = ph.block()

        @block.sync
        def _(sp):
            if_near(sp, T, lambda: near_sp(sp), lambda: far_sp(sp))

        @block.gpsimd
        def _(pool):
            if_near(pool, T, lambda: near_pool(pool), lambda: far_pool(pool))

        @block.tensor
        def _(pe):
            if_near(pe, T, lambda: near_pe(pe), lambda: far_pe(pe))

        @block.scalar
        def _(act):
            if_near(act, T, lambda: near_act(act), lambda: far_act(act))

        @block.vector
        def _(dve):
            if_near(dve, T, lambda: near_dve(dve), lambda: far_dve(dve))


def edge_layer3(nc, A, T):
    with Phase(nc, "e3") as ph:
        rows = ph.sb("rows", [P, 2, G, P])
        isrc = ph.sb("isrc", [P, 2, G], I32)
        idst = ph.sb("idst", [P, 2, G], I32)
        iout = ph.sb("iout", [P, 2, G], I32)
        xr = ph.sb("xr", [P, 2, G, XR])
        el = ph.sb("el", [P, 2, G, HEADS])
        z = ph.sb("z", [P, 2, G, HEADS])
        pay = ph.sb("pay", [P, G, PAY])
        cols = ph.sb("cols", [P, G])
        same = ph.sb("same", [P, G, P])
        msg = ph.sb("msg", [P, KACC, PAY])
        ps_m = ph.ps("ps_m", [P, 2, 512])
        s_ld = ph.sems("ld", 2)
        s_ge = ph.sems("ge", 2)
        s_ldfree, s_gfree, s_go, s_cols, s_z, s_exp, s_pay, s_same, s_sum, s_msg = (
            ph.sem(n) for n in ("ldfree", "gfree", "go", "cols", "z", "exp", "pay", "same", "sum", "msg"))
        s_add = ph.sems("add", KACC)


        def far_sp(sp):
            with sp.Fori(0, NG // 2) as b:
                for h in range(2):
                    g = b * 2 + h
                    sp.wait_ge(s_ldfree, g + 1)
                    sp.dma_start(rows[:, h].rearrange("p u f -> p (u f)"),
                                 bcast_rows(T.src_rows[ds(g * G * P, G * P)], P)).then_inc(s_ld[h], 16)
                    sp.dma_start(isrc[:, h, :], A["src_cols"][:, ds(g * G, G)]).then_inc(s_ld[h], 16)
                    sp.dma_start(idst[:, h, :], A["dst_cols"][:, ds(g * G, G)]).then_inc(s_ld[h], 16)
                    sp.dma_start(iout[:, h, :], T.srcu_cols[:, ds(g * G, G)]).then_inc(s_ld[h], 16)

        def far_pool(pool):
            pool.sem_inc(s_ldfree, 2)
            zero_accumulators(pool, T.acc3, T.zeros, s_add)
            with pool.Fori(0, NG // 2) as b:
                for h in range(2):
                    g = b * 2 + h
                    pool.wait_ge(s_ld[h], (b + 1) * 64)
                    pool.wait_ge(s_gfree, g + 1)
                    pool.sem_inc(s_go, 1)
                    for u in range(G):
                        pool.indirect_dma_start(xr[:, h, u, :], None, T.xr_tab,
                                                bass.IndirectOffsetOnAxis(idst[:, h, u:u + 1], 0)).then_inc(s_ge[h], 16)
                        pool.indirect_dma_start(el[:, h, u, :], None, T.el_tab,
                                                bass.IndirectOffsetOnAxis(isrc[:, h, u:u + 1], 0)).then_inc(s_ge[h], 16)
                    for u in range(G):
                        pool.wait_ge(s_msg, g * G + u + 3)
                        pool.wait_ge(s_add[u % KACC], (g * (G // KACC) + u // KACC + 1) * 16)
                        pool.sem_inc(s_go, 1)
                        pool.indirect_dma_start(T.acc3[u % KACC], bass.IndirectOffsetOnAxis(iout[:, h, u:u + 1], 0),
                                                msg[:, u % KACC, :], None,
                                                compute_op=ALU.add).then_inc(s_add[u % KACC], 16)
                    for k in range(KACC):
                        pool.wait_ge(s_add[k], ((g + 1) * (G // KACC) + 1) * 16)
                    pool.sem_inc(s_ldfree, 1)

        def far_pe(pe):
            with pe.Fori(0, NG // 2) as b:
                for h in range(2):
                    for u in range(G):
                        n = (b * 2 + h) * G + u
                        pe.wait_ge(s_pay, n * 2 + 2)
                        pe.wait_ge(s_msg, n + 1)
                        nc.tensor.matmul(ps_m[:, u % 2, 0:PAY], same[:, u, :], pay[:, u, :], start=True,
                                         stop=True).then_inc(s_sum, 1)

        def far_act(act):
            act.sem_inc(s_msg, 2)
            with act.Fori(0, NG) as g:
                act.wait_ge(s_z, (g + 1) * 2)
                nc.scalar.activation(pay[:, :, HEADS * DOUT:PAY], z[:, 1, :, :], ACT.Exp).then_inc(s_exp, 1)
                for u in range(G):
                    act.wait_ge(s_sum, g * G + u + 1)
                    act.wait_ge(s_add[u % KACC], (g * (G // KACC) + u // KACC + 1) * 16)
                    nc.scalar.activation(msg[:, u % KACC, :], ps_m[:, u % 2, 0:PAY], ACT.Copy).then_inc(s_msg, 1)

        def far_dve(dve):
            dve.sem_inc(s_gfree, 2)
            with dve.Fori(0, NG // 2) as b:
                for h in range(2):
                    g = b * 2 + h
                    nc.vector.tensor_copy(cols[:], T.src_f[:, ds(g * G, G)]).then_inc(s_cols, 1)
                    dve.wait_ge(s_ge[h], (b + 1) * 2 * G * 16)
                    nc.vector.tensor_tensor(z[:, 0, :, :], el[:, h, :, :], xr[:, h, :, DOUT:XR],
                                            ALU.add).then_inc(s_z, 1)
                    dve.wait_ge(s_z, g * 2 + 1)
                    nc.vector.scalar_tensor_tensor(z[:, 1, :, :], z[:, 0, :, :], 0.2, z[:, 0, :, :],
                                                   ALU.mult, ALU.max).then_inc(s_z, 1)
                    dve.wait_ge(s_ld[h], (b + 1) * 64)
                    dve.wait_ge(s_cols, g + 1)
                    for u in range(G):
                        nc.vector.tensor_scalar(same[:, u, :], rows[:, h, u, :], cols[:, u:u + 1], None,
                                                ALU.is_equal).then_inc(s_same, 1)
                    dve.wait_ge(s_exp, g + 1)
                    for u in range(G):
                        for e in range(2):
                            x2 = xr[:, h, u, None, 0:DOUT].to_broadcast([P, 2, DOUT])
                            e2 = pay[:, u, HEADS * DOUT + 2 * e:HEADS * DOUT + 2 * e + 2][:, :, None]
                            nc.vector.tensor_tensor(
                                pay[:, u, e * 2 * DOUT:(e + 1) * 2 * DOUT].rearrange("p (a d) -> p a d", a=2),
                                x2, e2.to_broadcast([P, 2, DOUT]), ALU.mult).then_inc(s_pay, 1)
                    dve.wait_ge(s_sum, (g + 1) * G)
                    dve.sem_inc(s_gfree, 1)

        nw = Near(ph, gathers=False)
        rowd = ph.sb("rowd", [P, 2, G * P])
        rowl = ph.sb("rowl", [P, 2, G * P])
        hotT = ph.sb("hotT", [P, 2, G * P])
        hotL = ph.sb("hotL", [P, 2, G * P])
        win = ph.sb("win", [P, 2, XR])
        idx2 = ph.sb("idx2", [P, 2, G], I32)
        uniq_all = ph.sb("uniq_all", [P, ET], I32)
        src2 = ph.sb("src2", [P, 2, G])
        hi2 = ph.sb("hi2", [P, 2, G])
        same2 = ph.sb("same2", [P, 2, G, P])
        pick = ph.sb("pick", [P, 2, 2, NT * HEADS])
        els = ph.sb("els", [P, 2, 2, HEADS])
        z2 = ph.sb("z2", [P, 2, 2, 2, HEADS])
        pay2 = ph.sb("pay2", [P, 4, 2, PAY])
        msg2 = ph.sb("msg2", [P, 4, 2, PAY])
        ps_e = ph.ps("ps_e", [P, 2, 512])
        ps_x = ph.ps("ps_x", [P, 2, 512])
        ps_n = ph.ps("ps_n", [P, 2, 512])
        sums2 = [ps_m, ps_n]
        s_hot, s_e, s_x, s_pick, s_els, s_sm, s_uniq, s_idx = (
            ph.sem(n) for n in ("hot", "e", "x", "pick", "els", "sm", "uniq", "idx"))
        LAST = NG // 2 - 1
        WE = NT * HEADS

        def near_sp(sp):
            sp.dma_start(uniq_all[:], T.srcu_cols).then_inc(s_uniq, 16)
            with sp.Fori(0, NG // 2) as b:
                for h in range(2):
                    g = b * 2 + h
                    first = sp.value_load(T.base[0:1, ds(g, 1)], min_val=0, max_val=NP - P)
                    sp.wait_ge(s_x, g * G + G)
                    sp.sem_inc(s_go, 1)
                    sp.wait_ge(s_sm, g * G + G)
                    sp.dma_start(rows[:, h].rearrange("p u f -> p (u f)"),
                                 bcast_rows(T.src_rows[ds(g * G * P, G * P)], P)).then_inc(s_ld[h], 16)
                    sp.dma_start(rowd[:, h, :], bcast_rows(T.dst_rows[ds(g * G * P, G * P)], P)).then_inc(s_ld[h], 16)
                    sp.dma_start(rowl[:, h, :], bcast_rows(T.lo_rows[ds(g * G * P, G * P)], P)).then_inc(s_ld[h], 16)
                    sp.dma_start(win[:, h, :], T.xr_tab[ds(first, P), :]).then_inc(s_ld[h], 16)

        def near_pool(pool):
            zero_accumulators(pool, T.acc3, T.zeros, s_add)
            pool.wait_ge(s_uniq, 16)
            pool.sem_inc(s_go, 1)

            def group(g, b, h):
                nc.gpsimd.tensor_copy(idx2[:, h, :], uniq_all[:, ds(g * G, G)]).then_inc(s_idx, 1)
                pool.wait_ge(s_idx, g + 1)
                for u in range(G):
                    k = u % KACC
                    pool.wait_ge(s_msg, g * 4 + u // 2 + 3)
                    pool.wait_ge(s_add[k], (g * (G // KACC) + u // KACC + 1) * 16)
                    pool.sem_inc(s_go, 1)
                    pool.indirect_dma_start(T.acc3[k], bass.IndirectOffsetOnAxis(idx2[:, h, u:u + 1], 0),
                                            msg2[:, u // 2, u % 2, :], None,
                                            compute_op=ALU.add).then_inc(s_add[k], 16)

            with pool.Fori(0, NG // 2) as b:
                group(b * 2, b, 0)
                group(b * 2 + 1, b, 1)
            for k in range(KACC):
                pool.wait_ge(s_add[k], (NG * (G // KACC) + 1) * 16)

        def near_pe(pe):
            pe.sem_inc(s_x, 2 * G)
            pe.sem_inc(s_sum, 8)

            def scores(g, b, h, i):
                n = g * 4 + i
                if i == 0:
                    pe.wait_ge(s_ld[h], (b + 1) * 64)
                    pe.wait_ge(s_hot, g + 1)
                pe.wait_ge(s_pick, n * 2 + 2)
                for v in range(2):
                    e = slice((2 * i + v) * P, (2 * i + v + 1) * P)
                    nc.tensor.matmul(ps_e[:, i % 2, v * WE:(v + 1) * WE], hotL[:, h, e],
                                     T.el_res[:].rearrange("p n k -> p (n k)"), start=True, stop=True).then_inc(s_e, 1)
                pe.wait_ge(s_pay, n + 1)
                for v in range(2):
                    e = slice((2 * i + v) * P, (2 * i + v + 1) * P)
                    nc.tensor.matmul(ps_x[:, i % 2, v * XR:(v + 1) * XR], hotT[:, h, e], win[:, h, :],
                                     start=True, stop=True).then_inc(s_x, 1)

            def sums(g, h, i):
                n = g * 4 + i
                pe.wait_ge(s_pay, n + 3)
                pe.wait_ge(s_msg, n + 1)
                for v in range(2):
                    last = nc.tensor.matmul(sums2[i % 2][:, v, 0:PAY], same2[:, h, 2 * i + v, :], pay2[:, i, v, :],
                                            start=True, stop=True)
                last.then_inc(s_sum, 1)

            def group(g, b, h, start=False):
                for i in range(4):
                    scores(g, b, h, i)
                    if i >= 2:
                        sums(g, h, i - 2)
                    elif not start:
                        sums(g - 1, 1 - h, i + 2)

            group(0, 0, 0, start=True)
            group(1, 0, 1)
            with pe.Fori(1, NG // 2) as b:
                group(b * 2, b, 0)
                group(b * 2 + 1, b, 1)
            sums(NG - 1, 1, 2)
            sums(NG - 1, 1, 3)

        def near_act(act):
            act.sem_inc(s_msg, 2)

            def weights(g, i):
                n = g * 4 + i
                act.wait_ge(s_z, n * 2 + 2)
                act.wait_ge(s_sum, n + 5)
                nc.scalar.activation(pay2[:, i, :, HEADS * DOUT:PAY], z2[:, i % 2, 1], ACT.Exp).then_inc(s_exp, 1)

            def messages(g, i):
                n = g * 4 + i
                act.wait_ge(s_sum, n + 9)
                for v in range(2):
                    u = 2 * i + v
                    if not isinstance(g, int) or 2 * g + u // KACC:
                        act.wait_ge(s_add[u % KACC], (g * (G // KACC) + u // KACC) * 16)
                nc.scalar.activation(msg2[:, i], sums2[i % 2][:, :, 0:PAY], ACT.Copy).then_inc(s_msg, 1)

            def group(g, start=False):
                for i in range(4):
                    weights(g, i)
                    if i >= 2:
                        messages(g, i - 2)
                    elif not start:
                        messages(g - 1, i + 2)

            group(0, start=True)
            group(1)
            with act.Fori(1, NG // 2) as b:
                group(b * 2)
                group(b * 2 + 1)
            messages(NG - 1, 2)
            messages(NG - 1, 3)

        def near_dve(dve):
            dve.sem_inc(s_sm, 2 * G)
            dve.sem_inc(s_pay, 2)
            dve.sem_inc(s_pick, 4)

            def hots(g, b, h):
                dve.wait_ge(s_ld[h], (b + 1) * 64)
                dve.wait_ge(s_x, g * G + G)
                nc.vector.tensor_scalar(hotT[:, h, :], rowd[:, h, :], T.window[:, ds(g, 1)], None, ALU.is_equal)
                nc.vector.tensor_scalar(hotL[:, h, :], rowl[:, h, :], T.iota_col[:], None,
                                        ALU.is_equal).then_inc(s_hot, 1)
                dve.wait_ge(s_sm, g * G + G)
                dve.sem_inc(s_go, 1)
                nc.vector.tensor_copy(src2[:, h, :], T.src_f[:, ds(g * G, G)])
                nc.vector.tensor_copy(hi2[:, h, :], T.hi_f[:, ds(g * G, G)]).then_inc(s_cols, 1)

            def same_source(g, h, u):
                if u == 0:
                    dve.wait_ge(s_cols, g + 1)
                dve.wait_ge(s_sum, g * 4 + u // 2 + 1)
                nc.vector.tensor_scalar(same2[:, h, u, :], rows[:, h, u, :], src2[:, h, u:u + 1], None,
                                        ALU.is_equal).then_inc(s_sm, 1)

            def payload(g, i):
                n = g * 4 + i
                dve.wait_ge(s_exp, n + 1)
                x4 = ps_x[:, i % 2, 0:2 * XR].rearrange("p (v d) -> p v d", v=2)[:, :, None, 0:DOUT]
                e4 = pay2[:, i, :, HEADS * DOUT:PAY][:, :, :, None]
                nc.vector.tensor_tensor(pay2[:, i, :, 0:HEADS * DOUT].rearrange("p v (k d) -> p v k d", k=HEADS),
                                        x4.to_broadcast([P, 2, HEADS, DOUT]),
                                        e4.to_broadcast([P, 2, HEADS, DOUT]), ALU.mult).then_inc(s_pay, 1)

            def group(g, b, h, last=False):
                for i in range(4):
                    n = g * 4 + i
                    dve.wait_ge(s_e, g * G + 2 * i + 2)
                    for v in range(2):
                        nc.vector.scalar_tensor_tensor(pick[:, i % 2, v, :], T.iota_hi[:].rearrange("p n k -> p (n k)"),
                                                       hi2[:, h, 2 * i + v:2 * i + v + 1],
                                                       ps_e[:, i % 2, v * WE:(v + 1) * WE], ALU.is_equal,
                                                       ALU.mult).then_inc(s_pick, 1)
                    if i == 0 and not last:
                        hots(g + 1, b + h, 1 - h)
                    if not last:
                        same_source(g + 1, 1 - h, 2 * i)
                    dve.wait_ge(s_pick, n * 2 + 6)
                    nc.vector.reduce_sum(els[:, i % 2], pick[:, i % 2].rearrange("p v (n k) -> p v k n", k=HEADS),
                                         axis=AX.X).then_inc(s_els, 1)
                    if not last:
                        same_source(g + 1, 1 - h, 2 * i + 1)
                    dve.wait_ge(s_els, n + 1)
                    dve.wait_ge(s_x, g * G + 2 * i + 2 + 2 * G)
                    nc.vector.tensor_tensor(z2[:, i % 2, 0], els[:, i % 2],
                                            ps_x[:, i % 2, 0:2 * XR].rearrange("p (v d) -> p v d", v=2)[:, :, DOUT:XR],
                                            ALU.add).then_inc(s_z, 1)
                    if i > 0:
                        payload(g, i - 1)
                    dve.wait_ge(s_z, n * 2 + 1)
                    nc.vector.scalar_tensor_tensor(z2[:, i % 2, 1], z2[:, i % 2, 0], 0.2, z2[:, i % 2, 0],
                                                   ALU.mult, ALU.max).then_inc(s_z, 1)
                payload(g, 3)

            hots(0, 0, 0)
            for u in range(G):
                same_source(0, 0, u)
            with dve.Fori(0, LAST) as b:
                group(b * 2, b, 0)
                group(b * 2 + 1, b, 1)
            group(NG - 2, LAST, 0)
            group(NG - 1, LAST, 1, last=True)

        block = ph.block()

        @block.sync
        def _(sp):
            if_near(sp, T, lambda: near_sp(sp), lambda: far_sp(sp))

        @block.gpsimd
        def _(pool):
            if_near(pool, T, lambda: near_pool(pool), lambda: far_pool(pool))

        @block.tensor
        def _(pe):
            if_near(pe, T, lambda: near_pe(pe), lambda: far_pe(pe))

        @block.scalar
        def _(act):
            if_near(act, T, lambda: near_act(act), lambda: far_act(act))

        @block.vector
        def _(dve):
            if_near(dve, T, lambda: near_dve(dve), lambda: far_dve(dve))


def node_after0(nc, A, ident, ones_row, tiles, acc0, x1_tab, x1s_tab, deg):
    with Phase(nc, "n0") as ph:
        w = ph.sb("w", [P, 2, H])
        bias = ph.sb("bias", [1, H])
        x = ph.sb("x", [P, NB, H])
        agg = ph.sb("agg", [P, NB, H + 1])
        xT = ph.sb("xT", [P, 2, 2, P])
        y = ph.sb("y", [P, NB, H])
        yhat = ph.sb("yhat", [P, NB, H])
        parts = ph.sb("parts", [P, NB, 2, H], F32R)
        stats = ph.sb("stats", [P, NB, 6])
        mv = ph.sb("mv", [P, NB, 2])
        rstd = ph.sb("rstd", [P, 3, NB])
        ps_t = ph.ps("ps_t", [P, 2, 4, P])
        ps_y = ph.ps("ps_y", [P, 2, 512])
        (s_w, s_ld, s_free, s_stats, s_var, s_sqrt, s_rinv, s_norm, s_t, s_xT, s_y, s_ys, s_go, s_st,
         s_yfree) = (ph.sem(n) for n in ("w", "ld", "free", "stats", "var", "sqrt", "rinv", "norm", "t", "xT", "y",
                                         "ys", "go", "st", "yfree"))
        s_hi, s_lo, s_deg = ph.sem("hi"), ph.sem("lo"), ph.sem("deg")
        block = ph.block()
        IT = NT // NB

        @block.sync
        def _(sp):
            sp.dma_start(w[:], A["WoT"].rearrange("(c p) n -> p c n", p=P)).then_inc(s_w, 16)
            sp.dma_start(bias[:], A["bo"].rearrange("(a n) -> a n", a=1)).then_inc(s_w, 16)
            with sp.Fori(0, IT) as it:
                sp.wait_ge(s_free, it + 1)
                sp.dma_start(x[:], tiles(A["x"])[:, ds(it * NB, NB), :]).then_inc(s_ld, 16)
                sp.dma_start(agg[:], tiles(acc0)[:, ds(it * NB, NB), :]).then_inc(s_ld, 16)

        @block.tensor
        def _(pe):
            pe.wait_ge(s_w, 32)
            with pe.Fori(0, IT) as it:
                pe.wait_ge(s_ld, (it + 1) * 32)
                for u in range(NB):
                    n = it * NB + u
                    pe.wait_ge(s_y, n + 1)
                    for c in range(2):
                        nc.tensor.transpose(ps_t[:, 0, c, :], agg[:, u, c * P:(c + 1) * P], ident[:]).then_inc(s_t, 1)
                    pe.wait_ge(s_xT, n + 1)
                    o = ps_y[:, 0, 0:H]
                    nc.tensor.matmul(o, xT[:, 0, 0, :], w[:, 0, :], start=True, stop=False)
                    nc.tensor.matmul(o, xT[:, 0, 1, :], w[:, 1, :], start=False, stop=False)
                    nc.tensor.matmul(o, ones_row[:], bias[:], start=False, stop=True).then_inc(s_ys, 1)

        @block.scalar
        def _(act):
            with act.Fori(0, IT) as it:
                for u in range(NB):
                    n = it * NB + u
                    act.wait_ge(s_t, n * 2 + 2)
                    nc.scalar.activation(xT[:, 0, :, :], ps_t[:, 0, 0:2, :], ACT.Copy).then_inc(s_xT, 1)
                layernorm_root(nc, act, rstd, s_var, s_sqrt, it)
                act.wait_ge(s_norm, (it + 1) * NB)
                act.wait_ge(s_yfree, it + 1)
                nc.scalar.activation(parts[:, :, 0, :], yhat[:], ACT.Copy).then_inc(s_hi, 1)

        @block.vector
        def _(dve):
            dve.sem_inc(s_free, 1)
            dve.sem_inc(s_y, 1)
            with dve.Fori(0, IT) as it:
                for u in range(NB):
                    dve.wait_ge(s_ys, it * NB + u + 1)
                    nc.vector.scalar_tensor_tensor(y[:, u, :], x[:, u, :], 2.0, ps_y[:, 0, 0:H], ALU.mult,
                                                   ALU.add).then_inc(s_y, 1)
                nc.vector.tensor_tensor(deg[:, ds(it * NB, NB)], deg[:, ds(it * NB, NB)], agg[:, :, H],
                                        ALU.add).then_inc(s_deg, 1)
                dve.wait_ge(s_y, (it + 1) * NB + 1)
                dve.wait_ge(s_deg, it + 1)
                dve.sem_inc(s_free, 1)
                dve.wait_ge(s_yfree, it + 1)
                layernorm_batch(nc, dve, y, yhat, stats, mv, rstd, s_stats, s_var, s_sqrt, s_rinv, s_norm, s_go, it)
                dve.wait_ge(s_hi, it + 1)
                nc.vector.tensor_tensor(parts[:, :, 1, :], yhat[:], parts[:, :, 0, :], ALU.subtract).then_inc(s_lo, 1)

        store_batches(nc, block, [(tiles(x1_tab), yhat[:]),
                                  (tiles(x1s_tab), parts[:].rearrange("p n a d -> p n (a d)").bitcast(F32))],
                      s_lo, 1, 0, s_go, s_st, s_yfree)


def store_batches(nc, block, pairs, s_ready, per, extra, s_go, s_st, s_free):
    @block.gpsimd
    def _(pool):
        pool.sem_inc(s_free, 1)
        with pool.Fori(0, NT // NB) as it:
            pool.wait_ge(s_ready, (it + 1) * per + extra)
            pool.sem_inc(s_go, 1)
            for dst, buf in pairs:
                pool.dma_start(dst[:, ds(it * NB, NB), :], buf).then_inc(s_st, 16)
            pool.wait_ge(s_st, (it + 1) * 16 * len(pairs))
            pool.sem_inc(s_free, 1)


def node_after1(nc, A, ident, ones_row, tiles, acc1, x1_tab, x2_tab, hs_tab, deg, dinv):
    IT = NT // NB
    with Phase(nc, "n1") as outer:
        hT = outer.sb("hT", [P, 2, NP])
        with Phase(nc, "n1a") as ph:
            w1 = ph.sb("w1", [P, 2, H])
            w2 = ph.sb("w2", [P, 2, H])
            b1 = ph.sb("b1", [P, 2])
            b2 = ph.sb("b2", [P, 2])
            part = ph.sb("part", [P, KACC, NB, H])
            agg = ph.sb("agg", [P, NB, H])
            aT = ph.sb("aT", [P, 2, P])
            hid = ph.sb("hid", [P, 2, P])
            ps_t = ph.ps("ps_t", [P, 512])
            ps_u = ph.ps("ps_u", [P, 2, 512])
            ps_h = ph.ps("ps_h", [P, 2, 512])
            s_w, s_ld, s_free, s_sum, s_t, s_aT, s_u, s_hid, s_h, s_hT, s_dyn = (
                ph.sem(n) for n in ("w", "ld", "free", "sum", "t", "aT", "u", "hid", "h", "hT", "dyn"))
            block = ph.block()

            @block.sync
            def _(sp):
                sp.dma_start(w1[:], A["Wu1"].rearrange("(c p) n -> p c n", p=P)).then_inc(s_w, 16)
                sp.dma_start(w2[:], A["Wu2"].rearrange("(c p) n -> p c n", p=P)).then_inc(s_w, 16)
                sp.dma_start(b1[:], A["bu1"].rearrange("(c p) -> p c", p=P)).then_inc(s_w, 16)
                sp.dma_start(b2[:], A["bu2"].rearrange("(c p) -> p c", p=P)).then_inc(s_w, 16)
                with sp.Fori(0, IT) as it:
                    sp.wait_ge(s_free, it + 1)
                    for k in range(KACC):
                        sp.dma_start(part[:, k], tiles(acc1[k])[:, ds(it * NB, NB), :]).then_inc(s_ld, 16)

            @block.tensor
            def _(pe):
                pe.wait_ge(s_w, 64)
                pe.sem_inc(s_dyn, 1)
                with pe.Fori(0, IT) as it:
                    for u in range(NB):
                        n = it * NB + u
                        pe.wait_ge(s_sum, (it + 1) * 3)
                        for c in range(2):
                            nc.tensor.transpose(ps_t[:, c * P:(c + 1) * P], agg[:, u, c * P:(c + 1) * P],
                                                ident[:]).then_inc(s_t, 1)
                        pe.wait_ge(s_aT, n + 1)
                        for c in range(2):
                            for k in range(2):
                                nc.tensor.matmul(ps_u[:, c, 0:P], w1[:, k, c * P:(c + 1) * P], aT[:, k, :],
                                                 start=(k == 0), stop=(k == 1)).then_inc(s_u, 1)
                        pe.wait_ge(s_hid, n * 2 + 2)
                        pe.wait_ge(s_hT, n * 2 + 1)
                        for c in range(2):
                            for k in range(2):
                                nc.tensor.matmul(ps_h[:, c, 0:P], w2[:, k, c * P:(c + 1) * P], hid[:, k, :],
                                                 start=(k == 0), stop=(k == 1)).then_inc(s_h, 1)

            @block.scalar
            def _(act):
                act.wait_ge(s_w, 64)
                act.sem_inc(s_dyn, 1)
                with act.Fori(0, NT) as n:
                    act.wait_ge(s_t, n * 2 + 2)
                    nc.scalar.activation(aT[:].rearrange("p a b -> p (a b)"), ps_t[:, 0:2 * P], ACT.Copy).then_inc(s_aT, 1)
                    act.wait_ge(s_u, n * 4 + 4)
                    for c in range(2):
                        nc.scalar.activation(hid[:, c, :], ps_u[:, c, 0:P], ACT.Silu,
                                             bias=b1[:, c:c + 1]).then_inc(s_hid, 1)

            @block.vector
            def _(dve):
                dve.sem_inc(s_hT, 1)
                dve.sem_inc(s_free, 1)
                with dve.Fori(0, IT) as it:
                    dve.wait_ge(s_ld, (it + 1) * 16 * KACC)
                    nc.vector.tensor_tensor(part[:, 0], part[:, 0], part[:, 1], ALU.add).then_inc(s_sum, 1)
                    nc.vector.tensor_tensor(part[:, 2], part[:, 2], part[:, 3], ALU.add).then_inc(s_sum, 1)
                    dve.wait_ge(s_sum, it * 3 + 2)
                    nc.vector.tensor_tensor(agg[:], part[:, 0], part[:, 2], ALU.add).then_inc(s_sum, 1)
                    dve.wait_ge(s_sum, it * 3 + 3)
                    dve.sem_inc(s_free, 1)
                    for u in range(NB):
                        n = it * NB + u
                        dve.wait_ge(s_h, n * 4 + 4)
                        for c in range(2):
                            nc.vector.tensor_scalar(hT[:, c, ds(n * P, P)], ps_h[:, c, 0:P], b2[:, c:c + 1], None,
                                                    ALU.add).then_inc(s_hT, 1)

        with Phase(nc, "n1b") as ph:
            w = ph.sb("w", [P, 2, H])
            gamma = ph.sb("gamma", [P, 2])
            beta = ph.sb("beta", [P, 2])
            chunks = [(c, min(512, N - c)) for c in range(0, N, 512)]
            bstats = ph.sb("bstats", [P, 2, len(chunks), 6])
            bmv = ph.sb("bmv", [P, 2, 2])
            bn = ph.sb("bn", [P, 5, 2])
            hb = ph.sb("hb", [P, 2, P])
            x = ph.sb("x", [P, NB, H])
            y = ph.sb("y", [P, NB, H])
            yhat = ph.sb("yhat", [P, NB, H])
            xT = ph.sb("xT", [P, 2, P])
            hs = ph.sb("hs", [P, NB, H])
            dcol = ph.sb("dcol", [P, NB])
            root = ph.sb("root", [P, 2, NT])
            stats = ph.sb("stats", [P, NB, 6])
            mv = ph.sb("mv", [P, NB, 2])
            rstd = ph.sb("rstd", [P, 3, NB])
            ps_b = ph.ps("ps_b", [P, 512])
            ps_t = ph.ps("ps_t", [P, 512])
            ps_y = ph.ps("ps_y", [P, 512])
            (s_w, s_ld, s_free, s_stats, s_var, s_sqrt, s_rinv, s_norm, s_t, s_xT, s_y, s_ys, s_go, s_st,
             s_yfree, s_hb, s_b, s_bn, s_bsq, s_hs, s_dc) = (
                ph.sem(n) for n in ("w", "ld", "free", "stats", "var", "sqrt", "rinv", "norm", "t", "xT", "y",
                                    "ys", "go", "st", "yfree", "hb", "b", "bn", "bsq", "hs", "dc"))
            block = ph.block()

            @block.sync
            def _(sp):
                sp.dma_start(w[:], A["W2"].rearrange("(c p) n -> p c n", p=P)).then_inc(s_w, 16)
                sp.dma_start(gamma[:], A["gamma"].rearrange("(c p) -> p c", p=P)).then_inc(s_w, 16)
                sp.dma_start(beta[:], A["beta"].rearrange("(c p) -> p c", p=P)).then_inc(s_w, 16)
                with sp.Fori(0, IT) as it:
                    sp.wait_ge(s_free, it + 1)
                    sp.dma_start(x[:], tiles(x1_tab)[:, ds(it * NB, NB), :]).then_inc(s_ld, 16)

            @block.tensor
            def _(pe):
                pe.wait_ge(s_w, 48)
                with pe.Fori(0, IT) as it:
                    for u in range(NB):
                        n = it * NB + u
                        pe.wait_ge(s_hb, n * 2 + 2)
                        pe.wait_ge(s_y, n + 1)
                        for c in range(2):
                            nc.tensor.transpose(ps_b[:, c * P:(c + 1) * P], hb[:, c, :], ident[:]).then_inc(s_b, 1)
                    for u in range(NB):
                        n = it * NB + u
                        pe.wait_ge(s_norm, n + 1)
                        for c in range(2):
                            nc.tensor.transpose(ps_t[:, c * P:(c + 1) * P], yhat[:, u, c * P:(c + 1) * P],
                                                ident[:]).then_inc(s_t, 1)
                        pe.wait_ge(s_xT, n + 1)
                        pe.wait_ge(s_hs, n + 1)
                        nc.tensor.matmul(ps_y[:, 0:H], xT[:, 0, :], w[:, 0, :], start=True, stop=False)
                        nc.tensor.matmul(ps_y[:, 0:H], xT[:, 1, :], w[:, 1, :], start=False, stop=True).then_inc(s_ys, 1)

            @block.scalar
            def _(act):
                act.wait_ge(s_bn, 1)
                nc.scalar.activation(bn[:, 1, :], bn[:, 0, :], ACT.Sqrt)
                nc.scalar.activation(root[:, 1, :], root[:, 0, :], ACT.Sqrt).then_inc(s_bsq, 1)
                act.sem_inc(s_hs, 1)
                with act.Fori(0, IT) as it:
                    layernorm_root(nc, act, rstd, s_var, s_sqrt, it)
                    act.wait_ge(s_dc, it + 1)
                    act.wait_ge(s_yfree, it + 1)
                    act.sem_inc(s_go, 1)
                    for u in range(NB):
                        n = it * NB + u
                        act.wait_ge(s_t, n * 2 + 2)
                        nc.scalar.activation(xT[:].rearrange("p a b -> p (a b)"), ps_t[:, 0:2 * P], ACT.Copy).then_inc(s_xT, 1)
                        act.wait_ge(s_ys, n + 1)
                        nc.scalar.activation(hs[:, u, :], ps_y[:, 0:H], ACT.Copy, scale=dcol[:, u:u + 1]).then_inc(s_hs, 1)

            @block.vector
            def _(dve):
                for c in range(2):
                    for k, (a, m) in enumerate(chunks):
                        nc.vector.bn_stats(bstats[:, c, k, :], hT[:, c, a:a + m]).then_inc(s_stats, 1)
                nb = 2 * len(chunks)
                dve.wait_ge(s_stats, nb)
                for c in range(2):
                    nc.vector.bn_aggr(bmv[:, c, :], bstats[:, c, :, :]).then_inc(s_dc, 1)
                dve.wait_ge(s_dc, 2)
                nc.vector.tensor_scalar(root[:, 0, :], deg[:], 1.0, None, ALU.add)
                nc.vector.tensor_scalar(bn[:, 0, :], bmv[:, :, 1], LN_EPS, None, ALU.add).then_inc(s_bn, 1)
                dve.wait_ge(s_bsq, 1)
                nc.vector.reciprocal(dinv[:], root[:, 1, :])
                nc.vector.reciprocal(bn[:, 2, :], bn[:, 1, :]).then_inc(s_bn, 1)
                dve.wait_ge(s_bn, 2)
                dve.wait_ge(s_w, 48)
                nc.vector.tensor_tensor(bn[:, 3, :], bn[:, 2, :], gamma[:], ALU.mult).then_inc(s_bn, 1)
                dve.wait_ge(s_bn, 3)
                nc.vector.tensor_tensor(bn[:, 4, :], bn[:, 3, :], bmv[:, :, 0], ALU.mult).then_inc(s_bn, 1)
                dve.wait_ge(s_bn, 4)
                nc.vector.tensor_tensor(bn[:, 4, :], beta[:], bn[:, 4, :], ALU.subtract).then_inc(s_bn, 1)
                dve.wait_ge(s_bn, 5)
                dve.sem_inc(s_free, 1)
                dve.sem_inc(s_y, 1)
                with dve.Fori(0, IT) as it:
                    dve.wait_ge(s_ld, (it + 1) * 16)
                    for u in range(NB):
                        n = it * NB + u
                        for c in range(2):
                            nc.vector.tensor_scalar(hb[:, c, :], hT[:, c, ds(n * P, P)], bn[:, 3, c:c + 1],
                                                    bn[:, 4, c:c + 1], ALU.mult, ALU.add).then_inc(s_hb, 1)
                        dve.wait_ge(s_b, n * 2 + 2)
                        nc.vector.scalar_tensor_tensor(y[:, u, :], x[:, u, :], 2.0, ps_b[:, 0:H], ALU.mult,
                                                       ALU.add).then_inc(s_y, 1)
                    dve.wait_ge(s_y, (it + 1) * NB + 1)
                    dve.sem_inc(s_free, 1)
                    dve.wait_ge(s_yfree, it + 1)
                    dve.wait_ge(s_hs, it * NB + 1)
                    dve.sem_inc(s_go, 1)
                    nc.vector.tensor_copy(dcol[:], dinv[:, ds(it * NB, NB)]).then_inc(s_dc, 1)
                    stats_from(nc, dve, y, yhat, stats, mv, rstd, s_stats, s_var, s_sqrt, s_rinv, s_norm, s_go, it, nb)

            @block.gpsimd
            def _(pool):
                pool.sem_inc(s_yfree, 1)
                with pool.Fori(0, IT) as it:
                    pool.wait_ge(s_norm, (it + 1) * NB)
                    pool.sem_inc(s_go, 1)
                    pool.dma_start(tiles(x2_tab)[:, ds(it * NB, NB), :], yhat[:]).then_inc(s_st, 16)
                    pool.wait_ge(s_hs, (it + 1) * NB + 1)
                    pool.sem_inc(s_go, 1)
                    pool.dma_start(tiles(hs_tab)[:, ds(it * NB, NB), :], hs[:]).then_inc(s_st, 16)
                    pool.wait_ge(s_st, (it + 1) * 32)
                    pool.sem_inc(s_yfree, 1)


def stats_from(nc, dve, y, yhat, stats, mv, rstd, s_stats, s_var, s_sqrt, s_rinv, s_norm, s_go, it, before):
    for u in range(NB):
        nc.vector.bn_stats(stats[:, u, :], y[:, u, :]).then_inc(s_stats, 1)
    dve.wait_ge(s_stats, (it + 1) * 2 * NB - NB + before)
    dve.sem_inc(s_go, 1)
    for u in range(NB):
        nc.vector.bn_aggr(mv[:, u, :], stats[:, u, :]).then_inc(s_stats, 1)
    dve.wait_ge(s_stats, (it + 1) * 2 * NB + before)
    nc.vector.tensor_scalar(rstd[:, 0, :], mv[:, :, 1], LN_EPS, None, ALU.add).then_inc(s_var, 1)
    dve.wait_ge(s_sqrt, it + 1)
    nc.vector.reciprocal(rstd[:, 2, :], rstd[:, 1, :]).then_inc(s_rinv, 1)
    dve.wait_ge(s_rinv, it + 1)
    for u in range(NB):
        nc.vector.tensor_scalar(yhat[:, u, :], y[:, u, :], mv[:, u, 0:1], rstd[:, 2, u:u + 1],
                                ALU.subtract, ALU.mult).then_inc(s_norm, 1)
    dve.wait_ge(s_norm, (it + 1) * NB)
    dve.sem_inc(s_go, 1)


def node_after2(nc, A, ident, ones_row, tiles, acc2, hs_tab, x2_tab, x3_tab, xr_tab, el_tab, el_res, dinv):
    IT = NT // NB
    WC = DOUT + 2 * HEADS
    with Phase(nc, "n2") as ph:
        w = ph.sb("w", [P, 2, WC])
        wT = ph.sb("wT", [DOUT, 2, P])
        wlr = ph.sb("wlr", [DOUT, 2 * HEADS])
        bias = ph.sb("bias", [P, H])
        dcol = ph.sb("dcol", [P, NB])
        x = ph.sb("x", [P, 3, NB, H])
        t = ph.sb("t", [P, 3, NB, H])
        y = ph.sb("y", [P, NB, H])
        yhat = ph.sb("yhat", [P, NB, H])
        xT = ph.sb("xT", [P, 2, P])
        xr = ph.sb("xr", [P, NB, WC])
        stats = ph.sb("stats", [P, NB, 6])
        mv = ph.sb("mv", [P, NB, 2])
        rstd = ph.sb("rstd", [P, 3, NB])
        ps_w = ph.ps("ps_w", [P, 512])
        ps_t = ph.ps("ps_t", [P, 512])
        ps_y = ph.ps("ps_y", [P, 512])
        (s_w, s_ld, s_free, s_stats, s_var, s_sqrt, s_rinv, s_norm, s_t, s_xT, s_e, s_ys, s_go, s_st,
         s_yfree, s_wp, s_wc, s_xr) = (
            ph.sem(n) for n in ("w", "ld", "free", "stats", "var", "sqrt", "rinv", "norm", "t", "xT", "e",
                                "ys", "go", "st", "yfree", "wp", "wc", "xr"))
        block = ph.block()

        @block.sync
        def _(sp):
            sp.dma_start(w[:, :, 0:DOUT], A["W3"].rearrange("(c p) n -> p c n", p=P)).then_inc(s_w, 16)
            sp.dma_start(wT[:], A["W3T"].rearrange("k (c n) -> k c n", c=2)).then_inc(s_w, 16)
            sp.dma_start(wlr[:, 0:HEADS], A["WrT"]).then_inc(s_w, 16)
            sp.dma_start(wlr[:, HEADS:], A["WlT"]).then_inc(s_w, 16)
            sp.dma_start(bias[:], bcast_rows(A["b2"], P)).then_inc(s_w, 16)
            with sp.Fori(0, IT) as it:
                sp.wait_ge(s_free, it + 1)
                for k, tab in enumerate((acc2, hs_tab, x2_tab)):
                    sp.dma_start(x[:, k], tiles(tab)[:, ds(it * NB, NB), :]).then_inc(s_ld, 16)

        @block.tensor
        def _(pe):
            pe.wait_ge(s_w, 80)
            for c in range(2):
                nc.tensor.matmul(ps_w[:, c * 8:c * 8 + 8], wT[:, c, :], wlr[:], start=True, stop=True).then_inc(s_wp, 1)
            pe.wait_ge(s_wc, 1)
            pe.sem_inc(s_go, 1)
            with pe.Fori(0, IT) as it:
                for u in range(NB):
                    n = it * NB + u
                    pe.wait_ge(s_norm, n + 1)
                    for c in range(2):
                        nc.tensor.transpose(ps_t[:, c * P:(c + 1) * P], yhat[:, u, c * P:(c + 1) * P],
                                            ident[:]).then_inc(s_t, 1)
                    pe.wait_ge(s_xT, n + 1)
                    pe.wait_ge(s_xr, n + 1)
                    nc.tensor.matmul(ps_y[:, 0:WC], xT[:, 0, :], w[:, 0, :], start=True, stop=False)
                    nc.tensor.matmul(ps_y[:, 0:WC], xT[:, 1, :], w[:, 1, :], start=False, stop=True).then_inc(s_ys, 1)

        @block.scalar
        def _(act):
            act.wait_ge(s_wp, 2)
            nc.scalar.activation(w[:, :, DOUT:WC], ps_w[:, 0:16].rearrange("p (c n) -> p c n", c=2),
                                 ACT.Copy).then_inc(s_wc, 1)
            act.sem_inc(s_xr, 1)
            with act.Fori(0, IT) as it:
                layernorm_root(nc, act, rstd, s_var, s_sqrt, it)
                act.wait_ge(s_yfree, it + 1)
                act.sem_inc(s_go, 1)
                for u in range(NB):
                    n = it * NB + u
                    act.wait_ge(s_t, n * 2 + 2)
                    nc.scalar.activation(xT[:].rearrange("p a b -> p (a b)"), ps_t[:, 0:2 * P], ACT.Copy).then_inc(s_xT, 1)
                    act.wait_ge(s_ys, n + 1)
                    nc.scalar.activation(el_res[:, ds(n, 1), :], ps_y[:, None, XR:WC], ACT.Copy)
                    nc.scalar.activation(xr[:, u, :], ps_y[:, 0:WC], ACT.Copy).then_inc(s_xr, 1)

        @block.vector
        def _(dve):
            dve.sem_inc(s_free, 1)
            S = 3 + NB
            with dve.Fori(0, IT) as it:
                dve.wait_ge(s_ld, (it + 1) * 48)
                nc.vector.tensor_tensor(t[:, 0], x[:, 0], x[:, 1], ALU.add)
                nc.vector.tensor_copy(dcol[:], dinv[:, ds(it * NB, NB)]).then_inc(s_e, 1)
                dve.wait_ge(s_e, it * S + 1)
                for u in range(NB):
                    nc.vector.scalar_tensor_tensor(t[:, 1, u, :], t[:, 0, u, :], dcol[:, u:u + 1], bias[:], ALU.mult,
                                                   ALU.add).then_inc(s_e, 1)
                dve.wait_ge(s_e, it * S + 1 + NB)
                nc.vector.scalar_tensor_tensor(t[:, 2], t[:, 1], 0.2, t[:, 1], ALU.mult, ALU.max).then_inc(s_e, 1)
                dve.wait_ge(s_e, it * S + 2 + NB)
                nc.vector.tensor_tensor(y[:], t[:, 2], x[:, 2], ALU.add).then_inc(s_e, 1)
                dve.wait_ge(s_e, it * S + S)
                dve.sem_inc(s_free, 1)
                dve.wait_ge(s_yfree, it + 1)
                layernorm_batch(nc, dve, y, yhat, stats, mv, rstd, s_stats, s_var, s_sqrt, s_rinv, s_norm, s_go, it)

        @block.gpsimd
        def _(pool):
            pool.sem_inc(s_yfree, 1)
            with pool.Fori(0, IT) as it:
                pool.wait_ge(s_norm, (it + 1) * NB)
                pool.sem_inc(s_go, 1)
                pool.dma_start(tiles(x3_tab)[:, ds(it * NB, NB), :], yhat[:]).then_inc(s_st, 16)
                pool.wait_ge(s_xr, (it + 1) * NB + 1)
                pool.sem_inc(s_go, 1)
                pool.dma_start(tiles(xr_tab)[:, ds(it * NB, NB), :], xr[:, :, 0:XR]).then_inc(s_st, 16)
                pool.dma_start(tiles(el_tab)[:, ds(it * NB, NB), :], xr[:, :, XR:WC]).then_inc(s_st, 16)
                pool.wait_ge(s_st, (it + 1) * 48)
                pool.sem_inc(s_yfree, 1)


def node_after3(nc, A, tiles, acc3, x3_tab, out):
    IT = NT // NB
    HD = HEADS * DOUT
    with Phase(nc, "n3") as ph:
        bias = ph.sb("bias", [P, HD])
        part = ph.sb("part", [P, KACC, NB, PAY])
        x = ph.sb("x", [P, NB, H])
        den = ph.sb("den", [P, 2, NB, HEADS])
        z = ph.sb("z", [P, NB, HD])
        neg = ph.sb("neg", [P, NB, HD])
        ex = ph.sb("ex", [P, NB, HD])
        pos = ph.sb("pos", [P, NB, HD])
        y = ph.sb("y", [P, NB, H])
        yhat = ph.sb("yhat", [P, NB, H])
        stats = ph.sb("stats", [P, NB, 6])
        mv = ph.sb("mv", [P, NB, 2])
        rstd = ph.sb("rstd", [P, 3, NB])
        (s_w, s_ld, s_free, s_stats, s_var, s_sqrt, s_rinv, s_norm, s_e, s_neg, s_ex, s_go, s_st,
         s_yfree) = (
            ph.sem(n) for n in ("w", "ld", "free", "stats", "var", "sqrt", "rinv", "norm", "e", "neg", "ex",
                                "go", "st", "yfree"))
        block = ph.block()

        @block.sync
        def _(sp):
            for hd in range(HEADS):
                sp.dma_start(bias[:, hd * DOUT:(hd + 1) * DOUT], bcast_rows(A["b3"], P)).then_inc(s_w, 16)
            with sp.Fori(0, IT) as it:
                sp.wait_ge(s_free, it + 1)
                for k in range(KACC):
                    sp.dma_start(part[:, k], tiles(acc3[k])[:, ds(it * NB, NB), :]).then_inc(s_ld, 16)
                sp.dma_start(x[:], tiles(x3_tab)[:, ds(it * NB, NB), :]).then_inc(s_ld, 16)

        @block.scalar
        def _(act):
            with act.Fori(0, IT) as it:
                act.wait_ge(s_neg, it + 1)
                nc.scalar.activation(ex[:], neg[:], ACT.Exp).then_inc(s_ex, 1)
                layernorm_root(nc, act, rstd, s_var, s_sqrt, it)

        @block.vector
        def _(dve):
            dve.sem_inc(s_free, 1)
            dve.wait_ge(s_w, 64)
            nc.vector.memset(rstd[:], 0.0)
            S = 5 + NB * HEADS + 2 + 1
            with dve.Fori(0, IT) as it:
                e = it * S
                dve.wait_ge(s_ld, (it + 1) * 16 * (KACC + 1))
                nc.vector.tensor_tensor(part[:, 0], part[:, 0], part[:, 1], ALU.add).then_inc(s_e, 1)
                nc.vector.tensor_tensor(part[:, 2], part[:, 2], part[:, 3], ALU.add).then_inc(s_e, 1)
                dve.wait_ge(s_e, e + 2)
                nc.vector.tensor_tensor(part[:, 0], part[:, 0], part[:, 2], ALU.add).then_inc(s_e, 1)
                dve.wait_ge(s_e, e + 3)
                nc.vector.tensor_scalar(den[:, 0], part[:, 0, :, HD:PAY], 1e-12, None, ALU.max).then_inc(s_e, 1)
                dve.wait_ge(s_e, e + 4)
                nc.vector.reciprocal(den[:, 1], den[:, 0]).then_inc(s_e, 1)
                dve.wait_ge(s_e, e + 5)
                for u in range(NB):
                    for hd in range(HEADS):
                        cc = slice(hd * DOUT, (hd + 1) * DOUT)
                        nc.vector.scalar_tensor_tensor(z[:, u, cc], part[:, 0, u, cc], den[:, 1, u, hd:hd + 1],
                                                       bias[:, cc], ALU.mult, ALU.add).then_inc(s_e, 1)
                dve.wait_ge(s_e, e + 5 + NB * HEADS)
                nc.vector.tensor_scalar(neg[:], z[:], 0.0, None, ALU.min).then_inc(s_neg, 1)
                nc.vector.scalar_tensor_tensor(pos[:], z[:], 0.0, x[:], ALU.max, ALU.add).then_inc(s_e, 1)
                dve.wait_ge(s_ex, it + 1)
                dve.wait_ge(s_e, e + 6 + NB * HEADS)
                nc.vector.scalar_tensor_tensor(y[:], ex[:], -1.0, pos[:], ALU.add, ALU.add).then_inc(s_e, 1)
                dve.wait_ge(s_e, e + 7 + NB * HEADS)
                dve.sem_inc(s_free, 1)
                dve.wait_ge(s_yfree, it + 1)
                nc.vector.tensor_scalar(y[:, 0, 0:1], y[:, 0, 0:1], 0.0, None, ALU.add).then_inc(s_e, 1)
                dve.wait_ge(s_e, e + S)
                layernorm_batch(nc, dve, y, yhat, stats, mv, rstd, s_stats, s_var, s_sqrt, s_rinv, s_norm, s_go, it)

        store_batches(nc, block, [(tiles(out), yhat[:])], s_norm, NB, 0, s_go, s_st, s_yfree)


_INS = ["x", "src_cols", "src_rows", "dst_cols", "dst_rows", "ew_cols", "ea20T", "ea64T", "ln_g", "ln_b",
        "WqT", "bq", "WkT", "bk", "WvT", "bv", "WoT", "bo", "WdkT", "bdk", "WdvT", "bdv",
        "Wf1", "bf1", "Wf2", "bf2", "Wu1", "bu1", "Wu2", "bu2", "gamma", "beta", "W2", "b2",
        "W3", "W3T", "WlT", "WrT", "b3"]


def lay_out(i):
    a = {k: np.asarray(v) for k, v in i.items()}
    pad_n, pad_e = NP - N, EP - E

    def wide(m):
        return np.concatenate([m, np.zeros((R20P - R20, m.shape[1]), np.float32)])

    x = np.concatenate([a["x"], np.zeros((pad_n, H), np.float32)])
    spare = np.full((pad_e,), N, np.int32)
    src = np.concatenate([a["src"], spare])
    dst = np.concatenate([a["dst"], spare])
    ew = np.concatenate([a["edge_weight"], np.zeros((pad_e,), np.float32)])
    e20 = np.concatenate([a["edge_attr_20"], np.zeros((pad_e, R20), np.float32)])
    e64 = np.concatenate([a["edge_attr_64"], np.zeros((pad_e, R64), np.float32)])
    d = {"x": x, "src_cols": src.reshape(ET, P).T, "src_rows": src, "dst_cols": dst.reshape(ET, P).T,
         "dst_rows": dst, "ew_cols": ew.reshape(ET, P).T, "ea20T": wide(e20.T), "ea64T": e64.T,
         "ln_g": a["L0_gnn_ln_g"], "ln_b": a["L0_gnn_ln_b"]}
    for n in ("Wq", "Wk", "Wv", "Wo", "Wdk", "Wdv"):
        d[n + "T"] = a["L0_gnn_" + n].T
    for n in ("bq", "bk", "bv", "bo", "bdk", "bdv"):
        d[n] = a["L0_gnn_" + n]
    for n in ("Wf1", "bf1", "Wf2", "bf2", "Wu1", "bu1", "Wu2", "bu2", "gamma", "beta"):
        d[n] = a["L1_gnn_" + n]
    d["Wf1"] = wide(d["Wf1"])
    d["W2"], d["b2"] = a["L2_gnn_W"], a["L2_gnn_b"]
    d["W3"], d["W3T"], d["b3"] = a["L3_gnn_W"], a["L3_gnn_W"].T, a["L3_gnn_b"]
    d["WlT"], d["WrT"] = a["L3_gnn_Wl"].T, a["L3_gnn_Wr"].T
    return {k: np.ascontiguousarray(d[k]) for k in _INS}


def kernel(**inputs):
    import concourse.bacc as _bacc
    from concourse.bass_utils import run_bass_kernel_spmd as _run

    nc = _bacc.Bacc("TRN2", target_bir_lowering=False, num_devices=1)
    arrays, A = {}, {}
    for name, a in lay_out(inputs).items():
        arrays[f"in_{name}_dram"] = a
        A[name] = nc.dram_tensor(f"in_{name}_dram", a.shape, mybir.dt.from_np(a.dtype), kind="ExternalInput").ap()
    out = nc.dram_tensor("out_0_dram", (NP, H), F32, kind="ExternalOutput").ap()
    gnn_kernel(nc, A, out)
    r = _run(nc, [arrays], core_ids=[0])
    return r.results[0]["out_0_dram"][:N]
```

```python
import numpy as np
import concourse.bass as bass
from concourse import mybir
from contextlib import ExitStack

F32 = mybir.dt.float32
F32R = mybir.dt.float32r
I32 = mybir.dt.int32
BF16 = mybir.dt.bfloat16
ALU = mybir.AluOpType
ACT = mybir.ActivationFunctionType
AX = mybir.AxisListType

P = 128
N = 6250
E = 106250
H = 256
R64 = 64
R20 = 20
R20P = 32
B2R = 2 * R20P + 1
HEADS = 4
DOUT = 64
XR = DOUT + HEADS
PAY = HEADS * DOUT + HEADS
NT = -(-N // P) + 1
NP = NT * P
TRASH = NP - P
ET = 832
EP = ET * P
G = 8
NG = ET // G
NB = 5
KACC = 4
K3 = 8
ZROWS = -(-NP // (NG // 4))
ZROWS += -ZROWS % P
LN_EPS = 1e-5
TWO_PI = 2.0 * np.pi
ROUND = 12582912.0
ds = bass.ds


def bcast_rows(ap, n):
    return ap.partition_broadcast(n)


class Phase:

    def __init__(self, nc, name):
        self.nc, self.name, self.ctx, self.used = nc, name, ExitStack(), []

    def __enter__(self):
        self.ctx.__enter__()
        return self

    def __exit__(self, *a):
        r = self.ctx.__exit__(*a)
        if self.used:
            self.nc.clear_and_free_semaphores(self.used)
            self.nc.all_engine_barrier()
        return r

    def sb(self, name, shape, dt=F32):
        return self.ctx.enter_context(self.nc.sbuf_tensor(f"{self.name}_{name}", shape, dt))

    def ps(self, name, shape, dt=F32):
        return self.ctx.enter_context(self.nc.psum_tensor(f"{self.name}_{name}", shape, dt))

    def sem(self, name):
        self.used.append(self.nc.alloc_semaphore(f"{self.name}_{name}"))
        return self.used[-1]

    def sems(self, name, n):
        return [self.sem(f"{name}{i}") for i in range(n)]

    def block(self):
        return self.ctx.enter_context(self.nc.Block())


def layernorm_batch(nc, dve, x, xhat, stats, mv, rstd, s_stats, s_var, s_sqrt, s_rinv, s_norm, s_go, it):
    for u in range(NB):
        nc.vector.bn_stats(stats[:, u, :], x[:, u, :]).then_inc(s_stats, 1)
    dve.wait_ge(s_stats, (it + 1) * 2 * NB - NB)
    dve.sem_inc(s_go, 1)
    for u in range(NB):
        nc.vector.bn_aggr(mv[:, u, :], stats[:, u, :]).then_inc(s_stats, 1)
    dve.wait_ge(s_stats, (it + 1) * 2 * NB)
    nc.vector.tensor_scalar(rstd[:, 0, :], mv[:, :, 1], LN_EPS, None, ALU.add).then_inc(s_var, 1)
    dve.wait_ge(s_sqrt, it + 1)
    nc.vector.reciprocal(rstd[:, 2, :], rstd[:, 1, :]).then_inc(s_rinv, 1)
    dve.wait_ge(s_rinv, it + 1)
    for u in range(NB):
        nc.vector.tensor_scalar(xhat[:, u, :], x[:, u, :], mv[:, u, 0:1], rstd[:, 2, u:u + 1],
                                ALU.subtract, ALU.mult).then_inc(s_norm, 1)
    dve.wait_ge(s_norm, (it + 1) * NB)
    dve.sem_inc(s_go, 1)


def layernorm_root(nc, act, rstd, s_var, s_sqrt, it):
    act.wait_ge(s_var, it + 1)
    nc.scalar.activation(rstd[:, 1, :], rstd[:, 0, :], ACT.Sqrt).then_inc(s_sqrt, 1)


def both_slots(eng, step):
    pairs = NT // NB // 2
    with eng.Fori(0, pairs - 1) as b:
        step(b * 2, b, 0, False)
        step(b * 2 + 1, b, 1, False)
    step(pairs * 2 - 2, pairs - 1, 0, False)
    step(pairs * 2 - 1, pairs - 1, 1, True)


def next_tile(it, h, u):
    return (it, h, u + 1) if u < NB - 1 else (it + 1, 1 - h, 0)


class Tables:
    pass


def gnn_kernel(nc, A, out):
    ctx = ExitStack()
    with ctx, nc.allow_non_contiguous_dma(reason="small tables of weights and indices"):
        def dram(name, shape, dt=F32):
            return nc.dram_tensor(name, shape, dt, kind="Internal").ap()

        def keep(name, shape, dt=F32):
            return ctx.enter_context(nc.sbuf_tensor(name, shape, dt))

        T = Tables()
        T.q_tab = dram("q_tab", [NP, H])
        T.qs_tab = dram("qs_tab", [NP, 2 * H])
        T.kv_tab = dram("kv_tab", [NP, 2 * H])
        T.x1_tab = dram("x1_tab", [NP, H])
        T.x1s_tab = dram("x1s_tab", [NP, 2 * H])
        T.x2_tab = dram("x2_tab", [NP, H])
        T.x3_tab = dram("x3_tab", [NP, H])
        T.hs_tab = dram("hs_tab", [NP, H])
        T.xr_tab = dram("xr_tab", [NP, XR])
        T.el_tab = dram("el_tab", [NP, HEADS])
        T.src_rows = dram("srcf_rows", [EP])
        T.dst_rows = dram("dstf_rows", [EP])
        T.lo_rows = dram("lof_rows", [EP])
        T.srcu_cols = dram("srcu_cols", [P, ET], I32)
        T.dstu_cols = dram("dstu_cols", [P, ET], I32)
        T.acc0 = dram("acc0", [NP, H + 1])
        T.acc1 = [dram(f"acc1_{k}", [NP, H]) for k in range(KACC)]
        T.acc2 = dram("acc2", [NP, H])
        T.acc3 = [dram(f"acc3_{k}", [ZROWS * (NG // 4), PAY]) for k in range(K3)]

        def tiles(ap):
            return ap.rearrange("(t p) d -> p t d", p=P)

        T.ident = keep("ident", [P, P])
        T.iota_row = keep("iota_row", [P, P])
        T.iota_col = keep("iota_col", [P, 1])
        T.iota_hi = keep("iota_hi", [P, NT, HEADS])
        T.earlier = keep("earlier", [P, P])
        T.trash = keep("trash", [P, 1])
        T.src_f = keep("src_f", [P, ET])
        T.dst_f = keep("dst_f", [P, ET])
        T.off_f = keep("off_f", [P, ET])
        T.hi_f = keep("hi_f", [P, ET])
        T.window = keep("window", [P, NG])
        T.base = keep("base", [1, NG], I32)
        T.far = keep("far", [1, 1], I32)
        T.cut = keep("cut", [P, ET])
        T.deg = keep("deg", [P, NT])
        T.dinv = keep("dinv", [P, NT])
        T.ones_row = keep("ones_row", [1, P])
        T.zeros = keep("zeros", [P, PAY])
        T.el_res = keep("el_res", [P, NT, HEADS])

        edge_indices(nc, A, T)
        edge_indices_far(nc, A, T)
        node_qkv(nc, A, T.ident, tiles, T.q_tab, T.qs_tab, T.kv_tab, T.zeros,
                 [T.acc0, *T.acc1, T.acc2])
        edge_layer0(nc, A, T)
        node_after0(nc, A, T.ident, T.ones_row, tiles, T.acc0, T.x1_tab, T.x1s_tab, T.deg)
        edge_layer1(nc, A, T)
        node_after1(nc, A, T.ident, tiles, T.acc1, T.x1_tab, T.x2_tab, T.hs_tab, T.deg, T.dinv)
        edge_layer2(nc, A, T)
        node_after2(nc, A, T.ident, tiles, T.acc2, T.hs_tab, T.x2_tab, T.x3_tab, T.xr_tab,
                    T.el_tab, T.el_res, T.dinv)
        edge_layer3(nc, A, T)
        node_after3(nc, T, tiles, A["b3"], out)


def if_near(eng, T, near, far):
    outside = eng.value_load(T.far[0:1, 0:1], min_val=0, max_val=EP)
    with eng.If(outside < 1):
        near()
    with eng.Else():
        far()


def if_far(eng, T, far):
    outside = eng.value_load(T.far[0:1, 0:1], min_val=0, max_val=EP)
    with eng.If(outside >= 1):
        far()


def edge_indices(nc, A, T):
    with Phase(nc, "ix") as ph:
        src_i = ph.sb("src_i", [P, ET], I32)
        dst_i = ph.sb("dst_i", [P, ET], I32)
        row_i = ph.sb("row_i", [P, 2, ET], I32)
        hi_i = ph.sb("hi_i", [P, ET], I32)
        lo_i = ph.sb("lo_i", [P, ET], I32)
        row_f = ph.sb("row_f", [P, 3, ET])
        ew = ph.sb("ew", [P, ET])
        turn = ph.sb("turn", [P, ET])
        turn_r = ph.sb("turn_r", [P, ET])
        inside = ph.sb("inside", [P, ET])
        half_pi = ph.sb("half_pi", [P, 1])
        first = ph.sb("first", [P, P])
        ones = ph.sb("ones", [P, P])
        beyond = ph.sb("beyond", [P, 2, ET])
        count = ph.sb("count", [P, 2])
        ps_base = ph.ps("ps_base", [P, NG])
        ps_far = ph.ps("ps_far", [P, 2])
        (s_in, s_const, s_f, s_bits, s_rowf, s_turn, s_sin, s_base, s_win, s_off, s_beyond, s_far, s_flag,
         s_out) = (ph.sem(n) for n in ("in", "const", "f", "bits", "rowf", "turn", "sin", "base", "win", "off",
                                       "beyond", "far", "flag", "out"))
        block = ph.block()

        @block.sync
        def _(sp):
            sp.dma_start(src_i[:], A["src_cols"]).then_inc(s_in, 16)
            sp.dma_start(dst_i[:], A["dst_cols"]).then_inc(s_in, 16)
            sp.dma_start(ew[:], A["ew_cols"]).then_inc(s_in, 16)
            sp.dma_start(row_i[:, 0, :], A["src_rows"].rearrange("(p k) -> p k", p=P)).then_inc(s_in, 16)
            sp.dma_start(row_i[:, 1, :], A["dst_rows"].rearrange("(p k) -> p k", p=P)).then_inc(s_in, 16)
            sp.wait_ge(s_rowf, 3)
            for k, tab in enumerate((T.src_rows, T.dst_rows, T.lo_rows)):
                sp.dma_start(tab.rearrange("(p k) -> p k", p=P), row_f[:, k, :]).then_inc(s_out, 16)
            sp.wait_ge(s_out, 48)

        @block.gpsimd
        def _(pool):
            nc.gpsimd.memset(T.ident[:], 0.0).then_inc(s_const, 1)
            nc.gpsimd.memset(T.earlier[:], 1.0).then_inc(s_const, 1)
            nc.gpsimd.memset(ones[:], 1.0).then_inc(s_const, 1)
            nc.gpsimd.memset(first[:], 0.0).then_inc(s_const, 1)
            pool.wait_ge(s_const, 4)
            nc.gpsimd.affine_select(out=T.ident[:], in_=T.ident[:], compare_op=ALU.not_equal, fill=1.0, base=0,
                                    pattern=[[-1, P]], channel_multiplier=1).then_inc(s_const, 1)
            nc.gpsimd.affine_select(out=T.earlier[:], in_=T.earlier[:], compare_op=ALU.is_ge, fill=0.0, base=0,
                                    pattern=[[-1, P]], channel_multiplier=1).then_inc(s_const, 1)
            nc.gpsimd.memset(first[0:1, :], 1.0).then_inc(s_const, 1)
            nc.gpsimd.iota(T.iota_row[:], [[1, P]], base=0, channel_multiplier=0,
                           allow_small_or_imprecise_dtypes=True).then_inc(s_const, 1)
            nc.gpsimd.iota(T.iota_col[:], [[1, 1]], base=0, channel_multiplier=1,
                           allow_small_or_imprecise_dtypes=True).then_inc(s_const, 1)
            nc.gpsimd.iota(T.iota_hi[:], [[1, NT], [0, HEADS]], base=0, channel_multiplier=0,
                           allow_small_or_imprecise_dtypes=True).then_inc(s_const, 1)
            nc.gpsimd.iota(T.trash[:], [[1, 1]], base=TRASH, channel_multiplier=1,
                           allow_small_or_imprecise_dtypes=True).then_inc(s_const, 1)

        @block.scalar
        def _(act):
            act.wait_ge(s_turn, 4)
            nc.scalar.activation(T.cut[:], turn_r[:], ACT.Sin, bias=half_pi[:], scale=-TWO_PI).then_inc(s_sin, 1)

        @block.tensor
        def _(pe):
            pe.wait_ge(s_const, 11)
            pe.wait_ge(s_f, 1)
            nc.tensor.matmul(ps_base[:], first[:], T.dst_f[:].rearrange("p (g u) -> p g u", u=G)[:, :, 0],
                             start=True, stop=True).then_inc(s_base, 1)
            pe.wait_ge(s_far, 2)
            nc.tensor.matmul(ps_far[:], ones[:], count[:], start=True, stop=True).then_inc(s_flag, 1)

        @block.vector
        def _(dve):
            nc.vector.memset(half_pi[:], np.pi / 2)
            nc.vector.memset(T.zeros[:], 0.0)
            nc.vector.memset(T.deg[:], 0.0)
            nc.vector.memset(T.ones_row[:], 1.0)
            dve.wait_ge(s_in, 80)
            nc.vector.tensor_copy(T.dst_f[:], dst_i[:]).then_inc(s_f, 1)
            nc.vector.tensor_copy(T.src_f[:], src_i[:])
            nc.vector.tensor_scalar(hi_i[:], src_i[:], 7, None, ALU.logical_shift_right)
            nc.vector.tensor_scalar(lo_i[:], row_i[:, 0, :], P - 1, None, ALU.bitwise_and).then_inc(s_bits, 1)
            nc.vector.tensor_copy(row_f[:, 0, :], row_i[:, 0, :]).then_inc(s_rowf, 1)
            nc.vector.tensor_copy(row_f[:, 1, :], row_i[:, 1, :]).then_inc(s_rowf, 1)
            nc.vector.tensor_scalar(turn[:], ew[:], 0.1, None, ALU.mult).then_inc(s_turn, 1)
            dve.wait_ge(s_bits, 1)
            nc.vector.tensor_copy(T.hi_f[:], hi_i[:])
            nc.vector.tensor_copy(row_f[:, 2, :], lo_i[:]).then_inc(s_rowf, 1)
            dve.wait_ge(s_turn, 1)
            nc.vector.tensor_scalar(turn_r[:], turn[:], ROUND, ROUND, ALU.add, ALU.subtract).then_inc(s_turn, 1)
            dve.wait_ge(s_turn, 2)
            nc.vector.tensor_tensor(turn[:], turn[:], turn_r[:], ALU.subtract).then_inc(s_turn, 1)
            dve.wait_ge(s_turn, 3)
            nc.vector.scalar_tensor_tensor(turn_r[:], turn[:], -1.0, turn[:], ALU.mult, ALU.max).then_inc(s_turn, 1)
            nc.vector.tensor_scalar(inside[:], ew[:], 5.0, 0.5, ALU.is_lt, ALU.mult).then_inc(s_turn, 1)
            dve.wait_ge(s_base, 1)
            dve.wait_ge(s_const, 11)
            nc.vector.tensor_scalar(T.window[:], ps_base[:], T.iota_col[:], None, ALU.add).then_inc(s_win, 1)
            nc.vector.tensor_copy(T.base[:], ps_base[0:1, :]).then_inc(s_win, 1)
            dst_g = T.dst_f[:].rearrange("p (g u) -> p g u", u=G)
            nc.vector.tensor_tensor(T.off_f[:].rearrange("p (g u) -> p g u", u=G), dst_g,
                                    ps_base[:, :, None].to_broadcast([P, NG, G]), ALU.subtract).then_inc(s_off, 1)
            dve.wait_ge(s_off, 1)
            nc.vector.tensor_scalar(beyond[:, 0, :], T.off_f[:], 0.0, None, ALU.is_lt).then_inc(s_beyond, 1)
            nc.vector.tensor_scalar(beyond[:, 1, :], T.off_f[:], float(P - 1), None, ALU.is_gt).then_inc(s_beyond, 1)
            dve.wait_ge(s_beyond, 2)
            for k in range(2):
                nc.vector.reduce_sum(count[:, k:k + 1], beyond[:, k, :], axis=AX.X).then_inc(s_far, 1)
            dve.wait_ge(s_sin, 1)
            dve.wait_ge(s_turn, 5)
            nc.vector.scalar_tensor_tensor(T.cut[:], T.cut[:], 1.0, inside[:], ALU.add, ALU.mult).then_inc(s_turn, 1)
            dve.wait_ge(s_flag, 1)
            nc.vector.reduce_sum(count[0:1, 0:1], ps_far[0:1, :], axis=AX.X).then_inc(s_flag, 1)
            dve.wait_ge(s_flag, 2)
            nc.vector.tensor_copy(T.far[:], count[0:1, 0:1])


def edge_indices_far(nc, A, T):
    with Phase(nc, "fx") as ph:
        dst_i = ph.sb("dst_i", [P, ET], I32)
        hi_i = ph.sb("hi_i", [P, ET], I32)
        lo_i = ph.sb("lo_i", [P, ET], I32)
        hi_f = ph.sb("hi_f", [P, ET])
        lo_f = ph.sb("lo_f", [P, ET])
        again = [ph.sb("again_s", [P, ET]), ph.sb("again_d", [P, ET])]
        room = [ph.sb("room_s", [P, ET]), ph.sb("room_d", [P, ET])]
        uniq = [ph.sb("uniq_s", [P, ET], I32), ph.sb("uniq_d", [P, ET], I32)]
        rows = [ph.sb("rows_s", [P, G, P]), ph.sb("rows_d", [P, G, P])]
        cols = ph.sb("cols", [P, 4, G])
        same = ph.sb("same", [P, 2, G, P], BF16)
        count = ph.sb("count", [P, 2, G])
        hot_lo = ph.sb("hot_lo", [P, G, P], BF16)
        hot_hi = ph.sb("hot_hi", [P, G, NT], BF16)
        none = ph.sb("none", [P, P], BF16)
        ps_deg = ph.ps("ps_deg", [P, NT])
        (s_in, s_split, s_rows, s_read, s_cols, s_same, s_count, s_hot, s_deg, s_uniq, s_out) = (
            ph.sem(n) for n in ("in", "split", "rows", "read", "cols", "same", "count", "hot", "deg", "uniq", "out"))
        block = ph.block()

        @block.sync
        def _(sp):
            def far():
                sp.dma_start(dst_i[:], A["dst_cols"]).then_inc(s_in, 16)
                with sp.Fori(0, NG) as g:
                    sp.wait_ge(s_read, g + 1)
                    for k, tab in enumerate((T.src_rows, T.dst_rows)):
                        sp.dma_start(rows[k][:].rearrange("p u f -> p (u f)"),
                                     bcast_rows(tab[ds(g * G * P, G * P)], P)).then_inc(s_rows, 16)
                sp.wait_ge(s_uniq, 6)
                sp.dma_start(T.srcu_cols, uniq[0][:]).then_inc(s_out, 16)
                sp.dma_start(T.dstu_cols, uniq[1][:]).then_inc(s_out, 16)
                sp.wait_ge(s_out, 32)
                sp.sem_inc(s_in, 1)
            if_far(sp, T, far)

        @block.tensor
        def _(pe):
            def far():
                pe.wait_ge(s_split, 1)
                nc.tensor.matmul(ps_deg[:], none[:], none[:, 0:NT], start=True, stop=False,
                                 skip_group_check=True).then_inc(s_deg, 1)
                with pe.Fori(0, NG) as g:
                    for u in range(G):
                        pe.wait_ge(s_hot, g * G + u + 1)
                        nc.tensor.matmul(ps_deg[:], hot_lo[:, u, :], hot_hi[:, u, :], start=False, stop=False,
                                         skip_group_check=True).then_inc(s_deg, 1)
            if_far(pe, T, far)

        @block.vector
        def _(dve):
            def far():
                nc.vector.memset(none[:], 0.0).then_inc(s_split, 1)
                dve.wait_ge(s_in, 16)
                nc.vector.tensor_scalar(hi_i[:], dst_i[:], 7, None, ALU.logical_shift_right)
                nc.vector.tensor_scalar(lo_i[:], dst_i[:], P - 1, None, ALU.bitwise_and).then_inc(s_split, 1)
                dve.wait_ge(s_split, 2)
                nc.vector.tensor_copy(hi_f[:], hi_i[:])
                nc.vector.tensor_copy(lo_f[:], lo_i[:]).then_inc(s_split, 1)
                dve.wait_ge(s_split, 3)
                dve.sem_inc(s_read, 1)
                with dve.Fori(0, NG) as g:
                    for k, col in enumerate((T.src_f, T.dst_f, lo_f, hi_f)):
                        nc.vector.tensor_copy(cols[:, k, :], col[:, ds(g * G, G)]).then_inc(s_cols, 1)
                    dve.wait_ge(s_rows, (g + 1) * 32)
                    dve.wait_ge(s_cols, (g + 1) * 4)
                    for k in range(2):
                        for u in range(G):
                            nc.vector.scalar_tensor_tensor(same[:, k, u, :], rows[k][:, u, :], cols[:, k, u:u + 1],
                                                           T.earlier[:], ALU.is_equal, ALU.mult,
                                                           accum_out=count[:, k, u:u + 1]).then_inc(s_same, 1)
                    dve.wait_ge(s_same, (g + 1) * 2 * G)
                    for k in range(2):
                        nc.vector.tensor_scalar(again[k][:, ds(g * G, G)], count[:, k, :], 2.0, -1.0,
                                                ALU.min, ALU.add).then_inc(s_count, 1)
                    dve.sem_inc(s_read, 1)
                    dve.wait_ge(s_deg, g * G + 1)
                    for u in range(G):
                        nc.vector.tensor_scalar(hot_lo[:, u, :], T.iota_row[:], cols[:, 2, u:u + 1], None,
                                                ALU.is_equal)
                        nc.vector.tensor_scalar(hot_hi[:, u, :], T.iota_row[:, 0:NT], cols[:, 3, u:u + 1], None,
                                                ALU.is_equal).then_inc(s_hot, 1)
                    dve.wait_ge(s_hot, (g + 1) * G)
                    dve.wait_ge(s_count, (g + 1) * 2)
                    dve.sem_inc(s_in, 1)
                for k, col in enumerate((T.src_f, T.dst_f)):
                    nc.vector.tensor_scalar(room[k][:], col[:], T.trash[:], -1.0, ALU.subtract,
                                            ALU.mult).then_inc(s_uniq, 1)
                dve.wait_ge(s_uniq, 2)
                for k in range(2):
                    nc.vector.tensor_tensor(room[k][:], room[k][:], again[k][:], ALU.mult).then_inc(s_uniq, 1)
                dve.wait_ge(s_uniq, 4)
                for k, col in enumerate((T.src_f, T.dst_f)):
                    nc.vector.tensor_tensor(uniq[k][:], room[k][:], col[:], ALU.add).then_inc(s_uniq, 1)
                dve.wait_ge(s_deg, ET + 1)
                nc.vector.tensor_copy(T.deg[:], ps_deg[:])
            if_far(dve, T, far)


def node_qkv(nc, A, ident, tiles, q_tab, qs_tab, kv_tab, zeros, accs):
    IT = NT // NB
    with Phase(nc, "qkv") as ph:
        w = ph.sb("w", [P, 2, 3 * H])
        bias = ph.sb("bias", [P, 3 * H])
        gb = ph.sb("gb", [P, 2, 2])
        x = ph.sb("x", [P, 2, NB, H])
        xhat = ph.sb("xhat", [P, 2, NB, H])
        xT = ph.sb("xT", [P, 2, 2, P])
        y = ph.sb("y", [P, 2, NB, 3 * H])
        ys = ph.sb("ys", [P, 2, NB, 2, H], F32R)
        stats = ph.sb("stats", [P, NB, 6])
        mv = ph.sb("mv", [P, NB, 2])
        rstd = ph.sb("rstd", [P, 3, NB])
        ps_t = ph.ps("ps_t", [P, 2, 4, P])
        ps_y = ph.ps("ps_y", [P, 2, 1024])
        s_x = ph.sems("x", 2)
        (s_w, s_xfree, s_stats, s_var, s_sqrt, s_rinv, s_norm, s_t, s_xT, s_m, s_y, s_hi, s_lo, s_st, s_yfree, s_go,
         s_zero) = (ph.sem(n) for n in ("w", "xfree", "stats", "var", "sqrt", "rinv", "norm", "t", "xT", "m", "y",
                                        "hi", "lo", "st", "yfree", "go", "zero"))
        block = ph.block()

        @block.sync
        def _(sp):
            sp.dma_start(w[:, :, 0:H], A["WqT"].rearrange("(c p) n -> p c n", p=P)).then_inc(s_w, 16)
            sp.dma_start(w[:, :, H:2 * H], A["WkT"].rearrange("(c p) n -> p c n", p=P)).then_inc(s_w, 16)
            sp.dma_start(w[:, :, 2 * H:], A["WvT"].rearrange("(c p) n -> p c n", p=P)).then_inc(s_w, 16)
            for k, b in enumerate(("bq", "bk", "bv")):
                sp.dma_start(bias[:, k * H:(k + 1) * H], bcast_rows(A[b], P)).then_inc(s_w, 16)
            sp.dma_start(gb[:, 0, :], A["ln_g"].rearrange("(c p) -> p c", p=P)).then_inc(s_w, 16)
            sp.dma_start(gb[:, 1, :], A["ln_b"].rearrange("(c p) -> p c", p=P)).then_inc(s_w, 16)
            with sp.Fori(0, IT // 2) as b:
                for h in range(2):
                    it = b * 2 + h
                    sp.wait_ge(s_xfree, it + 1)
                    sp.dma_start(x[:, h, :, :], tiles(A["x"])[:, ds(it * NB, NB), :]).then_inc(s_x[h], 16)
                    for acc in accs:
                        d = acc.shape[1]
                        sp.dma_start(tiles(acc)[:, ds(it * NB, NB), :],
                                     zeros[:, None, 0:d].to_broadcast([P, NB, d])).then_inc(s_zero, 16)
            sp.wait_ge(s_zero, IT * len(accs) * 16)

        @block.vector
        def _(dve):
            dve.sem_inc(s_xfree, 2)
            dve.sem_inc(s_y, 2)
            dve.wait_ge(s_w, 16 * 8)

            def normalise(it, b, h):
                dve.wait_ge(s_x[h], (b + 1) * 16)
                dve.wait_ge(s_t, (it + 1) * 2 * NB)
                layernorm_batch(nc, dve, x[:, h], xhat[:, h], stats, mv, rstd,
                                s_stats, s_var, s_sqrt, s_rinv, s_norm, s_go, it)
                dve.sem_inc(s_xfree, 1)

            def low(it, h, u):
                dve.wait_ge(s_hi, it * NB + u + 1)
                nc.vector.tensor_tensor(ys[:, h, u, 1, :], y[:, h, u, 0:H], ys[:, h, u, 0, :],
                                        ALU.subtract).then_inc(s_lo, 1)

            def step(it, b, h, last):
                if not last:
                    normalise(it + 1, b + h, 1 - h)
                dve.wait_ge(s_yfree, it + 1)
                for u in range(NB):
                    dve.wait_ge(s_m, it * NB + u + 3)
                    nc.vector.tensor_tensor(y[:, h, u, :], ps_y[:, (h * NB + u) % 2, 0:3 * H], bias[:],
                                            ALU.add).then_inc(s_y, 1)
                    if u > 0:
                        low(it, h, u - 1)
                low(it, h, NB - 1)

            normalise(0, 0, 0)
            both_slots(dve, step)

        @block.tensor
        def _(pe):
            pe.sem_inc(s_t, 4 * NB)
            pe.sem_inc(s_m, 2)
            pe.wait_ge(s_w, 16 * 8)

            def turn(it, h, u):
                n = it * NB + u
                pe.wait_ge(s_norm, n + 1)
                pe.wait_ge(s_xT, n + 1)
                for c in range(2):
                    nc.tensor.transpose(ps_t[:, (h * NB + u) % 2, c, :], xhat[:, h, u, c * P:(c + 1) * P],
                                        ident[:]).then_inc(s_t, 1)

            def step(it, b, h, last):
                for u in range(NB):
                    n = it * NB + u
                    v = (h * NB + u) % 2
                    if u < NB - 1:
                        turn(it, h, u + 1)
                    elif not last:
                        turn(it + 1, 1 - h, 0)
                    pe.wait_ge(s_xT, n + 3)
                    pe.wait_ge(s_y, n + 1)
                    for a, z in ((0, 512), (512, 768)):
                        for c in range(2):
                            last_mm = nc.tensor.matmul(ps_y[:, v, a:z], xT[:, v, c, :], w[:, c, a:z],
                                                       start=(c == 0), stop=(c == 1))
                    last_mm.then_inc(s_m, 1)

            turn(0, 0, 0)
            both_slots(pe, step)

        @block.scalar
        def _(act):
            act.sem_inc(s_xT, 2)
            act.wait_ge(s_w, 16 * 8)

            def high(it, h, u):
                act.wait_ge(s_y, it * NB + u + 3)
                nc.scalar.activation(ys[:, h, u, 0, :], y[:, h, u, 0:H], ACT.Copy).then_inc(s_hi, 1)

            def step(it, b, h, last):
                if not last:
                    layernorm_root(nc, act, rstd, s_var, s_sqrt, it + 1)
                for u in range(NB):
                    n = it * NB + u
                    v = (h * NB + u) % 2
                    act.wait_ge(s_t, n * 2 + 2 + 4 * NB)
                    act.wait_ge(s_m, n + 1)
                    for c in range(2):
                        done = nc.scalar.activation(xT[:, v, c, :], ps_t[:, v, c, :], ACT.Identity,
                                                    bias=gb[:, 1, c:c + 1], scale=gb[:, 0, c:c + 1])
                    done.then_inc(s_xT, 1)
                    if u > 0:
                        high(it, h, u - 1)
                high(it, h, NB - 1)

            layernorm_root(nc, act, rstd, s_var, s_sqrt, 0)
            both_slots(act, step)

        @block.gpsimd
        def _(pool):
            pool.sem_inc(s_yfree, 2)
            with pool.Fori(0, IT // 2) as b:
                for h in range(2):
                    it = b * 2 + h
                    pool.wait_ge(s_y, (it + 1) * NB + 2)
                    pool.sem_inc(s_go, 1)
                    pool.dma_start(tiles(q_tab)[:, ds(it * NB, NB), :], y[:, h, :, 0:H]).then_inc(s_st, 16)
                    pool.dma_start(tiles(kv_tab)[:, ds(it * NB, NB), :], y[:, h, :, H:3 * H]).then_inc(s_st, 16)
                    pool.wait_ge(s_lo, (it + 1) * NB)
                    pool.sem_inc(s_go, 1)
                    pool.dma_start(tiles(qs_tab)[:, ds(it * NB, NB), :],
                                   ys[:, h].rearrange("p n a d -> p n (a d)").bitcast(F32)).then_inc(s_st, 16)
                    pool.wait_ge(s_st, (it + 1) * 48)
                    pool.sem_inc(s_yfree, 1)


def start_additions(pool, accs, zeros, s_add):
    for acc, s in zip(accs, s_add):
        pool.dma_start(acc[NP - 1:NP, :], zeros[0:1, 0:acc.shape[1]]).then_inc(s, 16)


def edge_layer0(nc, A, T):
    with Phase(nc, "e0") as ph:
        w = ph.sb("w", [R64 + 1, 2 * H])
        ea = ph.sb("ea", [R64 + 1, 2, G * P])
        rows = ph.sb("rows", [P, 2, G, P])
        isrc = ph.sb("isrc", [P, 2, G], I32)
        idst = ph.sb("idst", [P, 2, G], I32)
        iout = ph.sb("iout", [P, 2, G], I32)
        kv = ph.sb("kv", [P, G, 2 * H])
        q = ph.sb("q", [P, G, H])
        qk = ph.sb("qk", [P, 2, H])
        junk = ph.sb("junk", [P, G, H], BF16)
        vd = ph.sb("vd", [P, G, H])
        raw = ph.sb("raw", [P, G])
        att = ph.sb("att", [P, 2, G])
        cols = ph.sb("cols", [P, 2, G])
        same = ph.sb("same", [P, G, P])
        msg = ph.sb("msg", [P, 2, H + 1])
        ps_d = ph.ps("ps_d", [P, 2, 512])
        ps_m = ph.ps("ps_m", [P, 2, 512])
        s_w, s_one = ph.sem("w"), ph.sem("one")
        s_ld = ph.sems("ld", 2)
        s_ldfree = ph.sem("ldfree")
        s_ge = ph.sems("ge", G)
        s_gfree = ph.sem("gfree")
        s_go = ph.sem("go")
        s_dl, s_si, s_cols, s_qk, s_raw, s_vd = (ph.sem(n) for n in ("dl", "si", "cols", "qk", "raw", "vd"))
        s_rs, s_att, s_same, s_sum, s_msg = (ph.sem(n) for n in ("rs", "att", "same", "sum", "msg"))
        s_add = ph.sem("add")


        def far_sp(sp):
            with sp.Fori(0, NG // 2) as b:
                for h in range(2):
                    g = b * 2 + h
                    sp.wait_ge(s_ldfree, g + 1)
                    sp.dma_start(ea[0:R64, h, :], A["ea64T"][:, ds(g * G * P, G * P)]).then_inc(s_ld[h], 16)
                    sp.dma_start(rows[:, h].rearrange("p u f -> p (u f)"),
                                 bcast_rows(T.dst_rows[ds(g * G * P, G * P)], P)).then_inc(s_ld[h], 16)
                    sp.dma_start(isrc[:, h, :], A["src_cols"][:, ds(g * G, G)]).then_inc(s_ld[h], 16)
                    sp.dma_start(idst[:, h, :], A["dst_cols"][:, ds(g * G, G)]).then_inc(s_ld[h], 16)
                    sp.dma_start(iout[:, h, :], T.dstu_cols[:, ds(g * G, G)]).then_inc(s_ld[h], 16)

        def far_pool(pool):
            pool.sem_inc(s_ldfree, 2)
            start_additions(pool, [T.acc0], T.zeros, [s_add])
            with pool.Fori(0, NG // 2) as b:
                for h in range(2):
                    g = b * 2 + h
                    pool.wait_ge(s_ld[h], (b + 1) * 80)
                    for u in range(G):
                        pool.wait_ge(s_gfree, g * G + u + 1)
                        pool.sem_inc(s_go, 1)
                        pool.indirect_dma_start(kv[:, u, :], None, T.kv_tab,
                                                bass.IndirectOffsetOnAxis(isrc[:, h, u:u + 1], 0)).then_inc(s_ge[u], 16)
                        pool.indirect_dma_start(q[:, u, :], None, T.q_tab,
                                                bass.IndirectOffsetOnAxis(idst[:, h, u:u + 1], 0)).then_inc(s_ge[u], 16)
                    for u in range(G):
                        pool.wait_ge(s_msg, g * G + u + 3)
                        pool.wait_ge(s_add, (g * G + u + 1) * 16)
                        pool.sem_inc(s_go, 1)
                        pool.indirect_dma_start(T.acc0, bass.IndirectOffsetOnAxis(iout[:, h, u:u + 1], 0),
                                                msg[:, u % 2, :], None, compute_op=ALU.add).then_inc(s_add, 16)
                    pool.wait_ge(s_add, (g * G + G + 1) * 16)
                    pool.sem_inc(s_ldfree, 1)

        def far_pe(pe):
            with pe.Fori(0, NG // 2) as b:
                for h in range(2):
                    g = b * 2 + h
                    pe.wait_ge(s_ld[h], (b + 1) * 80)
                    for u in range(G):
                        pe.wait_ge(s_vd, g * G + u + 1)
                        nc.tensor.matmul(ps_d[:, u % 2, :], ea[:, h, u * P:(u + 1) * P], w[:], start=True,
                                         stop=True).then_inc(s_dl, 1)
                    for u in range(G):
                        pe.wait_ge(s_same, g * G + u + 1)
                        pe.wait_ge(s_msg, g * G + u + 1)
                        nc.tensor.matmul(ps_m[:, u % 2, 0:H], same[:, u, :], vd[:, u, :], start=True,
                                         stop=True).then_inc(s_sum, 1)

        def far_act(act):
            nc.scalar.activation(msg[:, :, H:H + 1], T.zeros[:, None, 0:1].to_broadcast([P, 2, 1]), ACT.Copy)
            act.sem_inc(s_msg, 2)
            with act.Fori(0, NG) as g:
                for u in range(G):
                    act.wait_ge(s_dl, g * G + u + 1)
                    nc.scalar.activation(ps_d[:, u % 2, :], ps_d[:, u % 2, :], ACT.Silu).then_inc(s_si, 1)
                act.wait_ge(s_raw, (g + 1) * G)
                nc.scalar.activation(att[:, 0, :], raw[:], ACT.Silu).then_inc(s_rs, 1)
                for u in range(G):
                    act.wait_ge(s_sum, g * G + u + 1)
                    act.wait_ge(s_add, g * G * 16 + max(u, 1) * 16)
                    nc.scalar.activation(msg[:, u % 2, 0:H], ps_m[:, u % 2, 0:H], ACT.Copy).then_inc(s_msg, 1)

        def far_dve(dve):
            dve.sem_inc(s_gfree, G)
            dve.sem_inc(s_vd, 2)
            with dve.Fori(0, NG // 2) as b:
                for h in range(2):
                    g = b * 2 + h
                    nc.vector.tensor_copy(cols[:, 0, :], T.dst_f[:, ds(g * G, G)]).then_inc(s_cols, 1)
                    nc.vector.tensor_copy(cols[:, 1, :], T.cut[:, ds(g * G, G)]).then_inc(s_cols, 1)
                    for u in range(G):
                        n = g * G + u
                        dve.wait_ge(s_ge[u], (g + 1) * 32)
                        nc.vector.tensor_tensor(qk[:, u % 2, :], q[:, u, :], kv[:, u, 0:H], ALU.mult).then_inc(s_qk, 1)
                        dve.wait_ge(s_si, n + 1)
                        nc.vector.tensor_tensor(vd[:, u, :], kv[:, u, H:2 * H], ps_d[:, u % 2, H:2 * H],
                                                ALU.mult).then_inc(s_gfree, 1)
                        dve.wait_ge(s_qk, n + 1)
                        nc.vector.tensor_tensor_reduce(out=junk[:, u, :], in0=qk[:, u % 2, :], in1=ps_d[:, u % 2, 0:H],
                                                       scale=1.0, scalar=0.0, op0=ALU.mult, op1=ALU.add,
                                                       accum_out=raw[:, u:u + 1]).then_inc(s_raw, 1)
                        dve.wait_ge(s_raw, n + 1)
                        dve.sem_inc(s_vd, 1)
                    dve.wait_ge(s_rs, g + 1)
                    dve.wait_ge(s_cols, (g + 1) * 2)
                    nc.vector.tensor_tensor(att[:, 1, :], att[:, 0, :], cols[:, 1, :], ALU.mult).then_inc(s_att, 1)
                    dve.wait_ge(s_att, g + 1)
                    for u in range(G):
                        nc.vector.tensor_scalar(same[:, u, :], rows[:, h, u, :], cols[:, 0, u:u + 1],
                                                att[:, 1, u:u + 1], ALU.is_equal, ALU.mult).then_inc(s_same, 1)
                    dve.wait_ge(s_sum, (g + 1) * G)

        s_tile = [ph.sems(f"tile{h}_", G) for h in range(2)]
        hotT = ph.sb("hotT", [P, 2, G * P], F32R)
        win = ph.sb("win", [P, 2, 2 * H], F32R)
        kv2 = ph.sb("kv2", [P, 2, G, 2 * H])
        qk2 = ph.sb("qk2", [P, 2, 2, H])
        vd2 = ph.sb("vd2", [P, 2, G, H])
        att2 = ph.sb("att2", [P, 2, 3, G])
        hot = ph.sb("hot", [P, 2, G, P])
        count = ph.sb("count", [P, 2])
        ones_out = ph.sb("ones_out", [P, G * P], BF16)
        s_cnt = ph.sem("cnt")
        cut2 = ph.sb("cut2", [P, 2, G])
        off2 = ph.sb("off2", [P, 2, G])
        agg = ph.sb("agg", [P, 2, H + 1])
        ps_q = ph.ps("ps_q", [P, 2, 2, H])
        ps_k = ph.ps("ps_k", [P, 2, 2, H])
        ps_a = ps_m
        banks = [ps_d[:, 0, :], ps_d[:, 1, :], ps_k[:, 0].rearrange("p a d -> p (a d)"),
                 ps_k[:, 1].rearrange("p a d -> p (a d)")]
        dkv = [ps_d[:].rearrange("p t (a d) -> p t a d", a=2), ps_k[:]]
        s_hotT, s_q, s_pair, s_hotA, s_red, s_agg, s_vp = (
            ph.sem(n) for n in ("hotT", "q", "pair", "hotA", "red", "agg", "vp"))
        LAST = NG // 2 - 1

        def near_sp(sp):
            with sp.Fori(0, NG // 2) as b:
                for h in range(2):
                    g = b * 2 + h
                    first = sp.value_load(T.base[0:1, ds(g, 1)], min_val=0, max_val=NP - P)
                    sp.wait_ge(s_gfree, g + 1)
                    sp.dma_start(ea[0:R64, h, :], A["ea64T"][:, ds(g * G * P, G * P)]).then_inc(s_ld[h], 16)
                    sp.dma_start(rows[:, h].rearrange("p u f -> p (u f)"),
                                 bcast_rows(T.dst_rows[ds(g * G * P, G * P)], P)).then_inc(s_ld[h], 16)
                    sp.dma_start(isrc[:, h, :], A["src_cols"][:, ds(g * G, G)]).then_inc(s_ld[h], 16)
                    sp.dma_start(win[:, h, :].bitcast(F32), T.qs_tab[ds(first, P), :]).then_inc(s_ld[h], 16)

        def near_pool(pool):
            start_additions(pool, [T.acc0], T.zeros, [s_add])

            def gathers(g, b, h):
                pool.wait_ge(s_ld[h], (b + 1) * 64)
                pool.wait_ge(s_gfree, g + 1)
                pool.sem_inc(s_go, 1)
                for u in range(G):
                    pool.indirect_dma_start(kv2[:, h, u, :], None, T.kv_tab,
                                            bass.IndirectOffsetOnAxis(isrc[:, h, u:u + 1], 0)).then_inc(s_tile[h][u], 16)

            def add(g, h):
                first = pool.value_load(T.base[0:1, ds(g, 1)], min_val=0, max_val=NP - P)
                pool.wait_ge(s_agg, g + 3)
                pool.wait_ge(s_add, (g + 1) * 16)
                pool.sem_inc(s_go, 1)
                pool.dma_start(T.acc0[ds(first, P), :], agg[:, h, :], accum_op=ALU.add).then_inc(s_add, 16)

            gathers(0, 0, 0)
            gathers(1, 0, 1)
            with pool.Fori(0, LAST) as b:
                gathers(b * 2 + 2, b + 1, 0)
                add(b * 2, 0)
                gathers(b * 2 + 3, b + 1, 1)
                add(b * 2 + 1, 1)
            add(NG - 2, 0)
            add(NG - 1, 1)
            pool.wait_ge(s_add, (NG + 1) * 16)

        def near_pe(pe):
            def pair(g, b, h, i):
                if i == 0:
                    pe.wait_ge(s_ld[h], (b + 1) * 64)
                n = g * 4 + i
                pe.wait_ge(s_vp, n + 1)
                for v in range(2):
                    u = 2 * i + v
                    nc.tensor.matmul(banks[u % 4], ea[:, h, u * P:(u + 1) * P], w[:], start=True,
                                     stop=True).then_inc(s_dl, 1)
                pe.wait_ge(s_pair, n + 1)
                if i == 0:
                    pe.wait_ge(s_hotT, g + 1)
                for v in range(2):
                    e = hotT[:, h, (2 * i + v) * P:(2 * i + v + 1) * P]
                    nc.tensor.matmul(ps_q[:, i % 2, v, :], e, win[:, h, 0:H], start=True, stop=False)
                    nc.tensor.matmul(ps_q[:, i % 2, v, :], e, win[:, h, H:2 * H], start=False,
                                     stop=True).then_inc(s_q, 1)

            def reduce(g, h, us):
                for u in us:
                    pe.wait_ge(s_hotA, g * G + u + 1)
                    nc.tensor.matmul(ps_a[:, h, 0:H], hot[:, h, u, :], vd2[:, h, u, :], start=(u == 0),
                                     stop=(u == G - 1)).then_inc(s_red, 1)

            def group(g, b, h, start=False):
                pair(g, b, h, 0)
                pair(g, b, h, 1)
                if not start:
                    reduce(g - 1, 1 - h, range(0, G // 2))
                pair(g, b, h, 2)
                if not start:
                    reduce(g - 1, 1 - h, range(G // 2, G))
                pair(g, b, h, 3)

            group(0, 0, 0, start=True)
            group(1, 0, 1)
            with pe.Fori(1, NG // 2) as b:
                group(b * 2, b, 0)
                group(b * 2 + 1, b, 1)
            reduce(NG - 1, 1, range(G))

        def near_act(act):
            act.sem_inc(s_agg, 2)

            def filt(g, i):
                act.wait_ge(s_dl, g * G + 2 * i + 2)
                o = dkv[i % 2].rearrange("p t a d -> p (t a d)")
                nc.scalar.activation(o, o, ACT.Silu).then_inc(s_si, 1)

            def counts(g, h):
                act.wait_ge(s_hotT, g + 1)
                act.wait_ge(s_agg, g + 1)
                nc.scalar.activation(ones_out[:], hotT[:, h, :].bitcast(F32), ACT.Copy,
                                     accum_out=count[:, h:h + 1]).then_inc(s_cnt, 1)

            def sums(g, h):
                act.wait_ge(s_cnt, g + 1)
                act.wait_ge(s_red, (g + 1) * G)
                act.wait_ge(s_add, (g + 1) * 16)
                act.sem_inc(s_go, 1)
                nc.scalar.activation(agg[:, h, H:H + 1], count[:, h:h + 1], ACT.Copy)
                nc.scalar.activation(agg[:, h, 0:H], ps_a[:, h, 0:H], ACT.Copy).then_inc(s_agg, 1)

            def group(g, h, start=False):
                filt(g, 0)
                filt(g, 1)
                filt(g, 2)
                if not start:
                    sums(g - 1, 1 - h)
                filt(g, 3)
                counts(g, h)
                act.wait_ge(s_raw, (g + 1) * G)
                nc.scalar.activation(att2[:, h, 1, :], att2[:, h, 0, :], ACT.Silu).then_inc(s_rs, 1)

            group(0, 0, start=True)
            group(1, 1)
            with act.Fori(1, NG // 2) as b:
                group(b * 2, 0)
                group(b * 2 + 1, 1)
            sums(NG - 1, 1)

        def near_dve(dve):
            dve.sem_inc(s_gfree, 2)
            dve.sem_inc(s_pair, 2)
            dve.sem_inc(s_vp, 2)

            def onehots(g, b, h):
                dve.wait_ge(s_ld[h], (b + 1) * 64)
                dve.wait_ge(s_agg, g + 1)
                dve.sem_inc(s_go, 1)
                nc.vector.tensor_copy(cut2[:, h, :], T.cut[:, ds(g * G, G)]).then_inc(s_cols, 1)
                nc.vector.tensor_copy(off2[:, h, :], T.off_f[:, ds(g * G, G)]).then_inc(s_cols, 1)
                nc.vector.tensor_scalar(hotT[:, h, :], rows[:, h].rearrange("p u f -> p (u f)"),
                                        T.window[:, ds(g, 1)], None, ALU.is_equal).then_inc(s_hotT, 1)

            def attention(g, b, h, pairs):
                for i in pairs:
                    n = g * 4 + i
                    u = 2 * i
                    for v in range(2):
                        dve.wait_ge(s_tile[h][u + v], (b + 1) * 16)
                    dve.wait_ge(s_q, g * G + u + 2)
                    nc.vector.tensor_tensor(qk2[:, i % 2], ps_q[:, i % 2], kv2[:, h, u:u + 2, 0:H],
                                            ALU.mult).then_inc(s_pair, 1)
                    dve.wait_ge(s_si, n + 1)
                    nc.vector.tensor_tensor(vd2[:, h, u:u + 2, :], dkv[i % 2][:, :, 1, :], kv2[:, h, u:u + 2, H:2 * H],
                                            ALU.mult).then_inc(s_vd, 1)
                    dve.wait_ge(s_pair, n + 3)
                    for v in range(2):
                        nc.vector.tensor_tensor_reduce(out=junk[:, u + v, :], in0=qk2[:, i % 2, v, :],
                                                       in1=dkv[i % 2][:, v, 0, :], scale=1.0, scalar=0.0,
                                                       op0=ALU.mult, op1=ALU.add,
                                                       accum_out=att2[:, h, 0, u + v:u + v + 1]).then_inc(s_raw, 1)
                    dve.wait_ge(s_raw, g * G + u + 2)
                    dve.sem_inc(s_vp, 1)
                if i == 3:
                    dve.wait_ge(s_vd, g * 4 + 4)
                    dve.sem_inc(s_gfree, 1)

            def weigh(g, h):
                dve.wait_ge(s_rs, g + 1)
                dve.wait_ge(s_cols, (g + 1) * 2)
                nc.vector.tensor_tensor(att2[:, h, 2, :], att2[:, h, 1, :], cut2[:, h, :], ALU.mult).then_inc(s_att, 1)
                dve.wait_ge(s_att, g + 1)
                for u in range(G):
                    nc.vector.tensor_scalar(hot[:, h, u, :], T.iota_row[:], off2[:, h, u:u + 1],
                                            att2[:, h, 2, u:u + 1], ALU.is_equal, ALU.mult).then_inc(s_hotA, 1)

            def group(g, b, h, last=False):
                attention(g, b, h, range(3))
                if not last:
                    onehots(g + 1, b + h, 1 - h)
                attention(g, b, h, (3,))
                weigh(g, h)

            onehots(0, 0, 0)
            with dve.Fori(0, LAST) as b:
                group(b * 2, b, 0)
                group(b * 2 + 1, b, 1)
            group(NG - 2, LAST, 0)
            group(NG - 1, LAST, 1, last=True)

        block = ph.block()

        @block.sync
        def _(sp):
            sp.dma_start(w[0:R64, 0:H], A["WdkT"]).then_inc(s_w, 16)
            sp.dma_start(w[0:R64, H:2 * H], A["WdvT"]).then_inc(s_w, 16)
            sp.dma_start(w[R64:R64 + 1, 0:H], A["bdk"].rearrange("(a n) -> a n", a=1)).then_inc(s_w, 16)
            sp.dma_start(w[R64:R64 + 1, H:2 * H], A["bdv"].rearrange("(a n) -> a n", a=1)).then_inc(s_w, 16)
            if_near(sp, T, lambda: near_sp(sp), lambda: far_sp(sp))

        @block.gpsimd
        def _(pool):
            nc.gpsimd.memset(ea[R64:R64 + 1, :, :], 1.0).then_inc(s_one, 1)
            if_near(pool, T, lambda: near_pool(pool), lambda: far_pool(pool))

        @block.tensor
        def _(pe):
            pe.wait_ge(s_w, 64)
            pe.wait_ge(s_one, 1)
            if_near(pe, T, lambda: near_pe(pe), lambda: far_pe(pe))

        @block.scalar
        def _(act):
            if_near(act, T, lambda: near_act(act), lambda: far_act(act))

        @block.vector
        def _(dve):
            if_near(dve, T, lambda: near_dve(dve), lambda: far_dve(dve))


def edge_layer1(nc, A, T):
    with Phase(nc, "e1") as ph:
        w1 = ph.sb("w1", [P, H])
        b1 = ph.sb("b1", [P, 2])
        w2 = ph.sb("w2", [P, 2, H])
        b2 = ph.sb("b2", [B2R, H])
        ea = ph.sb("ea", [P, 2, G * P])
        rows = ph.sb("rows", [P, 2, G, P])
        idst = ph.sb("idst", [P, 2, G], I32)
        iout = ph.sb("iout", [P, 2, G], I32)
        hid = ph.sb("hid", [P, 2, 2, 512])
        xd = ph.sb("xd", [P, 2, G, H])
        cols = ph.sb("cols", [P, G])
        same = ph.sb("same", [P, 4, P])
        prod = ph.sb("prod", [P, 4, H])
        msg = ph.sb("msg", [P, KACC, H])
        ps_h = ph.ps("ps_h", [P, 2, 512])
        ps_f = ph.ps("ps_f", [P, 2, 512])
        ps_m = ph.ps("ps_m", [P, 2, 512])
        s_w = ph.sem("w")
        s_ld = ph.sems("ld", 2)
        s_rowfree, s_dyn = ph.sem("rowfree"), ph.sem("dyn")
        s_ge = [ph.sems(f"ge{h}_", G) for h in range(2)]
        s_win = ph.sems("win", 2)
        s_gfree, s_go, s_cols, s_h, s_hid, s_f, s_prod, s_same, s_sum, s_msg = (
            ph.sem(n) for n in ("gfree", "go", "cols", "h", "hid", "f", "prod", "same", "sum", "msg"))
        s_add = ph.sems("add", KACC)


        def far_sp(sp):
            with sp.Fori(0, NG // 2) as b:
                for h in range(2):
                    g = b * 2 + h
                    sp.wait_ge(s_rowfree, g + 1)
                    sp.dma_start(ea[0:R20, h, :], A["ea20T"][0:R20, ds(g * G * P, G * P)]).then_inc(s_ld[h], 16)
                    sp.dma_start(rows[:, h].rearrange("p u f -> p (u f)"),
                                 bcast_rows(T.src_rows[ds(g * G * P, G * P)], P)).then_inc(s_ld[h], 16)
                    sp.dma_start(idst[:, h, :], A["dst_cols"][:, ds(g * G, G)]).then_inc(s_ld[h], 16)
                    sp.dma_start(iout[:, h, :], T.srcu_cols[:, ds(g * G, G)]).then_inc(s_ld[h], 16)

        def far_pool(pool):
            pool.sem_inc(s_rowfree, 2)
            start_additions(pool, T.acc1, T.zeros, s_add)
            with pool.Fori(0, NG // 2) as b:
                for h in range(2):
                    g = b * 2 + h
                    pool.wait_ge(s_ld[h], (b + 1) * 64)
                    pool.wait_ge(s_gfree, g + 1)
                    pool.sem_inc(s_go, 1)
                    for u in range(G):
                        pool.indirect_dma_start(xd[:, h, u, :], None, T.x1_tab,
                                                bass.IndirectOffsetOnAxis(idst[:, h, u:u + 1], 0)).then_inc(s_ge[h][u], 16)
                    for u in range(G):
                        pool.wait_ge(s_msg, g * G + u + 3)
                        pool.wait_ge(s_add[u % KACC], (g * (G // KACC) + u // KACC + 1) * 16)
                        pool.sem_inc(s_go, 1)
                        pool.indirect_dma_start(T.acc1[u % KACC], bass.IndirectOffsetOnAxis(iout[:, h, u:u + 1], 0),
                                                msg[:, u % KACC, :], None,
                                                compute_op=ALU.add).then_inc(s_add[u % KACC], 16)
                    for k in range(KACC):
                        pool.wait_ge(s_add[k], ((g + 1) * (G // KACC) + 1) * 16)
                    pool.sem_inc(s_rowfree, 1)

        def far_pe(pe):
            pe.wait_ge(s_w, 112)
            pe.sem_inc(s_dyn, 1)
            with pe.Fori(0, NG // 2) as b:
                for h in range(2):
                    g = b * 2 + h
                    pe.wait_ge(s_ld[h], (b + 1) * 64)
                    for q in range(2):
                        m = g * 2 + q
                        for c in range(2):
                            pe.wait_ge(s_hid, m * 2 + c + 1)
                            nc.tensor.matmul(ps_h[:, c, :], w1[0:R20, c * P:(c + 1) * P],
                                             ea[0:R20, h, q * 512:(q + 1) * 512], start=True, stop=True).then_inc(s_h, 1)
                        pe.wait_ge(s_hid, m * 2 + 4)
                        for v in range(4):
                            u = q * 4 + v
                            n = g * G + u
                            pe.wait_ge(s_prod, n + 1)
                            o = ps_f[:, u % 2, 0:H]
                            nc.tensor.matmul(o, hid[:, q, 0, v * P:(v + 1) * P], w2[:, 0, :], start=True, stop=False)
                            nc.tensor.matmul(o, hid[:, q, 1, v * P:(v + 1) * P], w2[:, 1, :], start=False, stop=False)
                            nc.tensor.matmul(o, T.ones_row[:], b2[0:1, :], start=False, stop=True).then_inc(s_f, 1)
                            pe.wait_ge(s_prod, n + 3)
                            pe.wait_ge(s_same, n + 1)
                            pe.wait_ge(s_msg, n + 1)
                            nc.tensor.matmul(ps_m[:, u % 2, 0:H], same[:, v, :], prod[:, v, :], start=True,
                                             stop=True).then_inc(s_sum, 1)

        def far_act(act):
            act.sem_inc(s_msg, 2)
            act.sem_inc(s_hid, 2)
            act.wait_ge(s_w, 112)
            act.sem_inc(s_dyn, 1)
            with act.Fori(0, NG) as g:
                for q in range(2):
                    for c in range(2):
                        act.wait_ge(s_h, g * 4 + q * 2 + c + 1)
                        nc.scalar.activation(hid[:, q, c, :], ps_h[:, c, :], ACT.Silu,
                                             bias=b1[:, c:c + 1]).then_inc(s_hid, 1)
                    for v in range(4):
                        u = q * 4 + v
                        k = u % KACC
                        act.wait_ge(s_sum, g * G + u + 1)
                        act.wait_ge(s_add[k], (g * (G // KACC) + u // KACC + 1) * 16)
                        nc.scalar.activation(msg[:, k, :], ps_m[:, u % 2, 0:H], ACT.Copy).then_inc(s_msg, 1)

        def far_dve(dve):
            dve.sem_inc(s_gfree, 2)
            dve.sem_inc(s_prod, 2)
            with dve.Fori(0, NG // 2) as b:
                for h in range(2):
                    g = b * 2 + h
                    nc.vector.tensor_copy(cols[:], T.src_f[:, ds(g * G, G)]).then_inc(s_cols, 1)
                    dve.wait_ge(s_ld[h], (b + 1) * 64)
                    dve.wait_ge(s_cols, g + 1)
                    for u in range(G):
                        n = g * G + u
                        if u >= 4:
                            dve.wait_ge(s_sum, n - 3)
                        nc.vector.tensor_scalar(same[:, u % 4, :], rows[:, h, u, :], cols[:, u:u + 1], None,
                                                ALU.is_equal).then_inc(s_same, 1)
                        dve.wait_ge(s_ge[h][u], (b + 1) * 16)
                        dve.wait_ge(s_f, n + 1)
                        nc.vector.tensor_tensor(prod[:, u % 4, :], xd[:, h, u, :], ps_f[:, u % 2, 0:H],
                                                ALU.mult).then_inc(s_prod, 1)
                    dve.wait_ge(s_sum, (g + 1) * G)
                    dve.sem_inc(s_gfree, 1)

        rowd = ph.sb("rowd", [P, 2, G * P])
        hotT = ph.sb("hotT", [P, 2, G * P], F32R)
        win = ph.sb("win", [P, 2, 2 * H], F32R)
        first_of = ph.sb("first_of", [P, 2, G, P], F32R)
        count = ph.sb("count", [P, 2, G])
        place = ph.sb("place", [P, 2, 3, G])
        uniq = ph.sb("uniq", [P, 2, G], I32)
        uniq_all = ph.sb("uniq_all", [P, ET], I32)
        src2 = ph.sb("src2", [P, 2, G])
        xs = ph.sb("xs", [P, 2, 2, H])
        prod2 = ph.sb("prod2", [P, 4, 2, H])
        msg2 = ph.sb("msg2", [P, 4, 2, H])
        prod_s = ph.sb("prod_s", [P, 4, 2, 2, H], F32R)
        part = ph.sb("part", [B2R, 2, H])
        cut3 = ph.sb("cut3", [B2R, 3, H], BF16)
        b2p = ph.sb("b2p", [B2R, H], BF16)
        ones_b = ph.sb("ones_b", [B2R, P], BF16)
        w1s = ph.sb("w1s", [P, H], F32R)
        eas = ph.sb("eas", [P, 2, G * P], F32R)
        ps_x = ph.ps("ps_x", [P, 2, 2, H])
        s_hotT, s_x, s_xs, s_fo, s_pl, s_id, s_b2, s_out, s_eah, s_eas, s_hi, s_lo = (
            ph.sem(n) for n in ("hotT", "x", "xs", "fo", "pl", "id", "b2", "out", "eah", "eas", "hi", "lo"))
        ps_f2 = ps_f[:].rearrange("p t (a d) -> p t a d", a=2)
        ps_m2 = ps_m[:].rearrange("p t (a d) -> p t a d", a=2)
        LAST = NG // 2 - 1

        def near_sp(sp):
            with sp.Fori(0, NG // 2) as b:
                for h in range(2):
                    g = b * 2 + h
                    first = sp.value_load(T.base[0:1, ds(g, 1)], min_val=0, max_val=NP - P)
                    sp.wait_ge(s_id, g + 1)
                    for r in range(0, P, R20P):
                        sp.dma_start(ea[r:r + R20P, h, :], A["ea20T"][:, ds(g * G * P, G * P)]).then_inc(s_ld[h], 16)
                    sp.dma_start(rows[:, h].rearrange("p u f -> p (u f)"),
                                 bcast_rows(T.src_rows[ds(g * G * P, G * P)], P)).then_inc(s_ld[h], 16)
                    sp.dma_start(rowd[:, h, :], bcast_rows(T.dst_rows[ds(g * G * P, G * P)], P)).then_inc(s_ld[h], 16)
                    sp.wait_ge(s_f, g * 4 + 4)
                    sp.sem_inc(s_dyn, 1)
                    sp.dma_start(win[:, h, :].bitcast(F32), T.x1s_tab[ds(first, P), :]).then_inc(s_win[h], 16)
            sp.wait_ge(s_id, NG + 2)
            sp.dma_start(T.srcu_cols, uniq_all[:]).then_inc(s_out, 16)
            sp.wait_ge(s_out, 16)

        def near_pool(pool):
            start_additions(pool, T.acc1, T.zeros, s_add)
            with pool.Fori(0, NG // 2) as b:
                for h in range(2):
                    g = b * 2 + h
                    for u in range(G):
                        k = u % KACC
                        if u == 0:
                            pool.wait_ge(s_id, g + 3)
                        pool.wait_ge(s_msg, g * 4 + u // 2 + 3)
                        pool.wait_ge(s_add[k], (g * (G // KACC) + u // KACC + 1) * 16)
                        pool.sem_inc(s_go, 1)
                        pool.indirect_dma_start(T.acc1[k], bass.IndirectOffsetOnAxis(uniq[:, h, u:u + 1], 0),
                                                msg2[:, u // 2, u % 2, :], None,
                                                compute_op=ALU.add).then_inc(s_add[k], 16)
            for k in range(KACC):
                pool.wait_ge(s_add[k], (NG * (G // KACC) + 1) * 16)

        def near_pe(pe):
            pe.sem_inc(s_f, 8)
            pe.sem_inc(s_sum, 8)
            pe.wait_ge(s_b2, 13)
            pe.sem_inc(s_dyn, 1)

            def hidden(m, b, h, q):
                if q == 0:
                    pe.wait_ge(s_ld[h], (b + 1) * 96)
                pe.wait_ge(s_eas, m + 1)
                for c in range(2):
                    pe.wait_ge(s_hid, m * 2 + c + 1)
                    nc.tensor.matmul(ps_h[:, c, :], w1s[:, c * P:(c + 1) * P], eas[:, h, q * 512:(q + 1) * 512],
                                     start=True, stop=True).then_inc(s_h, 1)

            def filters(g, b, h, i):
                n = g * 4 + i
                q = i // 2
                if i == 0:
                    pe.wait_ge(s_win[h], (b + 1) * 16)
                pe.wait_ge(s_hotT, g + 1)
                pe.wait_ge(s_xs, n + 1)
                for v in range(2):
                    e = hotT[:, h, (2 * i + v) * P:(2 * i + v + 1) * P]
                    nc.tensor.matmul(ps_x[:, i % 2, v, :], e, win[:, h, 0:H], start=True, stop=False)
                    nc.tensor.matmul(ps_x[:, i % 2, v, :], e, win[:, h, H:2 * H], start=False,
                                     stop=True).then_inc(s_x, 1)
                pe.wait_ge(s_hid, (g * 2 + q) * 2 + 4)
                pe.wait_ge(s_prod, n + 1)
                for v in range(2):
                    e = ((2 * i + v) % 4) * P
                    o = ps_f2[:, i % 2, v, :]
                    nc.tensor.matmul(o, hid[:, q, 0, e:e + P], w2[:, 0, :], start=True, stop=False)
                    nc.tensor.matmul(o, hid[:, q, 1, e:e + P], w2[:, 1, :], start=False, stop=False)
                    last = nc.tensor.matmul(o, ones_b[:], b2p[:], start=False, stop=True)
                last.then_inc(s_f, 1)

            def sums(g, h, i):
                n = g * 4 + i
                pe.wait_ge(s_lo, n + 1)
                pe.wait_ge(s_fo, (g + 1) * G)
                pe.wait_ge(s_msg, n + 1)
                for v in range(2):
                    for k in range(2):
                        last = nc.tensor.matmul(ps_m2[:, i % 2, v, :], first_of[:, h, 2 * i + v, :],
                                                prod_s[:, i, v, k, :], start=(k == 0), stop=(k == 1))
                last.then_inc(s_sum, 1)

            def group(g, b, h, start=False, last=False):
                hidden(g * 2 + 1, b, h, 1)
                for i in range(4):
                    if i == 3 and not last:
                        hidden(g * 2 + 2, b + h, 1 - h, 0)
                    filters(g, b, h, i)
                    if i >= 2:
                        sums(g, h, i - 2)
                    elif not start:
                        sums(g - 1, 1 - h, i + 2)

            hidden(0, 0, 0, 0)
            group(0, 0, 0, start=True)
            group(1, 0, 1)
            with pe.Fori(1, LAST) as b:
                group(b * 2, b, 0)
                group(b * 2 + 1, b, 1)
            group(NG - 2, LAST, 0)
            group(NG - 1, LAST, 1, last=True)
            sums(NG - 1, 1, 2)
            sums(NG - 1, 1, 3)

        def near_act(act):
            act.sem_inc(s_hid, 2)
            act.sem_inc(s_xs, 2)
            act.sem_inc(s_msg, 2)
            act.wait_ge(s_w, 112)
            act.sem_inc(s_dyn, 1)

            def hidden(m, q):
                for c in range(2):
                    act.wait_ge(s_h, m * 2 + c + 1)
                    nc.scalar.activation(hid[:, q, c, :], ps_h[:, c, :], ACT.Silu,
                                         bias=b1[:, c:c + 1]).then_inc(s_hid, 1)

            def features(g, i):
                act.wait_ge(s_x, g * G + 2 * i + 2)
                act.wait_ge(s_prod, g * 4 + i + 1)
                nc.scalar.activation(xs[:, i % 2], ps_x[:, i % 2], ACT.Copy).then_inc(s_xs, 1)

            def messages(g, i):
                n = g * 4 + i
                act.wait_ge(s_sum, n + 9)
                for v in range(2):
                    u = 2 * i + v
                    if not isinstance(g, int) or 2 * g + u // KACC:
                        act.wait_ge(s_add[u % KACC], (g * (G // KACC) + u // KACC) * 16)
                nc.scalar.activation(msg2[:, i], ps_m2[:, i % 2], ACT.Copy).then_inc(s_msg, 1)

            def rounded(m, b, h, q):
                if q == 0:
                    act.wait_ge(s_ld[h], (b + 1) * 96)
                half = slice(q * 512, (q + 1) * 512)
                nc.scalar.activation(eas[:, h, half], ea[:, h, half], ACT.Copy).then_inc(s_eah, 1)

            def high(g, i):
                n = g * 4 + i
                act.wait_ge(s_prod, n + 3)
                act.wait_ge(s_sum, n + 5)
                nc.scalar.activation(prod_s[:, i, :, 0, :], prod2[:, i], ACT.Copy).then_inc(s_hi, 1)

            def group(g, b, h, start=False, last=False):
                hidden(g * 2 + 1, 1)
                for i in range(4):
                    if i == 3 and not last:
                        hidden(g * 2 + 2, 0)
                    features(g, i)
                    if i > 0:
                        high(g, i - 1)
                    elif not start:
                        high(g - 1, 3)
                    if i == 1 and not last:
                        rounded(g * 2 + 2, b + h, 1 - h, 0)
                        rounded(g * 2 + 3, b + h, 1 - h, 1)
                    if i == 3:
                        messages(g, 0)
                    elif not start:
                        messages(g - 1, i + 1)

            rounded(0, 0, 0, 0)
            rounded(1, 0, 0, 1)
            hidden(0, 0)
            group(0, 0, 0, start=True)
            group(1, 0, 1)
            with act.Fori(1, LAST) as b:
                group(b * 2, b, 0)
                group(b * 2 + 1, b, 1)
            group(NG - 2, LAST, 0)
            group(NG - 1, LAST, 1, last=True)
            high(NG - 1, 3)
            for i in range(1, 4):
                messages(NG - 1, i)

        def near_dve(dve):
            dve.sem_inc(s_prod, 2)
            dve.sem_inc(s_id, 2)
            nc.vector.memset(ones_b[:], 1.0).then_inc(s_b2, 1)
            nc.vector.memset(b2p[:], 0.0).then_inc(s_b2, 1)
            dve.wait_ge(s_w, 112)
            nc.vector.tensor_copy(w1s[:], w1[:]).then_inc(s_b2, 1)
            nc.vector.tensor_copy(cut3[:, 0, :], b2[:]).then_inc(s_b2, 1)
            dve.wait_ge(s_b2, 4)
            for r in (R20P, 3 * R20P):
                rr = slice(r, r + R20P)
                nc.vector.tensor_tensor(w1s[rr, :], w1[rr, :], w1s[rr, :], ALU.subtract).then_inc(s_b2, 1)
            nc.vector.tensor_tensor(part[:, 0, :], b2[:], cut3[:, 0, :], ALU.subtract).then_inc(s_b2, 1)
            dve.wait_ge(s_b2, 7)
            nc.vector.tensor_copy(cut3[:, 1, :], part[:, 0, :]).then_inc(s_b2, 1)
            dve.wait_ge(s_b2, 8)
            nc.vector.tensor_tensor(part[:, 1, :], part[:, 0, :], cut3[:, 1, :], ALU.subtract).then_inc(s_b2, 1)
            dve.wait_ge(s_b2, 9)
            nc.vector.tensor_copy(cut3[:, 2, :], part[:, 1, :]).then_inc(s_b2, 1)
            dve.wait_ge(s_b2, 10)
            for k in range(3):
                r = k * R20P
                nc.vector.tensor_copy(b2p[r:r + 1, :], cut3[r:r + 1, k, :]).then_inc(s_b2, 1)

            def leftover(m, h, q):
                dve.wait_ge(s_eah, m + 1)
                half = slice(q * 512, (q + 1) * 512)
                nc.vector.tensor_tensor(eas[P // 2:P, h, half], ea[P // 2:P, h, half], eas[P // 2:P, h, half],
                                        ALU.subtract).then_inc(s_eas, 1)

            def low(g, i):
                dve.wait_ge(s_hi, g * 4 + i + 1)
                nc.vector.tensor_tensor(prod_s[:, i, :, 1, :], prod2[:, i], prod_s[:, i, :, 0, :],
                                        ALU.subtract).then_inc(s_lo, 1)

            def onehots(g, b, h):
                dve.wait_ge(s_ld[h], (b + 1) * 96)
                dve.wait_ge(s_f, g * 4 + 4)
                nc.vector.tensor_scalar(hotT[:, h, :], rowd[:, h, :], T.window[:, ds(g, 1)], None,
                                        ALU.is_equal).then_inc(s_hotT, 1)
                dve.wait_ge(s_id, g + 1)
                dve.sem_inc(s_dyn, 1)
                nc.vector.tensor_copy(src2[:, h, :], T.src_f[:, ds(g * G, G)]).then_inc(s_cols, 1)
                dve.wait_ge(s_cols, g + 1)
                dve.wait_ge(s_sum, g * 4 + 4)
                dve.sem_inc(s_dyn, 1)

            def firsts(g, h, us):
                for u in us:
                    nc.vector.scalar_tensor_tensor(first_of[:, h, u, :], rows[:, h, u, :], src2[:, h, u:u + 1],
                                                   T.earlier[:], ALU.is_equal, ALU.mult,
                                                   accum_out=count[:, h, u:u + 1]).then_inc(s_fo, 1)

            def places(g, h):
                dve.wait_ge(s_fo, (g + 1) * G)
                if not isinstance(g, int) or g >= 1:
                    for k in range(KACC):
                        dve.wait_ge(s_add[k], (g * (G // KACC) - 1) * 16)
                nc.vector.tensor_scalar(place[:, h, 0, :], count[:, h, :], 2.0, -1.0, ALU.min,
                                        ALU.add).then_inc(s_pl, 1)
                nc.vector.tensor_scalar(place[:, h, 1, :], src2[:, h, :], T.trash[:], -1.0, ALU.subtract,
                                        ALU.mult).then_inc(s_pl, 1)
                dve.wait_ge(s_pl, g * 3 + 2)
                nc.vector.tensor_tensor(place[:, h, 2, :], place[:, h, 0, :], place[:, h, 1, :],
                                        ALU.mult).then_inc(s_pl, 1)
                dve.wait_ge(s_pl, g * 3 + 3)
                nc.vector.tensor_tensor(uniq_all[:, ds(g * G, G)], place[:, h, 2, :], src2[:, h, :], ALU.add)
                nc.vector.tensor_tensor(uniq[:, h, :], place[:, h, 2, :], src2[:, h, :], ALU.add).then_inc(s_id, 1)

            def product(g, i):
                n = g * 4 + i
                dve.wait_ge(s_xs, n + 3)
                dve.wait_ge(s_f, n + 9)
                dve.wait_ge(s_sum, n + 5)
                nc.vector.tensor_tensor(prod2[:, i], ps_f2[:, i % 2], xs[:, i % 2], ALU.mult).then_inc(s_prod, 1)

            def group(g, b, h, start=False, last=False):
                product(g, 0)
                if not start:
                    low(g - 1, 3)
                product(g, 1)
                low(g, 0)
                if not last:
                    leftover(g * 2 + 2, 1 - h, 0)
                    onehots(g + 1, b + h, 1 - h)
                    firsts(g + 1, 1 - h, (0,))
                product(g, 2)
                low(g, 1)
                if not last:
                    leftover(g * 2 + 3, 1 - h, 1)
                    firsts(g + 1, 1 - h, (1, 2, 3))
                product(g, 3)
                low(g, 2)
                if not last:
                    firsts(g + 1, 1 - h, (4, 5, 6, 7))
                    places(g + 1, 1 - h)

            leftover(0, 0, 0)
            leftover(1, 0, 1)
            onehots(0, 0, 0)
            firsts(0, 0, range(G))
            places(0, 0)
            group(0, 0, 0, start=True)
            group(1, 0, 1)
            with dve.Fori(1, LAST) as b:
                group(b * 2, b, 0)
                group(b * 2 + 1, b, 1)
            group(NG - 2, LAST, 0)
            group(NG - 1, LAST, 1, last=True)
            low(NG - 1, 3)

        block = ph.block()

        @block.sync
        def _(sp):
            for r in range(0, P, R20P):
                sp.dma_start(w1[r:r + R20P, :], A["Wf1"]).then_inc(s_w, 16)
            sp.dma_start(w2[:], A["Wf2"].rearrange("(c p) n -> p c n", p=P)).then_inc(s_w, 16)
            sp.dma_start(b1[:], A["bf1"].rearrange("(c p) -> p c", p=P)).then_inc(s_w, 16)
            sp.dma_start(b2[:], bcast_rows(A["bf2"], B2R)).then_inc(s_w, 16)
            if_near(sp, T, lambda: near_sp(sp), lambda: far_sp(sp))

        @block.gpsimd
        def _(pool):
            if_near(pool, T, lambda: near_pool(pool), lambda: far_pool(pool))

        @block.tensor
        def _(pe):
            if_near(pe, T, lambda: near_pe(pe), lambda: far_pe(pe))

        @block.scalar
        def _(act):
            if_near(act, T, lambda: near_act(act), lambda: far_act(act))

        @block.vector
        def _(dve):
            if_near(dve, T, lambda: near_dve(dve), lambda: far_dve(dve))


def edge_layer2(nc, A, T):
    with Phase(nc, "e2") as ph:
        rows = ph.sb("rows", [P, 2, G, P])
        isrc = ph.sb("isrc", [P, 2, G], I32)
        iout = ph.sb("iout", [P, 2, G], I32)
        xs = ph.sb("xs", [P, 2, G, H])
        cols = ph.sb("cols", [P, G])
        same = ph.sb("same", [P, G, P])
        msg = ph.sb("msg", [P, 2, H])
        ps_m = ph.ps("ps_m", [P, 2, 512])
        s_ld = ph.sems("ld", 2)
        s_ge = [ph.sems(f"ge{h}_", G) for h in range(2)]
        s_ldfree, s_gfree, s_go, s_cols, s_same, s_sum, s_msg, s_add = (
            ph.sem(n) for n in ("ldfree", "gfree", "go", "cols", "same", "sum", "msg", "add"))


        s_zero = ph.sem("zero")

        def far_sp(sp):
            for acc in T.acc3:
                sp.dma_start(acc.rearrange("(p t) d -> p t d", p=P),
                             T.zeros[:, None, :].to_broadcast([P, acc.shape[0] // P, PAY])).then_inc(s_zero, 16)
            sp.wait_ge(s_zero, K3 * 16)
            with sp.Fori(0, NG // 2) as b:
                for h in range(2):
                    g = b * 2 + h
                    sp.wait_ge(s_ldfree, g + 1)
                    sp.dma_start(rows[:, h].rearrange("p u f -> p (u f)"),
                                 bcast_rows(T.dst_rows[ds(g * G * P, G * P)], P)).then_inc(s_ld[h], 16)
                    sp.dma_start(isrc[:, h, :], A["src_cols"][:, ds(g * G, G)]).then_inc(s_ld[h], 16)
                    sp.dma_start(iout[:, h, :], T.dstu_cols[:, ds(g * G, G)]).then_inc(s_ld[h], 16)

        def far_pool(pool):
            pool.sem_inc(s_ldfree, 2)
            start_additions(pool, [T.acc2], T.zeros, [s_add])
            with pool.Fori(0, NG // 2) as b:
                for h in range(2):
                    g = b * 2 + h
                    pool.wait_ge(s_ld[h], (b + 1) * 48)
                    pool.wait_ge(s_gfree, g + 1)
                    pool.sem_inc(s_go, 1)
                    for u in range(G):
                        pool.indirect_dma_start(xs[:, h, u, :], None, T.hs_tab,
                                                bass.IndirectOffsetOnAxis(isrc[:, h, u:u + 1], 0)).then_inc(s_ge[h][u], 16)
                    for u in range(G):
                        pool.wait_ge(s_msg, g * G + u + 3)
                        pool.wait_ge(s_add, (g * G + u + 1) * 16)
                        pool.sem_inc(s_go, 1)
                        pool.indirect_dma_start(T.acc2, bass.IndirectOffsetOnAxis(iout[:, h, u:u + 1], 0),
                                                msg[:, u % 2, :], None, compute_op=ALU.add).then_inc(s_add, 16)
                    pool.wait_ge(s_add, (g * G + G + 1) * 16)
                    pool.sem_inc(s_ldfree, 1)

        def far_pe(pe):
            with pe.Fori(0, NG // 2) as b:
                for h in range(2):
                    for u in range(G):
                        n = (b * 2 + h) * G + u
                        pe.wait_ge(s_ge[h][u], (b + 1) * 16)
                        pe.wait_ge(s_same, n + 1)
                        pe.wait_ge(s_msg, n + 1)
                        nc.tensor.matmul(ps_m[:, u % 2, 0:H], same[:, u, :], xs[:, h, u, :], start=True,
                                         stop=True).then_inc(s_sum, 1)

        def far_act(act):
            act.sem_inc(s_msg, 2)
            with act.Fori(0, NG) as g:
                for u in range(G):
                    act.wait_ge(s_sum, g * G + u + 1)
                    act.wait_ge(s_add, g * G * 16 + max(u, 1) * 16)
                    nc.scalar.activation(msg[:, u % 2, :], ps_m[:, u % 2, 0:H], ACT.Copy).then_inc(s_msg, 1)

        def far_dve(dve):
            dve.sem_inc(s_gfree, 2)
            with dve.Fori(0, NG // 2) as b:
                for h in range(2):
                    g = b * 2 + h
                    nc.vector.tensor_copy(cols[:], T.dst_f[:, ds(g * G, G)]).then_inc(s_cols, 1)
                    dve.wait_ge(s_ld[h], (b + 1) * 48)
                    dve.wait_ge(s_cols, g + 1)
                    for u in range(G):
                        nc.vector.tensor_scalar(same[:, u, :], rows[:, h, u, :], cols[:, u:u + 1], None,
                                                ALU.is_equal).then_inc(s_same, 1)
                    dve.wait_ge(s_sum, (g + 1) * G)
                    dve.sem_inc(s_gfree, 1)

        s_tile = [ph.sems(f"tile{h}_", G) for h in range(4)]
        isrc4 = ph.sb("isrc4", [P, 4, G], I32)
        xs4 = ph.sb("xs4", [P, 4, G, H])
        hot = ph.sb("hot", [P, 2, G, P])
        off2 = ph.sb("off2", [P, 2, G])
        agg = ph.sb("agg", [P, 2, H])
        ps_a = ps_m
        s_ix = ph.sems("ix", 4)
        s_hot, s_red, s_agg = (ph.sem(n) for n in ("hot", "red", "agg"))
        Q = NG // 4

        def near_sp(sp):
            with sp.Fori(0, Q) as b:
                for acc in T.acc3:
                    sp.dma_start(acc[ds(b * ZROWS, ZROWS), :].rearrange("(p j) d -> p j d", p=P),
                                 T.zeros[:, None, :].to_broadcast([P, ZROWS // P, PAY])).then_inc(s_zero, 16)
                for h in range(4):
                    sp.wait_ge(s_agg, b * 4 + h + 1)
                    sp.dma_start(isrc4[:, h, :], A["src_cols"][:, ds((b * 4 + h) * G, G)]).then_inc(s_ix[h], 16)
            sp.wait_ge(s_zero, Q * K3 * 16)

        def near_pool(pool):
            start_additions(pool, [T.acc2], T.zeros, [s_add])

            def gathers(g, b, h):
                pool.wait_ge(s_ix[h], (b + 1) * 16)
                pool.sem_inc(s_go, 1)
                for u in range(G):
                    pool.indirect_dma_start(xs4[:, h, u, :], None, T.hs_tab,
                                            bass.IndirectOffsetOnAxis(isrc4[:, h, u:u + 1], 0)).then_inc(s_tile[h][u], 16)

            def add(g, h):
                first = pool.value_load(T.base[0:1, ds(g, 1)], min_val=0, max_val=NP - P)
                pool.wait_ge(s_agg, g + 5)
                pool.wait_ge(s_add, (g + 1) * 16)
                pool.sem_inc(s_go, 1)
                pool.dma_start(T.acc2[ds(first, P), :], agg[:, h % 2, :], accum_op=ALU.add).then_inc(s_add, 16)

            gathers(0, 0, 0)
            gathers(1, 0, 1)
            with pool.Fori(0, Q - 1) as b:
                for h in range(4):
                    gathers(b * 4 + h + 2, b + (h + 2) // 4, (h + 2) % 4)
                    add(b * 4 + h, h)
            for h in range(4):
                if h < 2:
                    gathers(NG - 2 + h, Q - 1, 2 + h)
                add(NG - 4 + h, h)
            pool.wait_ge(s_add, (NG + 1) * 16)

        def near_pe(pe):
            with pe.Fori(0, Q) as b:
                for h in range(4):
                    for u in range(G):
                        pe.wait_ge(s_tile[h][u], (b + 1) * 16)
                        pe.wait_ge(s_hot, (b * 4 + h) * G + u + 1)
                        nc.tensor.matmul(ps_a[:, h % 2, 0:H], hot[:, h % 2, u, :], xs4[:, h, u, :], start=(u == 0),
                                         stop=(u == G - 1)).then_inc(s_red, 1)

        def near_act(act):
            act.sem_inc(s_agg, 4)
            with act.Fori(0, Q) as b:
                for h in range(4):
                    g = b * 4 + h
                    act.wait_ge(s_red, (g + 1) * G)
                    act.wait_ge(s_add, (g + 1) * 16)
                    nc.scalar.activation(agg[:, h % 2, :], ps_a[:, h % 2, 0:H], ACT.Copy).then_inc(s_agg, 1)

        def near_dve(dve):
            with dve.Fori(0, NG // 2) as b:
                for h in range(2):
                    g = b * 2 + h
                    dve.wait_ge(s_agg, g + 3)
                    dve.sem_inc(s_ldfree, 1)
                    nc.vector.tensor_copy(off2[:, h, :], T.off_f[:, ds(g * G, G)]).then_inc(s_cols, 1)
                    dve.wait_ge(s_cols, g + 1)
                    for u in range(G):
                        nc.vector.tensor_scalar(hot[:, h, u, :], T.iota_row[:], off2[:, h, u:u + 1], None,
                                                ALU.is_equal).then_inc(s_hot, 1)

        block = ph.block()

        @block.sync
        def _(sp):
            if_near(sp, T, lambda: near_sp(sp), lambda: far_sp(sp))

        @block.gpsimd
        def _(pool):
            if_near(pool, T, lambda: near_pool(pool), lambda: far_pool(pool))

        @block.tensor
        def _(pe):
            if_near(pe, T, lambda: near_pe(pe), lambda: far_pe(pe))

        @block.scalar
        def _(act):
            if_near(act, T, lambda: near_act(act), lambda: far_act(act))

        @block.vector
        def _(dve):
            if_near(dve, T, lambda: near_dve(dve), lambda: far_dve(dve))


def edge_layer3(nc, A, T):
    with Phase(nc, "e3") as ph:
        rows = ph.sb("rows", [P, 2, G, P])
        isrc = ph.sb("isrc", [P, 2, G], I32)
        idst = ph.sb("idst", [P, 2, G], I32)
        iout = ph.sb("iout", [P, 2, G], I32)
        xr = ph.sb("xr", [P, 2, G, XR])
        el = ph.sb("el", [P, 2, G, HEADS])
        z = ph.sb("z", [P, 2, G, HEADS])
        pay = ph.sb("pay", [P, G, PAY])
        cols = ph.sb("cols", [P, G])
        same = ph.sb("same", [P, G, P])
        msg = ph.sb("msg", [P, K3, PAY])
        ps_m = ph.ps("ps_m", [P, 2, 512])
        s_ld = ph.sems("ld", 2)
        s_ge = ph.sems("ge", 2)
        s_ldfree, s_gfree, s_go, s_cols, s_z, s_exp, s_pay, s_same, s_sum, s_msg = (
            ph.sem(n) for n in ("ldfree", "gfree", "go", "cols", "z", "exp", "pay", "same", "sum", "msg"))
        s_add = ph.sems("add", K3)


        def far_sp(sp):
            with sp.Fori(0, NG // 2) as b:
                for h in range(2):
                    g = b * 2 + h
                    sp.wait_ge(s_ldfree, g + 1)
                    sp.dma_start(rows[:, h].rearrange("p u f -> p (u f)"),
                                 bcast_rows(T.src_rows[ds(g * G * P, G * P)], P)).then_inc(s_ld[h], 16)
                    sp.dma_start(isrc[:, h, :], A["src_cols"][:, ds(g * G, G)]).then_inc(s_ld[h], 16)
                    sp.dma_start(idst[:, h, :], A["dst_cols"][:, ds(g * G, G)]).then_inc(s_ld[h], 16)
                    sp.dma_start(iout[:, h, :], T.srcu_cols[:, ds(g * G, G)]).then_inc(s_ld[h], 16)

        def far_pool(pool):
            pool.sem_inc(s_ldfree, 2)
            start_additions(pool, T.acc3, T.zeros, s_add)
            with pool.Fori(0, NG // 2) as b:
                for h in range(2):
                    g = b * 2 + h
                    pool.wait_ge(s_ld[h], (b + 1) * 64)
                    pool.wait_ge(s_gfree, g + 1)
                    pool.sem_inc(s_go, 1)
                    for u in range(G):
                        pool.indirect_dma_start(xr[:, h, u, :], None, T.xr_tab,
                                                bass.IndirectOffsetOnAxis(idst[:, h, u:u + 1], 0)).then_inc(s_ge[h], 16)
                        pool.indirect_dma_start(el[:, h, u, :], None, T.el_tab,
                                                bass.IndirectOffsetOnAxis(isrc[:, h, u:u + 1], 0)).then_inc(s_ge[h], 16)
                    for u in range(G):
                        pool.wait_ge(s_msg, g * G + u + 3)
                        pool.wait_ge(s_add[u % K3], (g * (G // K3) + u // K3 + 1) * 16)
                        pool.sem_inc(s_go, 1)
                        pool.indirect_dma_start(T.acc3[u % K3], bass.IndirectOffsetOnAxis(iout[:, h, u:u + 1], 0),
                                                msg[:, u % K3, :], None,
                                                compute_op=ALU.add).then_inc(s_add[u % K3], 16)
                    for k in range(K3):
                        pool.wait_ge(s_add[k], ((g + 1) * (G // K3) + 1) * 16)
                    pool.sem_inc(s_ldfree, 1)

        def far_pe(pe):
            with pe.Fori(0, NG // 2) as b:
                for h in range(2):
                    for u in range(G):
                        n = (b * 2 + h) * G + u
                        pe.wait_ge(s_pay, n * 2 + 2)
                        pe.wait_ge(s_msg, n + 1)
                        nc.tensor.matmul(ps_m[:, u % 2, 0:PAY], same[:, u, :], pay[:, u, :], start=True,
                                         stop=True).then_inc(s_sum, 1)

        def far_act(act):
            act.sem_inc(s_msg, 2)
            with act.Fori(0, NG) as g:
                act.wait_ge(s_z, (g + 1) * 2)
                nc.scalar.activation(pay[:, :, HEADS * DOUT:PAY], z[:, 1, :, :], ACT.Exp).then_inc(s_exp, 1)
                for u in range(G):
                    act.wait_ge(s_sum, g * G + u + 1)
                    act.wait_ge(s_add[u % K3], (g * (G // K3) + u // K3 + 1) * 16)
                    nc.scalar.activation(msg[:, u % K3, :], ps_m[:, u % 2, 0:PAY], ACT.Copy).then_inc(s_msg, 1)

        def far_dve(dve):
            dve.sem_inc(s_gfree, 2)
            with dve.Fori(0, NG // 2) as b:
                for h in range(2):
                    g = b * 2 + h
                    nc.vector.tensor_copy(cols[:], T.src_f[:, ds(g * G, G)]).then_inc(s_cols, 1)
                    dve.wait_ge(s_ge[h], (b + 1) * 2 * G * 16)
                    nc.vector.tensor_tensor(z[:, 0, :, :], el[:, h, :, :], xr[:, h, :, DOUT:XR],
                                            ALU.add).then_inc(s_z, 1)
                    dve.wait_ge(s_z, g * 2 + 1)
                    nc.vector.scalar_tensor_tensor(z[:, 1, :, :], z[:, 0, :, :], 0.2, z[:, 0, :, :],
                                                   ALU.mult, ALU.max).then_inc(s_z, 1)
                    dve.wait_ge(s_ld[h], (b + 1) * 64)
                    dve.wait_ge(s_cols, g + 1)
                    for u in range(G):
                        nc.vector.tensor_scalar(same[:, u, :], rows[:, h, u, :], cols[:, u:u + 1], None,
                                                ALU.is_equal).then_inc(s_same, 1)
                    dve.wait_ge(s_exp, g + 1)
                    for u in range(G):
                        for e in range(2):
                            x2 = xr[:, h, u, None, 0:DOUT].to_broadcast([P, 2, DOUT])
                            e2 = pay[:, u, HEADS * DOUT + 2 * e:HEADS * DOUT + 2 * e + 2][:, :, None]
                            nc.vector.tensor_tensor(
                                pay[:, u, e * 2 * DOUT:(e + 1) * 2 * DOUT].rearrange("p (a d) -> p a d", a=2),
                                x2, e2.to_broadcast([P, 2, DOUT]), ALU.mult).then_inc(s_pay, 1)
                    dve.wait_ge(s_sum, (g + 1) * G)
                    dve.sem_inc(s_gfree, 1)

        rowd = ph.sb("rowd", [P, 2, G * P])
        rowl = ph.sb("rowl", [P, 2, G * P])
        hotT = ph.sb("hotT", [P, 2, G * P], F32R)
        hotL = ph.sb("hotL", [P, 2, G * P], F32R)
        win = ph.sb("win", [P, 2, XR])
        win_s = ph.sb("win_s", [P, 2, 2, XR], F32R)
        el_s = ph.sb("el_s", [P, 2, NT * HEADS], F32R)
        idx2 = ph.sb("idx2", [P, 2, G], I32)
        uniq_all = ph.sb("uniq_all", [P, ET], I32)
        src2 = ph.sb("src2", [P, 2, G])
        hi2 = ph.sb("hi2", [P, 2, G])
        same2 = ph.sb("same2", [P, 2, G, P])
        pick = ph.sb("pick", [P, 2, 2, NT * HEADS])
        els = ph.sb("els", [P, 2, 2, HEADS])
        z2 = ph.sb("z2", [P, 2, 2, 2, HEADS])
        pay2 = ph.sb("pay2", [P, 4, 2, PAY])
        msg2 = ph.sb("msg2", [P, 4, 2, PAY])
        ps_e = ph.ps("ps_e", [P, 2, 512])
        ps_x = ph.ps("ps_x", [P, 4, 512])
        s_hot, s_e, s_x, s_pick, s_els, s_sm, s_uniq, s_idx, s_ws, s_el = (
            ph.sem(n) for n in ("hot", "e", "x", "pick", "els", "sm", "uniq", "idx", "ws", "el"))
        s_row = ph.sems("row", 2)
        s_payb = ph.sem("payb")
        LAST = NG // 2 - 1
        WE = NT * HEADS

        def near_sp(sp):
            sp.dma_start(uniq_all[:], T.srcu_cols).then_inc(s_uniq, 16)
            with sp.Fori(0, NG // 2) as b:
                for h in range(2):
                    g = b * 2 + h
                    first = sp.value_load(T.base[0:1, ds(g, 1)], min_val=0, max_val=NP - P)
                    sp.wait_ge(s_hot, g + 1)
                    sp.sem_inc(s_go, 1)
                    sp.dma_start(rowd[:, h, :], bcast_rows(T.dst_rows[ds(g * G * P, G * P)], P)).then_inc(s_ld[h], 16)
                    sp.dma_start(rowl[:, h, :], bcast_rows(T.lo_rows[ds(g * G * P, G * P)], P)).then_inc(s_ld[h], 16)
                    sp.dma_start(win[:, h, :], T.xr_tab[ds(first, P), :]).then_inc(s_ld[h], 16)
                    sp.wait_ge(s_sm, g * G + G)
                    sp.dma_start(rows[:, h].rearrange("p u f -> p (u f)"),
                                 bcast_rows(T.src_rows[ds(g * G * P, G * P)], P)).then_inc(s_row[h], 16)

        def near_pool(pool):
            start_additions(pool, T.acc3, T.zeros, s_add)
            pool.wait_ge(s_uniq, 16)
            pool.sem_inc(s_go, 1)

            def group(g, b, h):
                nc.gpsimd.tensor_copy(idx2[:, h, :], uniq_all[:, ds(g * G, G)]).then_inc(s_idx, 1)
                pool.wait_ge(s_idx, g + 1)
                for u in range(G):
                    k = u % K3
                    pool.wait_ge(s_msg, g * 4 + u // 2 + 3)
                    pool.wait_ge(s_add[k], (g * (G // K3) + u // K3 + 1) * 16)
                    pool.sem_inc(s_go, 1)
                    pool.indirect_dma_start(T.acc3[k], bass.IndirectOffsetOnAxis(idx2[:, h, u:u + 1], 0),
                                            msg2[:, u // 2, u % 2, :], None,
                                            compute_op=ALU.add).then_inc(s_add[k], 16)

            with pool.Fori(0, NG // 2) as b:
                group(b * 2, b, 0)
                group(b * 2 + 1, b, 1)
            for k in range(K3):
                pool.wait_ge(s_add[k], (NG * (G // K3) + 1) * 16)

        def near_pe(pe):
            pe.sem_inc(s_x, 2 * G)
            pe.sem_inc(s_sum, 8)

            def scores(g, b, h, i):
                n = g * 4 + i
                if i == 0:
                    pe.wait_ge(s_ld[h], (b + 1) * 48)
                    pe.wait_ge(s_hot, g + 3)
                pe.wait_ge(s_pick, n * 2 + 2)
                for v in range(2):
                    e = slice((2 * i + v) * P, (2 * i + v + 1) * P)
                    o = ps_e[:, i % 2, v * WE:(v + 1) * WE]
                    nc.tensor.matmul(o, hotL[:, h, e], el_s[:, 0, :], start=True, stop=False)
                    nc.tensor.matmul(o, hotL[:, h, e], el_s[:, 1, :], start=False, stop=True).then_inc(s_e, 1)

            def features(g, h, i):
                pe.wait_ge(s_pay, g * 4 + i + 1)
                pe.wait_ge(s_payb, g * 4 + i + 1)
                for v in range(2):
                    e = slice((2 * i + v) * P, (2 * i + v + 1) * P)
                    o = ps_x[:, i % 2 * 2 + v, 0:XR]
                    nc.tensor.matmul(o, hotT[:, h, e], win_s[:, h, 0, :], start=True, stop=False)
                    nc.tensor.matmul(o, hotT[:, h, e], win_s[:, h, 1, :], start=False, stop=True).then_inc(s_x, 1)

            def sums(g, h, i):
                n = g * 4 + i
                pe.wait_ge(s_pay, n + 3)
                pe.wait_ge(s_payb, n + 3)
                pe.wait_ge(s_msg, n + 2)
                for v in range(2):
                    last = nc.tensor.matmul(ps_m[:, v, 0:PAY], same2[:, h, 2 * i + v, :], pay2[:, i, v, :],
                                            start=True, stop=True)
                last.then_inc(s_sum, 1)

            def group(g, b, h, start=False, last=False):
                for i in range(4):
                    features(g, h, i)
                    if i < 3:
                        scores(g, b, h, i + 1)
                    elif not last:
                        scores(g + 1, b + h, 1 - h, 0)
                    if i >= 2:
                        sums(g, h, i - 2)
                    elif not start:
                        sums(g - 1, 1 - h, i + 2)

            pe.wait_ge(s_el, 2)
            scores(0, 0, 0, 0)
            group(0, 0, 0, start=True)
            group(1, 0, 1)
            with pe.Fori(1, LAST) as b:
                group(b * 2, b, 0)
                group(b * 2 + 1, b, 1)
            group(NG - 2, LAST, 0)
            group(NG - 1, LAST, 1, last=True)
            sums(NG - 1, 1, 2)
            sums(NG - 1, 1, 3)

        def near_act(act):
            act.sem_inc(s_msg, 2)
            act.sem_inc(s_payb, 2)

            def weights(g, i):
                n = g * 4 + i
                act.wait_ge(s_z, n * 2 + 2)
                act.wait_ge(s_sum, n + 5)
                nc.scalar.activation(pay2[:, i, :, HEADS * DOUT:PAY], z2[:, i % 2, 1], ACT.Exp).then_inc(s_exp, 1)

            def payload(g, i):
                act.wait_ge(s_exp, g * 4 + i + 1)
                for k in range(HEADS):
                    done = nc.scalar.activation(pay2[:, i, 1, k * DOUT:(k + 1) * DOUT],
                                                ps_x[:, i % 2 * 2 + 1, 0:DOUT], ACT.Copy,
                                                scale=pay2[:, i, 1, HEADS * DOUT + k:HEADS * DOUT + k + 1])
                done.then_inc(s_payb, 1)

            def messages(g, i):
                n = g * 4 + i
                act.wait_ge(s_sum, n + 9)
                for v in range(2):
                    u = 2 * i + v
                    act.wait_ge(s_add[u], (g + 1) * 16)
                nc.scalar.activation(msg2[:, i], ps_m[:, :, 0:PAY], ACT.Copy).then_inc(s_msg, 1)

            def group(g, start=False):
                for i in range(4):
                    weights(g, i)
                    payload(g, i)
                    if i >= 2:
                        messages(g, i - 2)
                    elif not start:
                        messages(g - 1, i + 2)

            group(0, start=True)
            group(1)
            with act.Fori(1, NG // 2) as b:
                group(b * 2)
                group(b * 2 + 1)
            messages(NG - 1, 2)
            messages(NG - 1, 3)

        def near_dve(dve):
            dve.sem_inc(s_sm, 2 * G)
            dve.sem_inc(s_pay, 2)
            dve.sem_inc(s_pick, 4)
            dve.sem_inc(s_hot, 2)
            el = T.el_res[:].rearrange("p n k -> p (n k)")
            nc.vector.tensor_copy(el_s[:, 0, :], el).then_inc(s_el, 1)
            dve.wait_ge(s_el, 1)
            nc.vector.tensor_tensor(el_s[:, 1, :], el, el_s[:, 0, :], ALU.subtract).then_inc(s_el, 1)

            def hots(g, b, h):
                dve.wait_ge(s_ld[h], (b + 1) * 48)
                dve.wait_ge(s_x, g * G + G)
                nc.vector.tensor_copy(win_s[:, h, 0, :], win[:, h, :]).then_inc(s_ws, 1)
                nc.vector.tensor_scalar(hotT[:, h, :], rowd[:, h, :], T.window[:, ds(g, 1)], None, ALU.is_equal)
                dve.wait_ge(s_ws, g + 1)
                nc.vector.tensor_tensor(win_s[:, h, 1, :], win[:, h, :], win_s[:, h, 0, :], ALU.subtract)
                nc.vector.tensor_scalar(hotL[:, h, :], rowl[:, h, :], T.iota_col[:], None,
                                        ALU.is_equal).then_inc(s_hot, 1)
                dve.wait_ge(s_sm, g * G + G)
                dve.sem_inc(s_go, 1)
                nc.vector.tensor_copy(src2[:, h, :], T.src_f[:, ds(g * G, G)])
                nc.vector.tensor_copy(hi2[:, h, :], T.hi_f[:, ds(g * G, G)]).then_inc(s_cols, 1)

            def same_source(g, b, h, u):
                if u == 0:
                    dve.wait_ge(s_row[h], (b + 1) * 16)
                dve.wait_ge(s_sum, g * 4 + u // 2 + 1)
                nc.vector.tensor_scalar(same2[:, h, u, :], rows[:, h, u, :], src2[:, h, u:u + 1], None,
                                        ALU.is_equal).then_inc(s_sm, 1)

            def payload(g, i):
                n = g * 4 + i
                dve.wait_ge(s_exp, n + 1)
                x4 = ps_x[:, i % 2 * 2, None, 0:DOUT]
                e4 = pay2[:, i, 0, HEADS * DOUT:PAY][:, :, None]
                nc.vector.tensor_tensor(pay2[:, i, 0, 0:HEADS * DOUT].rearrange("p (k d) -> p k d", k=HEADS),
                                        x4.to_broadcast([P, HEADS, DOUT]),
                                        e4.to_broadcast([P, HEADS, DOUT]), ALU.mult).then_inc(s_pay, 1)

            def group(g, b, h, last=False):
                for i in range(4):
                    n = g * 4 + i
                    if i == 0:
                        dve.wait_ge(s_cols, g + 1)
                    dve.wait_ge(s_e, g * G + 2 * i + 2)
                    for v in range(2):
                        nc.vector.scalar_tensor_tensor(pick[:, i % 2, v, :], T.iota_hi[:].rearrange("p n k -> p (n k)"),
                                                       hi2[:, h, 2 * i + v:2 * i + v + 1],
                                                       ps_e[:, i % 2, v * WE:(v + 1) * WE], ALU.is_equal,
                                                       ALU.mult).then_inc(s_pick, 1)
                    if i == 2 and not last:
                        hots(g + 1, b + h, 1 - h)
                    same_source(g, b, h, 2 * i)
                    dve.wait_ge(s_pick, n * 2 + 6)
                    nc.vector.reduce_sum(els[:, i % 2], pick[:, i % 2].rearrange("p v (n k) -> p v k n", k=HEADS),
                                         axis=AX.X).then_inc(s_els, 1)
                    same_source(g, b, h, 2 * i + 1)
                    dve.wait_ge(s_els, n + 1)
                    dve.wait_ge(s_x, g * G + 2 * i + 2 + 2 * G)
                    nc.vector.tensor_tensor(z2[:, i % 2, 0], els[:, i % 2],
                                            ps_x[:, i % 2 * 2:i % 2 * 2 + 2, DOUT:XR],
                                            ALU.add).then_inc(s_z, 1)
                    if i > 0:
                        payload(g, i - 1)
                    dve.wait_ge(s_z, n * 2 + 1)
                    nc.vector.scalar_tensor_tensor(z2[:, i % 2, 1], z2[:, i % 2, 0], 0.2, z2[:, i % 2, 0],
                                                   ALU.mult, ALU.max).then_inc(s_z, 1)
                payload(g, 3)

            hots(0, 0, 0)
            with dve.Fori(0, LAST) as b:
                group(b * 2, b, 0)
                group(b * 2 + 1, b, 1)
            group(NG - 2, LAST, 0)
            group(NG - 1, LAST, 1, last=True)

        block = ph.block()

        @block.sync
        def _(sp):
            if_near(sp, T, lambda: near_sp(sp), lambda: far_sp(sp))

        @block.gpsimd
        def _(pool):
            if_near(pool, T, lambda: near_pool(pool), lambda: far_pool(pool))

        @block.tensor
        def _(pe):
            if_near(pe, T, lambda: near_pe(pe), lambda: far_pe(pe))

        @block.scalar
        def _(act):
            if_near(act, T, lambda: near_act(act), lambda: far_act(act))

        @block.vector
        def _(dve):
            if_near(dve, T, lambda: near_dve(dve), lambda: far_dve(dve))


def node_after0(nc, A, ident, ones_row, tiles, acc0, x1_tab, x1s_tab, deg):
    with Phase(nc, "n0") as ph:
        w = ph.sb("w", [P, 2, H])
        bias = ph.sb("bias", [1, H])
        x = ph.sb("x", [P, 2, NB, H])
        agg = ph.sb("agg", [P, 2, NB, H + 1])
        xT = ph.sb("xT", [P, 2, 2, P])
        y = ph.sb("y", [P, NB, H])
        yhat = ph.sb("yhat", [P, 2, NB, H])
        parts = ph.sb("parts", [P, 2, NB, 2, H], F32R)
        stats = ph.sb("stats", [P, NB, 6])
        mv = ph.sb("mv", [P, NB, 2])
        rstd = ph.sb("rstd", [P, 3, NB])
        ps_t = ph.ps("ps_t", [P, 2, 4, P])
        ps_y = ph.ps("ps_y", [P, NB, 512])
        s_ld = ph.sems("ld", 2)
        (s_w, s_free, s_stats, s_var, s_sqrt, s_rinv, s_norm, s_t, s_xT, s_m, s_y, s_go, s_st, s_yfree, s_hi, s_lo,
         s_deg) = (ph.sem(n) for n in ("w", "free", "stats", "var", "sqrt", "rinv", "norm", "t", "xT", "m", "y",
                                       "go", "st", "yfree", "hi", "lo", "deg"))
        block = ph.block()

        @block.sync
        def _(sp):
            sp.dma_start(w[:], A["WoT"].rearrange("(c p) n -> p c n", p=P)).then_inc(s_w, 16)
            sp.dma_start(bias[:], A["bo"].rearrange("(a n) -> a n", a=1)).then_inc(s_w, 16)
            with sp.Fori(0, NT // NB // 2) as b:
                for h in range(2):
                    it = b * 2 + h
                    sp.wait_ge(s_free, it + 1)
                    sp.dma_start(x[:, h], tiles(A["x"])[:, ds(it * NB, NB), :]).then_inc(s_ld[h], 16)
                    sp.dma_start(agg[:, h], tiles(acc0)[:, ds(it * NB, NB), :]).then_inc(s_ld[h], 16)

        @block.tensor
        def _(pe):
            pe.sem_inc(s_m, 2)
            pe.wait_ge(s_w, 32)

            def turn(it, b, h, u):
                n = it * NB + u
                if u == 0:
                    pe.wait_ge(s_ld[h], (b + 1) * 32)
                pe.wait_ge(s_xT, n + 1)
                for c in range(2):
                    done = nc.tensor.transpose(ps_t[:, (h * NB + u) % 2, c, :], agg[:, h, u, c * P:(c + 1) * P],
                                               ident[:])
                done.then_inc(s_t, 1)

            def step(it, b, h, last):
                for u in range(NB):
                    n = it * NB + u
                    v = (h * NB + u) % 2
                    if u < NB - 1:
                        turn(it, b, h, u + 1)
                    elif not last:
                        turn(it + 1, b + h, 1 - h, 0)
                    pe.wait_ge(s_xT, n + 3)
                    pe.wait_ge(s_y, n + 1)
                    o = ps_y[:, u, 0:H]
                    nc.tensor.matmul(o, xT[:, v, 0, :], w[:, 0, :], start=True, stop=False)
                    nc.tensor.matmul(o, xT[:, v, 1, :], w[:, 1, :], start=False, stop=False)
                    nc.tensor.matmul(o, ones_row[:], bias[:], start=False, stop=True).then_inc(s_m, 1)

            turn(0, 0, 0, 0)
            both_slots(pe, step)

        @block.scalar
        def _(act):
            act.sem_inc(s_xT, 2)

            def copies(it, h):
                for u in range(NB):
                    n = it * NB + u
                    v = (h * NB + u) % 2
                    act.wait_ge(s_t, n + 1)
                    act.wait_ge(s_m, n + 1)
                    nc.scalar.activation(xT[:, v, :, :], ps_t[:, v, 0:2, :], ACT.Copy).then_inc(s_xT, 1)

            def step(it, b, h, last):
                layernorm_root(nc, act, rstd, s_var, s_sqrt, it)
                if not last:
                    copies(it + 1, 1 - h)
                act.wait_ge(s_norm, (it + 1) * NB)
                act.wait_ge(s_yfree, it + 1)
                nc.scalar.activation(parts[:, h, :, 0, :], yhat[:, h], ACT.Copy).then_inc(s_hi, 1)

            copies(0, 0)
            both_slots(act, step)

        @block.vector
        def _(dve):
            dve.sem_inc(s_free, 2)
            dve.sem_inc(s_y, NB)

            def low(it, h):
                dve.wait_ge(s_hi, it + 1)
                nc.vector.tensor_tensor(parts[:, h, :, 1, :], yhat[:, h], parts[:, h, :, 0, :],
                                        ALU.subtract).then_inc(s_lo, 1)

            def step(it, b, h, last, start=False):
                dve.wait_ge(s_ld[h], (b + 1) * 32)
                for u in range(NB):
                    dve.wait_ge(s_m, it * NB + u + 3)
                    nc.vector.scalar_tensor_tensor(y[:, u, :], x[:, h, u, :], 2.0, ps_y[:, u, 0:H], ALU.mult,
                                                   ALU.add).then_inc(s_y, 1)
                nc.vector.tensor_tensor(deg[:, ds(it * NB, NB)], deg[:, ds(it * NB, NB)], agg[:, h, :, H],
                                        ALU.add).then_inc(s_deg, 1)
                dve.wait_ge(s_y, (it + 2) * NB)
                dve.wait_ge(s_deg, it + 1)
                dve.sem_inc(s_free, 1)
                dve.wait_ge(s_yfree, it + 1)
                layernorm_batch(nc, dve, y, yhat[:, h], stats, mv, rstd, s_stats, s_var, s_sqrt, s_rinv, s_norm,
                                s_go, it)
                if not start:
                    low(it - 1, 1 - h)

            step(0, 0, 0, False, start=True)
            step(1, 0, 1, False)
            with dve.Fori(1, NT // NB // 2) as b:
                step(b * 2, b, 0, False)
                step(b * 2 + 1, b, 1, False)
            low(NT // NB - 1, 1)

        @block.gpsimd
        def _(pool):
            pool.sem_inc(s_yfree, 2)
            with pool.Fori(0, NT // NB // 2) as b:
                for h in range(2):
                    it = b * 2 + h
                    pool.wait_ge(s_lo, it + 1)
                    pool.sem_inc(s_go, 1)
                    pool.dma_start(tiles(x1_tab)[:, ds(it * NB, NB), :], yhat[:, h]).then_inc(s_st, 16)
                    pool.dma_start(tiles(x1s_tab)[:, ds(it * NB, NB), :],
                                   parts[:, h].rearrange("p n a d -> p n (a d)").bitcast(F32)).then_inc(s_st, 16)
                    pool.wait_ge(s_st, (it + 1) * 32)
                    pool.sem_inc(s_yfree, 1)


def node_after1(nc, A, ident, tiles, acc1, x1_tab, x2_tab, hs_tab, deg, dinv):
    with Phase(nc, "n1") as outer:
        hT = outer.sb("hT", [P, 2, NP])
        with Phase(nc, "n1a") as ph:
            w1 = ph.sb("w1", [P, 2, H])
            w2 = ph.sb("w2", [P, 2, H])
            b1 = ph.sb("b1", [P, 2])
            b2 = ph.sb("b2", [P, 2])
            part = ph.sb("part", [P, 2, KACC, NB, H])
            agg = ph.sb("agg", [P, 2, NB, H])
            aT = ph.sb("aT", [P, 2, 2, P])
            hid = ph.sb("hid", [P, 2, 2, P])
            ps_t = ph.ps("ps_t", [P, 2, 512])
            ps_u = ph.ps("ps_u", [P, 2, 512])
            ps_h = ph.ps("ps_h", [P, 2, 512])
            s_ld = ph.sems("ld", 2)
            s_w, s_free, s_sum, s_t, s_aT, s_u, s_hid, s_h, s_hT = (
                ph.sem(n) for n in ("w", "free", "sum", "t", "aT", "u", "hid", "h", "hT"))
            block = ph.block()

            @block.sync
            def _(sp):
                sp.dma_start(w1[:], A["Wu1"].rearrange("(c p) n -> p c n", p=P)).then_inc(s_w, 16)
                sp.dma_start(w2[:], A["Wu2"].rearrange("(c p) n -> p c n", p=P)).then_inc(s_w, 16)
                sp.dma_start(b1[:], A["bu1"].rearrange("(c p) -> p c", p=P)).then_inc(s_w, 16)
                sp.dma_start(b2[:], A["bu2"].rearrange("(c p) -> p c", p=P)).then_inc(s_w, 16)
                with sp.Fori(0, NT // NB // 2) as b:
                    for h in range(2):
                        it = b * 2 + h
                        sp.wait_ge(s_free, it + 1)
                        for k in range(KACC):
                            sp.dma_start(part[:, h, k], tiles(acc1[k])[:, ds(it * NB, NB), :]).then_inc(s_ld[h], 16)

            @block.tensor
            def _(pe):
                pe.sem_inc(s_t, 2 * NB)
                pe.sem_inc(s_u, 2)
                pe.sem_inc(s_h, 2)
                pe.wait_ge(s_w, 64)

                def turn(it, h, u):
                    n = it * NB + u
                    if u == 0:
                        pe.wait_ge(s_sum, (it + 1) * 3)
                    pe.wait_ge(s_aT, n + 1)
                    for c in range(2):
                        done = nc.tensor.transpose(ps_t[:, (h * NB + u) % 2, c * P:(c + 1) * P],
                                                   agg[:, h, u, c * P:(c + 1) * P], ident[:])
                    done.then_inc(s_t, 1)

                def layer(o, w, x, sem):
                    for c in range(2):
                        for k in range(2):
                            done = nc.tensor.matmul(o[:, c * P:(c + 1) * P], w[:, k, c * P:(c + 1) * P], x[:, k, :],
                                                    start=(k == 0), stop=(k == 1))
                    done.then_inc(sem, 1)

                def second(it, h, u):
                    n = it * NB + u
                    v = (h * NB + u) % 2
                    pe.wait_ge(s_hid, n + 3)
                    pe.wait_ge(s_hT, n + 1)
                    layer(ps_h[:, v], w2, hid[:, v], s_h)

                def step(it, b, h, last):
                    for u in range(NB):
                        n = it * NB + u
                        v = (h * NB + u) % 2
                        if u < NB - 1 or not last:
                            turn(*next_tile(it, h, u))
                        pe.wait_ge(s_aT, n + 3)
                        pe.wait_ge(s_hid, n + 1)
                        layer(ps_u[:, v], w1, aT[:, v], s_u)
                        if u > 0:
                            second(it, h, u - 1)
                    second(it, h, NB - 1)

                turn(0, 0, 0)
                both_slots(pe, step)

            @block.scalar
            def _(act):
                act.sem_inc(s_aT, 2)
                act.sem_inc(s_hid, 2)
                act.wait_ge(s_w, 64)

                def copy(it, h, u):
                    n = it * NB + u
                    v = (h * NB + u) % 2
                    act.wait_ge(s_t, n + 1 + 2 * NB)
                    act.wait_ge(s_u, n + 1)
                    nc.scalar.activation(aT[:, v].rearrange("p a b -> p (a b)"), ps_t[:, v, 0:2 * P],
                                         ACT.Copy).then_inc(s_aT, 1)

                def step(it, b, h, last):
                    for u in range(NB):
                        n = it * NB + u
                        v = (h * NB + u) % 2
                        if u < NB - 1 or not last:
                            copy(*next_tile(it, h, u))
                        act.wait_ge(s_u, n + 3)
                        act.wait_ge(s_h, n + 1)
                        for c in range(2):
                            done = nc.scalar.activation(hid[:, v, c, :], ps_u[:, v, c * P:(c + 1) * P], ACT.Silu,
                                                        bias=b1[:, c:c + 1])
                        done.then_inc(s_hid, 1)

                copy(0, 0, 0)
                both_slots(act, step)

            @block.vector
            def _(dve):
                dve.sem_inc(s_hT, 2)
                dve.sem_inc(s_free, 2)
                dve.wait_ge(s_w, 64)

                def summed(it, b, h):
                    dve.wait_ge(s_ld[h], (b + 1) * 16 * KACC)
                    dve.wait_ge(s_t, (it + 1) * NB)
                    nc.vector.tensor_tensor(part[:, h, 0], part[:, h, 0], part[:, h, 1], ALU.add).then_inc(s_sum, 1)
                    nc.vector.tensor_tensor(part[:, h, 2], part[:, h, 2], part[:, h, 3], ALU.add).then_inc(s_sum, 1)
                    dve.wait_ge(s_sum, it * 3 + 2)
                    nc.vector.tensor_tensor(agg[:, h], part[:, h, 0], part[:, h, 2], ALU.add).then_inc(s_sum, 1)
                    dve.wait_ge(s_sum, it * 3 + 3)
                    dve.sem_inc(s_free, 1)

                def step(it, b, h, last):
                    if not last:
                        summed(it + 1, b + h, 1 - h)
                    for u in range(NB):
                        n = it * NB + u
                        dve.wait_ge(s_h, n + 3)
                        for c in range(2):
                            done = nc.vector.tensor_scalar(hT[:, c, ds(n * P, P)],
                                                           ps_h[:, (h * NB + u) % 2, c * P:(c + 1) * P],
                                                           b2[:, c:c + 1], None, ALU.add)
                        done.then_inc(s_hT, 1)

                summed(0, 0, 0)
                both_slots(dve, step)

        with Phase(nc, "n1b") as ph:
            w = ph.sb("w", [P, 2, H])
            gamma = ph.sb("gamma", [P, 2])
            beta = ph.sb("beta", [P, 2])
            chunks = [(c, min(512, N - c)) for c in range(0, N, 512)]
            bstats = ph.sb("bstats", [P, 2, len(chunks), 6])
            bmv = ph.sb("bmv", [P, 2, 2])
            bn = ph.sb("bn", [P, 5, 2])
            hb = ph.sb("hb", [P, 2, 2, P])
            x = ph.sb("x", [P, 2, NB, H])
            y = ph.sb("y", [P, NB, H])
            yhat = ph.sb("yhat", [P, 2, NB, H])
            xT = ph.sb("xT", [P, 2, 2, P])
            hs = ph.sb("hs", [P, 2, NB, H])
            dcol = ph.sb("dcol", [P, 2, NB])
            root = ph.sb("root", [P, 2, NT])
            stats = ph.sb("stats", [P, NB, 6])
            mv = ph.sb("mv", [P, NB, 2])
            rstd = ph.sb("rstd", [P, 3, NB])
            ps_b = ph.ps("ps_b", [P, 2, 512])
            ps_t = ph.ps("ps_t", [P, 2, 512])
            ps_y = ph.ps("ps_y", [P, 2, 512])
            s_ld = ph.sems("ld", 2)
            (s_w, s_free, s_bst, s_stats, s_var, s_sqrt, s_rinv, s_norm, s_t, s_xT, s_y, s_m, s_go, s_st,
             s_yfree, s_hb, s_b, s_bn, s_bsq, s_hs, s_dc) = (
                ph.sem(n) for n in ("w", "free", "bst", "stats", "var", "sqrt", "rinv", "norm", "t", "xT", "y",
                                    "m", "go", "st", "yfree", "hb", "b", "bn", "bsq", "hs", "dc"))
            block = ph.block()

            @block.sync
            def _(sp):
                sp.dma_start(w[:], A["W2"].rearrange("(c p) n -> p c n", p=P)).then_inc(s_w, 16)
                sp.dma_start(gamma[:], A["gamma"].rearrange("(c p) -> p c", p=P)).then_inc(s_w, 16)
                sp.dma_start(beta[:], A["beta"].rearrange("(c p) -> p c", p=P)).then_inc(s_w, 16)
                with sp.Fori(0, NT // NB // 2) as b:
                    for h in range(2):
                        it = b * 2 + h
                        sp.wait_ge(s_free, it + 1)
                        sp.dma_start(x[:, h], tiles(x1_tab)[:, ds(it * NB, NB), :]).then_inc(s_ld[h], 16)

            @block.tensor
            def _(pe):
                pe.sem_inc(s_b, 2)
                pe.sem_inc(s_t, 2 * NB)
                pe.sem_inc(s_m, 2)
                pe.wait_ge(s_w, 48)

                def turn_back(it, h):
                    for u in range(NB):
                        n = it * NB + u
                        v = (h * NB + u) % 2
                        pe.wait_ge(s_hb, n + 1)
                        pe.wait_ge(s_y, n + 1)
                        for c in range(2):
                            done = nc.tensor.transpose(ps_b[:, v, c * P:(c + 1) * P], hb[:, v, c, :], ident[:])
                        done.then_inc(s_b, 1)

                def turn(it, h, u):
                    n = it * NB + u
                    pe.wait_ge(s_norm, n + 1)
                    pe.wait_ge(s_xT, n + 1)
                    for c in range(2):
                        done = nc.tensor.transpose(ps_t[:, (h * NB + u) % 2, c * P:(c + 1) * P],
                                                   yhat[:, h, u, c * P:(c + 1) * P], ident[:])
                    done.then_inc(s_t, 1)

                def step(it, b, h, last):
                    if not last:
                        turn_back(it + 1, 1 - h)
                    turn(it, h, 0)
                    for u in range(NB):
                        n = it * NB + u
                        v = (h * NB + u) % 2
                        if u < NB - 1:
                            turn(it, h, u + 1)
                        pe.wait_ge(s_xT, n + 3)
                        pe.wait_ge(s_hs, n + 1)
                        nc.tensor.matmul(ps_y[:, v, 0:H], xT[:, v, 0, :], w[:, 0, :], start=True, stop=False)
                        nc.tensor.matmul(ps_y[:, v, 0:H], xT[:, v, 1, :], w[:, 1, :], start=False,
                                         stop=True).then_inc(s_m, 1)

                turn_back(0, 0)
                both_slots(pe, step)

            @block.scalar
            def _(act):
                act.wait_ge(s_bn, 1)
                nc.scalar.activation(bn[:, 1, :], bn[:, 0, :], ACT.Sqrt)
                nc.scalar.activation(root[:, 1, :], root[:, 0, :], ACT.Sqrt).then_inc(s_bsq, 1)
                act.sem_inc(s_hs, 2)
                act.sem_inc(s_xT, 2)
                act.wait_ge(s_bn, 5)

                def normed(it, h):
                    for u in range(NB):
                        n = it * NB + u
                        v = (h * NB + u) % 2
                        act.wait_ge(s_b, n + 1)
                        act.sem_inc(s_go, 1)
                        for c in range(2):
                            done = nc.scalar.activation(hb[:, v, c, :], hT[:, c, ds(n * P, P)], ACT.Identity,
                                                        bias=bn[:, 4, c:c + 1], scale=bn[:, 3, c:c + 1])
                        done.then_inc(s_hb, 1)

                def step(it, b, h, last):
                    if not last:
                        normed(it + 1, 1 - h)
                    act.wait_ge(s_dc, it + 1)
                    act.wait_ge(s_yfree, it + 1)
                    act.sem_inc(s_go, 1)
                    for u in range(NB):
                        n = it * NB + u
                        v = (h * NB + u) % 2
                        act.wait_ge(s_t, n + 1 + 2 * NB)
                        act.wait_ge(s_m, n + 1)
                        nc.scalar.activation(xT[:, v].rearrange("p a b -> p (a b)"), ps_t[:, v, 0:2 * P],
                                             ACT.Copy).then_inc(s_xT, 1)
                        if u > 0:
                            scaled(it, h, u - 1)
                    scaled(it, h, NB - 1)
                    if not last:
                        layernorm_root(nc, act, rstd, s_var, s_sqrt, it + 1)

                def scaled(it, h, u):
                    act.wait_ge(s_m, it * NB + u + 3)
                    nc.scalar.activation(hs[:, h, u, :], ps_y[:, (h * NB + u) % 2, 0:H], ACT.Copy,
                                         scale=dcol[:, h, u:u + 1]).then_inc(s_hs, 1)

                normed(0, 0)
                layernorm_root(nc, act, rstd, s_var, s_sqrt, 0)
                both_slots(act, step)

            @block.vector
            def _(dve):
                for c in range(2):
                    for k, (a, m) in enumerate(chunks):
                        nc.vector.bn_stats(bstats[:, c, k, :], hT[:, c, a:a + m]).then_inc(s_bst, 1)
                dve.wait_ge(s_bst, 2 * len(chunks))
                for c in range(2):
                    nc.vector.bn_aggr(bmv[:, c, :], bstats[:, c, :, :]).then_inc(s_bst, 1)
                dve.wait_ge(s_bst, 2 * len(chunks) + 2)
                nc.vector.tensor_scalar(root[:, 0, :], deg[:], 1.0, None, ALU.add)
                nc.vector.tensor_scalar(bn[:, 0, :], bmv[:, :, 1], LN_EPS, None, ALU.add).then_inc(s_bn, 1)
                dve.wait_ge(s_bsq, 1)
                nc.vector.reciprocal(dinv[:], root[:, 1, :])
                nc.vector.reciprocal(bn[:, 2, :], bn[:, 1, :]).then_inc(s_bn, 1)
                dve.wait_ge(s_bn, 2)
                dve.wait_ge(s_w, 48)
                nc.vector.tensor_tensor(bn[:, 3, :], bn[:, 2, :], gamma[:], ALU.mult).then_inc(s_bn, 1)
                dve.wait_ge(s_bn, 3)
                nc.vector.tensor_tensor(bn[:, 4, :], bn[:, 3, :], bmv[:, :, 0], ALU.mult).then_inc(s_bn, 1)
                dve.wait_ge(s_bn, 4)
                nc.vector.tensor_tensor(bn[:, 4, :], beta[:], bn[:, 4, :], ALU.subtract).then_inc(s_bn, 1)
                dve.wait_ge(s_bn, 5)
                dve.sem_inc(s_free, 2)
                dve.sem_inc(s_y, 2)

                with dve.Fori(0, NT // NB // 2) as b:
                    for h in range(2):
                        it = b * 2 + h
                        dve.wait_ge(s_ld[h], (b + 1) * 16)
                        for u in range(NB):
                            dve.wait_ge(s_b, it * NB + u + 3)
                            nc.vector.scalar_tensor_tensor(y[:, u, :], x[:, h, u, :], 2.0,
                                                           ps_b[:, (h * NB + u) % 2, 0:H], ALU.mult,
                                                           ALU.add).then_inc(s_y, 1)
                        dve.wait_ge(s_y, (it + 1) * NB + 2)
                        dve.sem_inc(s_free, 1)
                        dve.wait_ge(s_yfree, it + 1)
                        dve.wait_ge(s_t, (it + 1) * NB)
                        dve.sem_inc(s_go, 1)
                        nc.vector.tensor_copy(dcol[:, h], dinv[:, ds(it * NB, NB)]).then_inc(s_dc, 1)
                        layernorm_batch(nc, dve, y, yhat[:, h], stats, mv, rstd, s_stats, s_var, s_sqrt, s_rinv,
                                        s_norm, s_go, it)

            @block.gpsimd
            def _(pool):
                pool.sem_inc(s_yfree, 2)
                with pool.Fori(0, NT // NB // 2) as b:
                    for h in range(2):
                        it = b * 2 + h
                        pool.wait_ge(s_norm, (it + 1) * NB)
                        pool.sem_inc(s_go, 1)
                        pool.dma_start(tiles(x2_tab)[:, ds(it * NB, NB), :], yhat[:, h]).then_inc(s_st, 16)
                        pool.wait_ge(s_hs, (it + 1) * NB + 2)
                        pool.sem_inc(s_go, 1)
                        pool.dma_start(tiles(hs_tab)[:, ds(it * NB, NB), :], hs[:, h]).then_inc(s_st, 16)
                        pool.wait_ge(s_st, (it + 1) * 32)
                        pool.sem_inc(s_yfree, 1)


def node_after2(nc, A, ident, tiles, acc2, hs_tab, x2_tab, x3_tab, xr_tab, el_tab, el_res, dinv):
    IT = NT // NB
    WC = DOUT + 2 * HEADS
    with Phase(nc, "n2") as ph:
        w = ph.sb("w", [P, 2, WC])
        wT = ph.sb("wT", [DOUT, 2, P])
        wlr = ph.sb("wlr", [DOUT, 2 * HEADS])
        bias = ph.sb("bias", [P, H])
        dcol = ph.sb("dcol", [P, NB])
        x = ph.sb("x", [P, 2, 3, NB, H])
        t = ph.sb("t", [P, 3, NB, H])
        y = ph.sb("y", [P, NB, H])
        yhat = ph.sb("yhat", [P, 2, NB, H])
        xT = ph.sb("xT", [P, 2, 2, P])
        xr = ph.sb("xr", [P, 2, NB, WC])
        stats = ph.sb("stats", [P, NB, 6])
        mv = ph.sb("mv", [P, NB, 2])
        rstd = ph.sb("rstd", [P, 3, NB])
        ps_w = ph.ps("ps_w", [P, 512])
        ps_t = ph.ps("ps_t", [P, 2, 512])
        ps_y = ph.ps("ps_y", [P, 2, 512])
        s_ld = ph.sems("ld", 2)
        (s_w, s_free, s_stats, s_var, s_sqrt, s_rinv, s_norm, s_t, s_xT, s_e, s_ys, s_go, s_st,
         s_yfree, s_wp, s_wc, s_xr) = (
            ph.sem(n) for n in ("w", "free", "stats", "var", "sqrt", "rinv", "norm", "t", "xT", "e",
                                "ys", "go", "st", "yfree", "wp", "wc", "xr"))
        block = ph.block()

        @block.sync
        def _(sp):
            sp.dma_start(w[:, :, 0:DOUT], A["W3"].rearrange("(c p) n -> p c n", p=P)).then_inc(s_w, 16)
            sp.dma_start(wT[:], A["W3T"].rearrange("k (c n) -> k c n", c=2)).then_inc(s_w, 16)
            sp.dma_start(wlr[:, 0:HEADS], A["WrT"]).then_inc(s_w, 16)
            sp.dma_start(wlr[:, HEADS:], A["WlT"]).then_inc(s_w, 16)
            sp.dma_start(bias[:], bcast_rows(A["b2"], P)).then_inc(s_w, 16)
            with sp.Fori(0, IT // 2) as b:
                for h in range(2):
                    it = b * 2 + h
                    sp.wait_ge(s_free, it + 1)
                    for k, tab in enumerate((acc2, hs_tab, x2_tab)):
                        sp.dma_start(x[:, h, k], tiles(tab)[:, ds(it * NB, NB), :]).then_inc(s_ld[h], 16)

        @block.tensor
        def _(pe):
            pe.wait_ge(s_w, 80)
            for c in range(2):
                nc.tensor.matmul(ps_w[:, c * 8:c * 8 + 8], wT[:, c, :], wlr[:], start=True, stop=True).then_inc(s_wp, 1)
            pe.wait_ge(s_wc, 1)
            pe.sem_inc(s_t, 2 * NB)
            pe.sem_inc(s_ys, 2)

            def turn(it, h, u):
                n = it * NB + u
                pe.wait_ge(s_norm, n + 1)
                pe.wait_ge(s_xT, n + 1)
                for c in range(2):
                    done = nc.tensor.transpose(ps_t[:, (h * NB + u) % 2, c * P:(c + 1) * P],
                                               yhat[:, h, u, c * P:(c + 1) * P], ident[:])
                done.then_inc(s_t, 1)

            def step(it, b, h, last):
                turn(it, h, 0)
                for u in range(NB):
                    n = it * NB + u
                    v = (h * NB + u) % 2
                    if u < NB - 1:
                        turn(it, h, u + 1)
                    pe.wait_ge(s_xT, n + 3)
                    pe.wait_ge(s_xr, n + 1)
                    nc.tensor.matmul(ps_y[:, v, 0:WC], xT[:, v, 0, :], w[:, 0, :], start=True, stop=False)
                    nc.tensor.matmul(ps_y[:, v, 0:WC], xT[:, v, 1, :], w[:, 1, :], start=False,
                                     stop=True).then_inc(s_ys, 1)

            both_slots(pe, step)

        @block.scalar
        def _(act):
            act.wait_ge(s_wp, 2)
            nc.scalar.activation(w[:, :, DOUT:WC], ps_w[:, 0:16].rearrange("p (c n) -> p c n", c=2),
                                 ACT.Copy).then_inc(s_wc, 1)
            act.sem_inc(s_xr, 2)
            act.sem_inc(s_xT, 2)

            def kept(it, h, u):
                n = it * NB + u
                v = (h * NB + u) % 2
                act.wait_ge(s_ys, n + 3)
                act.sem_inc(s_go, 1)
                nc.scalar.activation(el_res[:, ds(n, 1), :], ps_y[:, v, None, XR:WC], ACT.Copy)
                nc.scalar.activation(xr[:, h, u, :], ps_y[:, v, 0:WC], ACT.Copy).then_inc(s_xr, 1)

            def step(it, b, h, last):
                if not last:
                    layernorm_root(nc, act, rstd, s_var, s_sqrt, it + 1)
                act.wait_ge(s_yfree, it + 1)
                for u in range(NB):
                    n = it * NB + u
                    v = (h * NB + u) % 2
                    act.wait_ge(s_t, n + 1 + 2 * NB)
                    act.wait_ge(s_ys, n + 1)
                    nc.scalar.activation(xT[:, v].rearrange("p a b -> p (a b)"), ps_t[:, v, 0:2 * P],
                                         ACT.Copy).then_inc(s_xT, 1)
                    if u > 0:
                        kept(it, h, u - 1)
                kept(it, h, NB - 1)

            layernorm_root(nc, act, rstd, s_var, s_sqrt, 0)
            both_slots(act, step)

        @block.vector
        def _(dve):
            dve.sem_inc(s_free, 2)
            dve.wait_ge(s_w, 80)
            S = 3 + NB
            with dve.Fori(0, IT // 2) as b:
                for h in range(2):
                    it = b * 2 + h
                    dve.wait_ge(s_ld[h], (b + 1) * 48)
                    nc.vector.tensor_tensor(t[:, 0], x[:, h, 0], x[:, h, 1], ALU.add)
                    nc.vector.tensor_copy(dcol[:], dinv[:, ds(it * NB, NB)]).then_inc(s_e, 1)
                    dve.wait_ge(s_e, it * S + 1)
                    for u in range(NB):
                        nc.vector.scalar_tensor_tensor(t[:, 1, u, :], t[:, 0, u, :], dcol[:, u:u + 1], bias[:],
                                                       ALU.mult, ALU.add).then_inc(s_e, 1)
                    dve.wait_ge(s_e, it * S + 1 + NB)
                    nc.vector.scalar_tensor_tensor(t[:, 2], t[:, 1], 0.2, t[:, 1], ALU.mult, ALU.max).then_inc(s_e, 1)
                    dve.wait_ge(s_e, it * S + 2 + NB)
                    nc.vector.tensor_tensor(y[:], t[:, 2], x[:, h, 2], ALU.add).then_inc(s_e, 1)
                    dve.wait_ge(s_e, it * S + S)
                    dve.sem_inc(s_free, 1)
                    dve.wait_ge(s_yfree, it + 1)
                    dve.wait_ge(s_t, (it + 1) * NB)
                    layernorm_batch(nc, dve, y, yhat[:, h], stats, mv, rstd, s_stats, s_var, s_sqrt, s_rinv,
                                    s_norm, s_go, it)

        @block.gpsimd
        def _(pool):
            pool.sem_inc(s_yfree, 2)
            with pool.Fori(0, IT // 2) as b:
                for h in range(2):
                    it = b * 2 + h
                    pool.wait_ge(s_norm, (it + 1) * NB)
                    pool.sem_inc(s_go, 1)
                    pool.dma_start(tiles(x3_tab)[:, ds(it * NB, NB), :], yhat[:, h]).then_inc(s_st, 16)
                    pool.wait_ge(s_xr, (it + 1) * NB + 2)
                    pool.sem_inc(s_go, 1)
                    pool.dma_start(tiles(xr_tab)[:, ds(it * NB, NB), :], xr[:, h, :, 0:XR]).then_inc(s_st, 16)
                    pool.dma_start(tiles(el_tab)[:, ds(it * NB, NB), :], xr[:, h, :, XR:WC]).then_inc(s_st, 16)
                    pool.wait_ge(s_st, (it + 1) * 48)
                    pool.sem_inc(s_yfree, 1)


def store_batches(nc, block, pairs, s_ready, per, extra, s_go, s_st, s_free):
    @block.gpsimd
    def _(pool):
        pool.sem_inc(s_free, 1)
        with pool.Fori(0, NT // NB) as it:
            pool.wait_ge(s_ready, (it + 1) * per + extra)
            pool.sem_inc(s_go, 1)
            for dst, buf in pairs:
                pool.dma_start(dst[:, ds(it * NB, NB), :], buf).then_inc(s_st, 16)
            pool.wait_ge(s_st, (it + 1) * 16 * len(pairs))
            pool.sem_inc(s_free, 1)


def node_after3(nc, T, tiles, b3, out):
    IT = NT // NB
    HD = HEADS * DOUT
    with Phase(nc, "n3") as ph:
        bias = ph.sb("bias", [P, HD])
        part = ph.sb("part", [P, 2, K3, NB, PAY])
        x = ph.sb("x", [P, 2, NB, H])
        den = ph.sb("den", [P, 2, NB, HEADS])
        z = ph.sb("z", [P, NB, HD])
        neg = ph.sb("neg", [P, NB, HD])
        ex = ph.sb("ex", [P, NB, HD])
        pos = ph.sb("pos", [P, NB, HD])
        y = ph.sb("y", [P, NB, H])
        yhat = ph.sb("yhat", [P, NB, H])
        stats = ph.sb("stats", [P, NB, 6])
        mv = ph.sb("mv", [P, NB, 2])
        rstd = ph.sb("rstd", [P, 3, NB])
        ps_s = ph.ps("ps_s", [P, NB, 512])
        s_ld = ph.sems("ld", 2)
        (s_w, s_free, s_sum, s_z, s_stats, s_var, s_sqrt, s_rinv, s_norm, s_e, s_neg, s_ex, s_go, s_st,
         s_yfree) = (
            ph.sem(n) for n in ("w", "free", "sum", "z", "stats", "var", "sqrt", "rinv", "norm", "e", "neg", "ex",
                                "go", "st", "yfree"))
        block = ph.block()

        @block.sync
        def _(sp):
            for hd in range(HEADS):
                sp.dma_start(bias[:, hd * DOUT:(hd + 1) * DOUT], bcast_rows(b3, P)).then_inc(s_w, 16)
            with sp.Fori(0, IT // 2) as b:
                for h in range(2):
                    it = b * 2 + h
                    sp.wait_ge(s_free, it + 1)
                    for k in range(K3):
                        sp.dma_start(part[:, h, k], tiles(T.acc3[k])[:, ds(it * NB, NB), :]).then_inc(s_ld[h], 16)
                    sp.dma_start(x[:, h], tiles(T.x3_tab)[:, ds(it * NB, NB), :]).then_inc(s_ld[h], 16)

        @block.tensor
        def _(pe):
            with pe.Fori(0, IT // 2) as b:
                for h in range(2):
                    it = b * 2 + h
                    pe.wait_ge(s_ld[h], (b + 1) * 16 * (K3 + 1))
                    for u in range(NB):
                        pe.wait_ge(s_z, it * NB + u + 1)
                        for k in range(K3):
                            last = nc.tensor.matmul(ps_s[:, u, 0:PAY], T.ident[:], part[:, h, k, u, :],
                                                    start=(k == 0), stop=(k == K3 - 1))
                        last.then_inc(s_sum, 1)

        @block.scalar
        def _(act):
            with act.Fori(0, IT) as it:
                act.wait_ge(s_neg, it + 1)
                nc.scalar.activation(ex[:], neg[:], ACT.Exp).then_inc(s_ex, 1)
                layernorm_root(nc, act, rstd, s_var, s_sqrt, it)

        @block.vector
        def _(dve):
            dve.sem_inc(s_free, 2)
            dve.sem_inc(s_z, NB)
            dve.wait_ge(s_w, 64)
            S = NB + 3
            with dve.Fori(0, IT // 2) as b:
                for h in range(2):
                    it = b * 2 + h
                    e = it * S
                    for u in range(NB):
                        dve.wait_ge(s_sum, it * NB + u + 1)
                        nc.vector.tensor_scalar(den[:, 0, u, :], ps_s[:, u, HD:PAY], 1e-12, None,
                                                ALU.max).then_inc(s_e, 1)
                    dve.wait_ge(s_e, e + NB)
                    nc.vector.reciprocal(den[:, 1], den[:, 0]).then_inc(s_e, 1)
                    dve.wait_ge(s_e, e + NB + 1)
                    for u in range(NB):
                        for hd in range(HEADS):
                            cc = slice(hd * DOUT, (hd + 1) * DOUT)
                            last = nc.vector.scalar_tensor_tensor(z[:, u, cc], ps_s[:, u, cc], den[:, 1, u, hd:hd + 1],
                                                                  bias[:, cc], ALU.mult, ALU.add)
                        last.then_inc(s_z, 1)
                    dve.wait_ge(s_z, (it + 2) * NB)
                    nc.vector.tensor_scalar(neg[:], z[:], 0.0, None, ALU.min).then_inc(s_neg, 1)
                    dve.wait_ge(s_ld[h], (b + 1) * 16 * (K3 + 1))
                    nc.vector.scalar_tensor_tensor(pos[:], z[:], 0.0, x[:, h], ALU.max, ALU.add).then_inc(s_e, 1)
                    dve.wait_ge(s_ex, it + 1)
                    dve.wait_ge(s_e, e + NB + 2)
                    dve.sem_inc(s_free, 1)
                    nc.vector.scalar_tensor_tensor(y[:], ex[:], -1.0, pos[:], ALU.add, ALU.add).then_inc(s_e, 1)
                    dve.wait_ge(s_e, e + S)
                    dve.wait_ge(s_yfree, it + 1)
                    layernorm_batch(nc, dve, y, yhat, stats, mv, rstd, s_stats, s_var, s_sqrt, s_rinv, s_norm,
                                    s_go, it)

        store_batches(nc, block, [(tiles(out), yhat[:])], s_norm, NB, 0, s_go, s_st, s_yfree)


_INS = ["x", "src_cols", "src_rows", "dst_cols", "dst_rows", "ew_cols", "ea20T", "ea64T", "ln_g", "ln_b",
        "WqT", "bq", "WkT", "bk", "WvT", "bv", "WoT", "bo", "WdkT", "bdk", "WdvT", "bdv",
        "Wf1", "bf1", "Wf2", "bf2", "Wu1", "bu1", "Wu2", "bu2", "gamma", "beta", "W2", "b2",
        "W3", "W3T", "WlT", "WrT", "b3"]


def lay_out(i):
    a = {k: np.asarray(v) for k, v in i.items()}
    pad_n, pad_e = NP - N, EP - E

    def wide(m):
        return np.concatenate([m, np.zeros((R20P - R20, m.shape[1]), np.float32)])

    x = np.concatenate([a["x"], np.zeros((pad_n, H), np.float32)])
    spare = np.full((pad_e,), N, np.int32)
    src = np.concatenate([a["src"], spare])
    dst = np.concatenate([a["dst"], spare])
    ew = np.concatenate([a["edge_weight"], np.zeros((pad_e,), np.float32)])
    e20 = np.concatenate([a["edge_attr_20"], np.zeros((pad_e, R20), np.float32)])
    e64 = np.concatenate([a["edge_attr_64"], np.zeros((pad_e, R64), np.float32)])
    d = {"x": x, "src_cols": src.reshape(ET, P).T, "src_rows": src, "dst_cols": dst.reshape(ET, P).T,
         "dst_rows": dst, "ew_cols": ew.reshape(ET, P).T, "ea20T": wide(e20.T), "ea64T": e64.T,
         "ln_g": a["L0_gnn_ln_g"], "ln_b": a["L0_gnn_ln_b"]}
    for n in ("Wq", "Wk", "Wv", "Wo", "Wdk", "Wdv"):
        d[n + "T"] = a["L0_gnn_" + n].T
    for n in ("bq", "bk", "bv", "bo", "bdk", "bdv"):
        d[n] = a["L0_gnn_" + n]
    for n in ("Wf1", "bf1", "Wf2", "bf2", "Wu1", "bu1", "Wu2", "bu2", "gamma", "beta"):
        d[n] = a["L1_gnn_" + n]
    d["Wf1"] = wide(d["Wf1"])
    d["W2"], d["b2"] = a["L2_gnn_W"], a["L2_gnn_b"]
    d["W3"], d["W3T"], d["b3"] = a["L3_gnn_W"], a["L3_gnn_W"].T, a["L3_gnn_b"]
    d["WlT"], d["WrT"] = a["L3_gnn_Wl"].T, a["L3_gnn_Wr"].T
    return {k: np.ascontiguousarray(d[k]) for k in _INS}


def kernel(**inputs):
    import concourse.bacc as _bacc
    from concourse.bass_utils import run_bass_kernel_spmd as _run

    nc = _bacc.Bacc("TRN2", target_bir_lowering=False, num_devices=1)
    arrays, A = {}, {}
    for name, a in lay_out(inputs).items():
        arrays[f"in_{name}_dram"] = a
        A[name] = nc.dram_tensor(f"in_{name}_dram", a.shape, mybir.dt.from_np(a.dtype), kind="ExternalInput").ap()
    out = nc.dram_tensor("out_0_dram", (NP, H), F32, kind="ExternalOutput").ap()
    gnn_kernel(nc, A, out)
    r = _run(nc, [arrays], core_ids=[0])
    return r.results[0]["out_0_dram"][:N]
```
